# Optimizing a Trainium2 kernel written in Bass

```python
import numpy as np
import jax
import jax.numpy as jnp

def _softmax(x, axis=-1):
    return jax.nn.softmax(x, axis=axis)

def _gelu(x):
    return jax.nn.gelu(x, approximate=True)

def _silu(x):
    return jax.nn.silu(x)

def _sigmoid(x):
    return jax.nn.sigmoid(x)

def _layernorm(x, axis=-1, eps=1e-05):
    m = jnp.mean(x, axis=axis, keepdims=True)
    v = jnp.var(x, axis=axis, keepdims=True)
    return (x - m) / jnp.sqrt(v + eps)

def _scatter_add(tgt, idx, src, axis=0):
    return tgt.at[idx].add(src)

def _segment_sum(src, seg, n):
    return jax.ops.segment_sum(src, seg, n)
kernel_name = 'mk_seq_postln_d2_jaxref_r8_9d0209'

def setup_inputs(seed: int=0):
    np.random.seed(seed)
    _w = jnp.asarray

    def _L0_attn_setup():
        import jax, jax.numpy as jnp
        import numpy as np
        HEADS, HEAD_SIZE, FREQS, MAX_PERIOD = (16, 64, 32, 1250)
        D_MODEL = 128
        NEG_INF = -1000000000.0

        def sinusoid_embedding(seq_len, frequencies, max_period):
            pos = np.arange(seq_len, dtype=np.float64)[:, None]
            idx = np.arange(frequencies)[None, :]
            inv_freq = max_period ** (-(idx // 2 * 2) / frequencies)
            angle = pos * inv_freq
            table = np.where(idx % 2 == 0, np.sin(angle), np.cos(angle))
            return table.astype(np.float32)

        def relative_causal(scores):
            L = scores.shape[-1]
            d = jnp.clip(jnp.arange(L)[:, None] - jnp.arange(L)[None, :], 0, L - 1)
            return jnp.take_along_axis(scores, d[None, None, :, :], axis=-1)
        key = jax.random.key(seed)
        ks = jax.random.split(key, 4)
        u = np.sqrt(3.0)
        inp = jax.random.normal(ks[0], (2, 256, D_MODEL), dtype=jnp.float32)
        qkv = jax.random.uniform(ks[1], (D_MODEL, 3, HEADS, HEAD_SIZE), jnp.float32, -u, u)
        q_bias = jnp.zeros((HEADS, HEAD_SIZE), jnp.float32)
        positional = jax.random.uniform(ks[2], (FREQS, HEADS, HEAD_SIZE), jnp.float32, -u, u)
        out_kernel = jax.random.uniform(ks[3], (HEADS * HEAD_SIZE, D_MODEL), jnp.float32, -u, u)
        out_bias = jnp.zeros((D_MODEL,), jnp.float32)
        return {'input': inp, 'qkv': qkv, 'q_bias': q_bias, 'positional': positional, 'out_kernel': out_kernel, 'out_bias': out_bias}
    _L0_attn_in = _L0_attn_setup()

    def _L0_ffn_setup():
        import jax, jax.numpy as jnp
        import numpy as np
        D_MODEL = 128
        NUM_EXPERTS = 8
        TOP_K = 2
        B, S = (4, 256)
        key = jax.random.key(seed)
        ks = jax.random.split(key, 7)
        scale_in = 1.0 / np.sqrt(D_MODEL)
        scale_hid = 1.0 / np.sqrt(2 * D_MODEL)
        return {'x': jax.random.normal(ks[0], (B, S, D_MODEL), dtype=jnp.float32), 'Wg': jax.random.normal(ks[1], (D_MODEL, NUM_EXPERTS), dtype=jnp.float32) * scale_in, 'bg': jnp.zeros((NUM_EXPERTS,), dtype=jnp.float32), 'W1': jax.random.normal(ks[2], (NUM_EXPERTS, D_MODEL, 2 * D_MODEL), dtype=jnp.float32) * scale_in, 'b1': jnp.zeros((NUM_EXPERTS, 2 * D_MODEL), dtype=jnp.float32), 'W2': jax.random.normal(ks[3], (NUM_EXPERTS, 2 * D_MODEL, D_MODEL), dtype=jnp.float32) * scale_hid, 'b2': jnp.zeros((NUM_EXPERTS, D_MODEL), dtype=jnp.float32)}
    _L0_ffn_in = _L0_ffn_setup()

    def _L1_attn_setup():
        import jax, jax.numpy as jnp
        import numpy as np
        B, S, DM, H = (4, 128, 128, 16)
        D = DM // H

        def _split_heads(x):
            return x.reshape(x.shape[0], x.shape[1], H, D).transpose(0, 2, 1, 3)
        key = jax.random.key(seed)
        ks = jax.random.split(key, 16)
        sc = 0.02
        return {'hidden_states': jax.random.normal(ks[0], (B, S, DM), jnp.float32), 'wq': jax.random.normal(ks[1], (DM, DM), jnp.float32) * sc, 'bq': jax.random.normal(ks[2], (DM,), jnp.float32) * sc, 'wk': jax.random.normal(ks[3], (DM, DM), jnp.float32) * sc, 'bk': jax.random.normal(ks[4], (DM,), jnp.float32) * sc, 'wv': jax.random.normal(ks[5], (DM, DM), jnp.float32) * sc, 'bv': jax.random.normal(ks[6], (DM,), jnp.float32) * sc, 'wo': jax.random.normal(ks[7], (DM, DM), jnp.float32) * sc, 'bo': jax.random.normal(ks[8], (DM,), jnp.float32) * sc, 'wfq': jax.random.normal(ks[9], (DM, DM), jnp.float32) * sc, 'bfq': jax.random.normal(ks[10], (DM,), jnp.float32) * sc, 'wfg': jax.random.normal(ks[11], (DM, DM), jnp.float32) * sc, 'bfg': jax.random.normal(ks[12], (DM,), jnp.float32) * sc, 'up': jax.random.normal(ks[13], (H, 1, D), jnp.float32) * sc, 'uz': jax.random.normal(ks[14], (H, 1, D), jnp.float32) * sc}
    _L1_attn_in = _L1_attn_setup()

    def _L1_ffn_setup():
        import jax, jax.numpy as jnp
        import numpy as np
        B, S, D = (4, 256, 128)
        E = 8
        F = 512
        T = B * S
        CAP = 160
        key = jax.random.key(seed)
        k1, k2, k3, k4 = jax.random.split(key, 4)
        inputs = jax.random.normal(k1, (B, S, D), dtype=jnp.float32)
        gate_w = jax.random.normal(k2, (D, E), dtype=jnp.float32) / np.sqrt(D)
        w1 = jax.random.normal(k3, (E, D, F), dtype=jnp.float32) / np.sqrt(D)
        w2 = jax.random.normal(k4, (E, F, D), dtype=jnp.float32) / np.sqrt(F)
        return {'inputs': inputs, 'gate_w': gate_w, 'w1': w1, 'w2': w2}
    _L1_ffn_in = _L1_ffn_setup()
    _d = {'L0_attn_input': _L0_attn_in['input'], 'L0_attn_qkv': _L0_attn_in['qkv'], 'L0_attn_q_bias': _L0_attn_in['q_bias'], 'L0_attn_positional': _L0_attn_in['positional'], 'L0_attn_out_kernel': _L0_attn_in['out_kernel'], 'L0_attn_out_bias': _L0_attn_in['out_bias'], 'L0_ffn_Wg': _L0_ffn_in['Wg'], 'L0_ffn_bg': _L0_ffn_in['bg'], 'L0_ffn_W1': _L0_ffn_in['W1'], 'L0_ffn_b1': _L0_ffn_in['b1'], 'L0_ffn_W2': _L0_ffn_in['W2'], 'L0_ffn_b2': _L0_ffn_in['b2'], 'L1_attn_wq': _L1_attn_in['wq'], 'L1_attn_bq': _L1_attn_in['bq'], 'L1_attn_wk': _L1_attn_in['wk'], 'L1_attn_bk': _L1_attn_in['bk'], 'L1_attn_wv': _L1_attn_in['wv'], 'L1_attn_bv': _L1_attn_in['bv'], 'L1_attn_wo': _L1_attn_in['wo'], 'L1_attn_bo': _L1_attn_in['bo'], 'L1_attn_wfq': _L1_attn_in['wfq'], 'L1_attn_bfq': _L1_attn_in['bfq'], 'L1_attn_wfg': _L1_attn_in['wfg'], 'L1_attn_bfg': _L1_attn_in['bfg'], 'L1_attn_up': _L1_attn_in['up'], 'L1_attn_uz': _L1_attn_in['uz'], 'L1_ffn_gate_w': _L1_ffn_in['gate_w'], 'L1_ffn_w1': _L1_ffn_in['w1'], 'L1_ffn_w2': _L1_ffn_in['w2']}
    _x0 = _d['L0_attn_input']
    _d['L0_attn_input'] = jax.random.normal(jax.random.fold_in(jax.random.key(seed), 1), (8, 512, 128), dtype=_x0.dtype)
    del _x0
    return _d

def reference(L0_attn_input, L0_attn_qkv, L0_attn_q_bias, L0_attn_positional, L0_attn_out_kernel, L0_attn_out_bias, L0_ffn_Wg, L0_ffn_bg, L0_ffn_W1, L0_ffn_b1, L0_ffn_W2, L0_ffn_b2, L1_attn_wq, L1_attn_bq, L1_attn_wk, L1_attn_bk, L1_attn_wv, L1_attn_bv, L1_attn_wo, L1_attn_bo, L1_attn_wfq, L1_attn_bfq, L1_attn_wfg, L1_attn_bfg, L1_attn_up, L1_attn_uz, L1_ffn_gate_w, L1_ffn_w1, L1_ffn_w2):

    def _L0_attn_ref(input, qkv, q_bias, positional, out_kernel, out_bias):
        import jax, jax.numpy as jnp
        import numpy as np
        HEADS, HEAD_SIZE, FREQS, MAX_PERIOD = (16, 64, 32, 1250)
        D_MODEL = 128
        NEG_INF = -1000000000.0

        def sinusoid_embedding(seq_len, frequencies, max_period):
            pos = np.arange(seq_len, dtype=np.float64)[:, None]
            idx = np.arange(frequencies)[None, :]
            inv_freq = max_period ** (-(idx // 2 * 2) / frequencies)
            angle = pos * inv_freq
            table = np.where(idx % 2 == 0, np.sin(angle), np.cos(angle))
            return table.astype(np.float32)

        def relative_causal(scores):
            L = scores.shape[-1]
            d = jnp.clip(jnp.arange(L)[:, None] - jnp.arange(L)[None, :], 0, L - 1)
            return jnp.take_along_axis(scores, d[None, None, :, :], axis=-1)
        b, s, x = input.shape
        n, h = (HEADS, HEAD_SIZE)
        w = qkv * (3.0 * x * h * n) ** (-0.25)
        q, k, v = jnp.einsum('bsx,xAnh->Abnsh', input, w)
        q = q + q_bias[:, None, :]
        a = jnp.einsum('bnqh,bnkh->bnqk', q, k) * h ** (-0.5)
        sins = jnp.asarray(np.sqrt(2.0) * sinusoid_embedding(s, FREQS, MAX_PERIOD))
        emb = jnp.einsum('sf,fnh->nsh', sins, positional * FREQS ** (-0.5))
        pos_scores = jnp.einsum('bnqh,nvh->bnqv', q, emb) * h ** (-0.5)
        a = a + relative_causal(pos_scores)
        mask = jnp.tril(jnp.ones((s, s), dtype=bool))
        a = jax.nn.softmax(jnp.where(mask, a, NEG_INF), axis=-1)
        o = jnp.einsum('bnqk,bnkh->bqnh', a, v).reshape(b, s, n * h)
        fan_in, fan_out = out_kernel.shape
        out = o @ (out_kernel * (fan_in * fan_out) ** (-0.25)) + out_bias
        return out

    def _L0_ffn_ref(x, Wg, bg, W1, b1, W2, b2):
        import jax, jax.numpy as jnp
        import numpy as np
        D_MODEL = 128
        NUM_EXPERTS = 8
        TOP_K = 2
        B, S = (4, 256)
        Bb, Ss, D = x.shape
        E = Wg.shape[1]
        xf = x.reshape(-1, D)
        logits = xf @ Wg + bg
        probs = jax.nn.softmax(logits, axis=-1)
        w, idx = jax.lax.top_k(probs, TOP_K)
        w = w / jnp.sum(w, axis=-1, keepdims=True)
        comb = jnp.sum(jax.nn.one_hot(idx, E, dtype=xf.dtype) * w[..., None], axis=1)
        h = jax.nn.relu(jnp.einsum('nd,edh->enh', xf, W1) + b1[:, None, :])
        y = jnp.einsum('enh,ehd->end', h, W2) + b2[:, None, :]
        out = jnp.einsum('end,ne->nd', y, comb)
        return out.reshape(Bb, Ss, D)

    def _L1_attn_ref(hidden_states, wq, bq, wk, bk, wv, bv, wo, bo, wfq, bfq, wfg, bfg, up, uz):
        import jax, jax.numpy as jnp
        import numpy as np
        B, S, DM, H = (4, 128, 128, 16)
        D = DM // H

        def _split_heads(x):
            return x.reshape(x.shape[0], x.shape[1], H, D).transpose(0, 2, 1, 3)
        key_len = hidden_states.shape[1]
        mixed_q = hidden_states @ wq + bq
        mixed_k = hidden_states @ wk + bk
        mixed_v = hidden_states @ wv + bv
        glo = jnp.mean(mixed_q, axis=1, keepdims=True)
        c = jnp.tanh(mixed_q @ wfq + bfq + (glo @ wfg + bfg))
        c = _split_heads(c)
        p = jnp.sum(c * up[None], axis=-1)
        z = jnp.sum(c * uz[None], axis=-1)
        P = jax.nn.sigmoid(p) * key_len
        Z = jax.nn.sigmoid(z) * key_len
        j = jnp.arange(key_len, dtype=P.dtype)
        G = -(j[None, None, None, :] - P[..., None]) ** 2 * 2.0 / Z[..., None] ** 2
        q = _split_heads(mixed_q)
        k = _split_heads(mixed_k)
        v = _split_heads(mixed_v)
        scores = jnp.einsum('bhqd,bhkd->bhqk', q, k) / jnp.sqrt(jnp.float32(D))
        scores = scores + G
        probs = jax.nn.softmax(scores, axis=-1)
        ctx = jnp.einsum('bhqk,bhkd->bhqd', probs, v)
        ctx = ctx.transpose(0, 2, 1, 3).reshape(ctx.shape[0], key_len, H * D)
        return ctx @ wo + bo

    def _L1_ffn_ref(inputs, gate_w, w1, w2):
        import jax, jax.numpy as jnp
        import numpy as np
        B, S, D = (4, 256, 128)
        E = 8
        F = 512
        T = B * S
        CAP = 160
        tokens = inputs.reshape(-1, D)
        logits = tokens @ gate_w
        probs = jax.nn.softmax(logits, axis=-1)
        expert_idx = jnp.argmax(probs, axis=-1)
        mask1 = jax.nn.one_hot(expert_idx, E, dtype=tokens.dtype)
        pos = (jnp.cumsum(mask1, axis=0) - 1.0).astype(jnp.int32)
        sec_mask = mask1[:, :, None] * jax.nn.one_hot(pos, CAP, dtype=tokens.dtype)
        combine_weights = probs[:, :, None] * sec_mask
        expert_input = jnp.einsum('tec,td->ecd', sec_mask, tokens)
        h = jax.nn.relu(jnp.einsum('ecd,edf->ecf', expert_input, w1))
        expert_output = jnp.einsum('ecf,efd->ecd', h, w2)
        out = jnp.einsum('tec,ecd->td', combine_weights, expert_output)
        return out.reshape(inputs.shape)
    x = L0_attn_input
    x = _layernorm(x + _L0_attn_ref(x, L0_attn_qkv, L0_attn_q_bias, L0_attn_positional, L0_attn_out_kernel, L0_attn_out_bias), axis=-1)
    x = _layernorm(x + _L0_ffn_ref(x, L0_ffn_Wg, L0_ffn_bg, L0_ffn_W1, L0_ffn_b1, L0_ffn_W2, L0_ffn_b2), axis=-1)
    x = _layernorm(x + _L1_attn_ref(x, L1_attn_wq, L1_attn_bq, L1_attn_wk, L1_attn_bk, L1_attn_wv, L1_attn_bv, L1_attn_wo, L1_attn_bo, L1_attn_wfq, L1_attn_bfq, L1_attn_wfg, L1_attn_bfg, L1_attn_up, L1_attn_uz), axis=-1)
    x = _layernorm(x + _L1_ffn_ref(x, L1_ffn_gate_w, L1_ffn_w1, L1_ffn_w2), axis=-1)
    return x

_drawn_inputs = setup_inputs


def setup_inputs(seed=0):
    import zlib

    import numpy as np

    out = dict(_drawn_inputs(seed))
    spreads = {'L0_attn_q_bias': (0.0, 0.1),
     'L0_attn_out_bias': (0.0, 0.1),
     'L0_ffn_bg': (0.0, 0.1),
     'L0_ffn_b1': (0.0, 0.1),
     'L0_ffn_b2': (0.0, 0.1)}
    factors = {'L1_attn_wq': 8.0,
     'L1_attn_bq': 8.0,
     'L1_attn_wk': 8.0,
     'L1_attn_bk': 64.0,
     'L1_attn_wv': 3.506,
     'L1_attn_bv': 4.66,
     'L1_attn_wo': 2.726,
     'L1_attn_wfq': 8.0,
     'L1_attn_bfq': 56.653,
     'L1_attn_wfg': 23.413,
     'L1_attn_bfg': 39.037,
     'L1_attn_up': 8.0,
     'L1_attn_uz': 8.0}
    for name, (base, spread) in spreads.items():
        noise = np.random.default_rng([zlib.crc32(name.encode()), seed]).standard_normal(out[name].shape)
        drawn = base * np.exp(spread * noise) if base else spread * noise
        out[name] = jnp.asarray(drawn.astype(out[name].dtype))
    for name, factor in factors.items():
        out[name] = (out[name] * factor).astype(out[name].dtype)
    return out
```

```python
from contextlib import ExitStack

import numpy as np

import concourse.bass as bass
from concourse import mybir

F32 = mybir.dt.float32
F16 = mybir.dt.float16
BF16 = mybir.dt.bfloat16
U32 = mybir.dt.uint32
ALU = mybir.AluOpType
ACT = mybir.ActivationFunctionType
AX = mybir.AxisListType
ds = bass.ds

P = 128
B, S, D = 8, 512, 128
NT = B * S
NCH = NT // P
QC = S // P
LN_EPS = 1e-5

H0, HD, FREQS, MAX_PERIOD = 16, 64, 32, 1250
PAIRS = H0 // 2
W_SCALE = (3.0 * D * HD * H0) ** -0.25
O_SCALE = (H0 * HD * D) ** -0.25
QK_SCALE = HD ** -0.25
P_SCALE = 64.0

E0, F0 = 8, 2 * D

H1 = 16
D1 = D // H1

E1, F1, CAP = 8, 512, 160


def shape_constants():
    pos = np.arange(S, dtype=np.float64)
    idx = np.arange(FREQS)
    ang = pos[None, :] * (MAX_PERIOD ** (-(idx // 2 * 2) / FREQS))[:, None]
    sin, cos = np.sin(ang), np.cos(ang)
    odd = (idx % 2 == 1)[:, None]
    alpha, beta = np.where(odd, cos, sin), np.where(odd, sin, -cos)
    t_scale = W_SCALE * np.sqrt(2.0) * FREQS ** -0.5 * HD ** -0.5
    rel = np.concatenate([alpha, beta]) * t_scale
    plain = np.full((HD, S), W_SCALE * QK_SCALE)
    q_mult = np.stack([np.concatenate([plain, rel]), np.concatenate([rel, plain])], 1)
    k_tab = np.tile(np.concatenate([cos, sin]), (2, 1))
    qi, ki = np.arange(P)[:, None], np.arange(P)[None, :]
    causal = np.where(ki <= qi, 0.0, -1e30)
    j = (np.arange(S) - (S - 1) / 2) / 16
    j2_h = (j * j).astype(np.float16)
    j2_l = (j * j - j2_h).astype(np.float16)
    one = np.ones(S)
    key_rows = np.stack([j2_h, j2_l, j2_h, j, j, one, one, one])
    return {
        "c_tri": np.triu(np.ones((P, P))).astype(np.float16),
        "c_key_rows": key_rows.astype(np.float16),
        "c_q_mult": q_mult.astype(np.float32),
        "c_k_tab": k_tab.astype(np.float32),
        "c_causal": causal.astype(np.float32),
        "c_ident": np.eye(P, dtype=np.float32),
        "c_iota8": np.tile(np.arange(8, dtype=np.float32), (P, 1)),
    }


class Steps:

    def __init__(self, eng, sem, base=0):
        self.eng, self.sem, self.base, self.k = eng, sem, base, 0

    def done(self, ins):
        ins.then_inc(self.sem, 1)
        self.k += 1

    def wait(self):
        self.eng.wait_ge(self.sem, self.base + self.k)

    def step(self, ins):
        self.done(ins)
        self.wait()


def vector_gate(nc, m):
    nc.vector.memset(m.gate_v[:, :], 0.0)


def layer_norm_vector(nc, dve, m, n, y, st, mv, rstd, out):
    for c in range(QC):
        last = nc.vector.bn_stats(st[:, c, :], y[:, c, :])
    last.then_inc(m.stats_ready, 1)
    dve.wait_ge(m.stats_ready, n + 1)
    vector_gate(nc, m)
    for c in range(QC):
        last = nc.vector.bn_aggr(mv[:, c, :], st[:, c, :])
    last.then_inc(m.var_ready, 1)
    dve.wait_ge(m.rstd_ready, n + 1)
    for c in range(QC):
        last = nc.vector.tensor_scalar(out[:, c, :], y[:, c, :], mv[:, c, 0:1], rstd[:, c:c + 1],
                                       ALU.subtract, ALU.mult)
    return last


def pool_gate(nc, m, rows):
    nc.gpsimd.tensor_tensor(m.gate[rows, 0:1], m.mhalf[rows, 0:1], m.mhalf[rows, 1:2], ALU.add)


def layer_norm_gpsimd(nc, pool, m, n, mv, ve, rstd):
    steps = Steps(pool, m.ln_pool, n)
    pool.wait_ge(m.var_ready, n + 1)
    steps.step(nc.gpsimd.tensor_tensor(ve[:, :], mv[:, :, 1], m.eps[:, :], ALU.add))
    nc.gpsimd.tensor_tensor(rstd[:, :], ve[:, :], m.mhalf[:, :], ALU.pow).then_inc(m.rstd_ready, 1)


def setup_phase(nc, io, m):
    with ExitStack() as ctx:
        sb = lambda name, shape, dt: ctx.enter_context(nc.sbuf_tensor(name, shape, dt))
        sem = lambda name: ctx.enter_context(nc.semaphore(name))
        w_raw = sb("w_raw", [P, 3, H0, HD], F32)
        wo_raw = sb("wo_raw", [P, PAIRS, D], F32)
        posit = sb("posit", [FREQS, H0 * HD], F32)
        qb_rows = sb("qb_rows", [PAIRS, P], F32)
        qb_cols = sb("qb_cols", [P, PAIRS], F32)
        wq_t = sb("wq_t", [P, PAIRS, P], F32)
        pos_t = sb("pos_t", [P, PAIRS, P], F32)
        tab32 = sb("tab32", [P, S], F32)
        mask32 = sb("mask32", [P, P], F32)
        tp = [ctx.enter_context(nc.psum_tensor(f"tp{i}", [P, 512], F32)) for i in range(2)]
        wps = ctx.enter_context(nc.psum_tensor("wps", [P, 2, 512], F32))
        pps = ctx.enter_context(nc.psum_tensor("pps", [P, 512], F32))
        bps = ctx.enter_context(nc.psum_tensor("bps", [P, 512], F32))

        x_in, ident_in, w_in, misc_in = sem("x_in"), sem("ident_in"), sem("w_in"), sem("misc_in")
        xt_mm, xt_hi, xt_lo = sem("xt_mm"), sem("xt_hi"), sem("xt_lo")
        wt_mm, wt_out, g_mm, g_hi, dve_steps = sem("wt_mm"), sem("wt_out"), sem("g_mm"), sem("g_hi"), sem("su_steps")
        act_done = sem("act_done")
        block = ctx.enter_context(nc.Block())

        @block.sync
        def _(sp):
            sp.dma_start(m.ident[:, :], io["c_ident"]).then_inc(ident_in, 16)
            for b in range(B):
                sp.dma_start(m.x[:, b * QC:(b + 1) * QC, :],
                             io["L0_attn_input"][b].rearrange("(c p) d -> p c d", p=P)).then_inc(m.x_loaded[b], 16)

        @block.scalar
        def _(act):
            act.dma_start(w_raw[:, :, :, :], io["L0_attn_qkv"]).then_inc(w_in, 16)
            act.dma_start(posit[:, :], io["L0_attn_positional"].rearrange("f n h -> f (n h)")).then_inc(misc_in, 16)
            act.dma_start(qb_rows[:, :], io["L0_attn_q_bias"].rearrange("(a n) h -> a (n h)", n=2)).then_inc(misc_in, 16)
            act.dma_start(wo_raw[:, :, :], io["L0_attn_out_kernel"].rearrange("(a p) d -> p a d", p=P)).then_inc(misc_in, 16)
            act.dma_start(tab32[:, :], io["c_k_tab"]).then_inc(misc_in, 16)
            act.dma_start(m.q_mult[:, :, :], io["c_q_mult"]).then_inc(misc_in, 16)
            act.dma_start(mask32[:, :], io["c_causal"]).then_inc(misc_in, 16)
            act.dma_start(m.bo_bc[:, :], io["L0_attn_out_bias"].rearrange("(a d) -> a d", a=1).broadcast_to([P, D])).then_inc(misc_in, 16)
            for b in range(B):
                act.wait_ge(xt_mm, b + 1)
                nc.scalar.activation(m.xt_h[:, b * S:(b + 1) * S], tp[b % 2][:, :], ACT.Copy).then_inc(xt_hi, 1)
            act.wait_ge(wt_mm, 1)
            nc.scalar.activation(wq_t[:, :, :].rearrange("p a b -> p (a b)").rearrange("p (a b) -> p a b", a=2), wps[:, :, :], ACT.Copy).then_inc(act_done, 1)
            act.wait_ge(g_mm, 2)
            nc.scalar.activation(m.w_h[:, :, 64:192], wps[:, :, :].rearrange("p a (b n) -> p (a b) n", n=P),
                                 ACT.Copy).then_inc(g_hi, 1)

        @block.tensor
        def _(pe):
            pe.wait_ge(ident_in, 16)
            for b in range(B):
                pe.wait_ge(m.x_loaded[b], 16)
                if b >= 2:
                    pe.wait_ge(xt_lo, b - 1)
                for c in range(QC):
                    last = nc.tensor.transpose(tp[b % 2][:, c * P:(c + 1) * P], m.x[:, b * QC + c, :], m.ident[:, :])
                last.then_inc(xt_mm, 1)
            pe.wait_ge(w_in, 16)
            for a in range(PAIRS):
                last = nc.tensor.transpose(wps[:, a // 4, (a % 4) * P:(a % 4 + 1) * P],
                                           w_raw[:, 0, 2 * a:2 * a + 2, :].rearrange("p n h -> p (n h)"), m.ident[:, :])
            last.then_inc(wt_mm, 1)
            pe.wait_ge(misc_in, 112)
            for a in range(PAIRS):
                last = nc.tensor.transpose(pps[:, a * FREQS:(a + 1) * FREQS], posit[:, a * P:(a + 1) * P],
                                           m.ident[0:FREQS, 0:FREQS])
            last = nc.tensor.transpose(pps[:, 256:256 + PAIRS], qb_rows[:, :], m.ident[0:PAIRS, 0:PAIRS])
            last.then_inc(wt_mm, 1)
            pe.wait_ge(act_done, 1)
            pe.wait_ge(wt_out, 1)
            for a in range(PAIRS):
                nc.tensor.matmul(bps[0:64, a:a + 1], pos_t[:, a, 64:128], qb_cols[:, a:a + 1], start=True, stop=True)
                last = nc.tensor.matmul(bps[64:128, a:a + 1], pos_t[:, a, 0:64], qb_cols[:, a:a + 1], start=True, stop=True)
            last.then_inc(g_mm, 1)
            for a in range(PAIRS):
                last = nc.tensor.matmul(wps[:, a // 4, (a % 4) * P:(a % 4 + 1) * P], wq_t[:, a, :], pos_t[:, a, :],
                                        start=True, stop=True)
            last.then_inc(g_mm, 1)

        @block.vector
        def _(dve):
            steps = Steps(dve, dve_steps)
            steps.done(nc.vector.memset(pos_t[:, :, :], 0.0))
            steps.done(nc.vector.memset(m.zeros[:, :], 0.0))
            steps.done(nc.vector.memset(m.xt_h[:, NT:NT + S], 0.0))
            steps.done(nc.vector.memset(m.xt_l[:, NT:NT + S], 0.0))
            for b in range(B):
                dve.wait_ge(xt_hi, b + 1)
                nc.vector.tensor_tensor(m.xt_l[:, b * S:(b + 1) * S], tp[b % 2][:, :], m.xt_h[:, b * S:(b + 1) * S],
                                        ALU.subtract).then_inc(xt_lo, 1)
            dve.wait_ge(w_in, 16)
            parts = [(0, 64, w_raw[:, 0, 0::2, :]), (192, 256, w_raw[:, 0, 1::2, :]),
                     (256, 384, w_raw[:, 1, :, :].rearrange("p (a n) h -> p a (n h)", n=2)),
                     (384, 512, w_raw[:, 2, :, :].rearrange("p (a n) h -> p a (n h)", n=2))]
            for lo, hi, src in parts:
                steps.done(nc.vector.tensor_copy(m.w_h[:, :, lo:hi], src))
            steps.wait()
            for lo, hi, src in parts:
                steps.done(nc.vector.tensor_tensor(m.w_l[:, :, lo:hi], src, m.w_h[:, :, lo:hi], ALU.subtract))
            dve.wait_ge(misc_in, 112)
            dve.wait_ge(wt_mm, 2)
            for h in range(2):
                r = slice(64 * h, 64 * h + 64)
                for k in range(2):
                    steps.done(nc.vector.tensor_copy(pos_t[r, :, 64 * h + 32 * k:64 * h + 32 * k + 32],
                                                     pps[r, 0:256].rearrange("p (a f) -> p a f", f=FREQS)))
            nc.vector.tensor_copy(qb_cols[:, :], pps[:, 256:256 + PAIRS]).then_inc(wt_out, 1)
            steps.done(nc.vector.tensor_copy(m.wo_h[:, :, :], wo_raw[:, :, :]))
            for h in range(2):
                steps.done(nc.vector.tensor_copy(m.k_h[h][:, :], tab32[:, :]))
            steps.done(nc.vector.tensor_copy(m.causal[:, :], mask32[:, :]))
            steps.done(nc.vector.tensor_copy(m.ident_bf[:, :], m.ident[:, :]))
            steps.wait()
            nc.vector.tensor_tensor(m.wo_l[:, :, :], wo_raw[:, :, :], m.wo_h[:, :, :], ALU.subtract)
            for h in range(2):
                nc.vector.tensor_tensor(m.k_l[h][:, :], tab32[:, :], m.k_h[h][:, :], ALU.subtract)
            dve.wait_ge(g_mm, 1)
            dve.wait_ge(wt_out, 1)
            inv = 1.0 / W_SCALE
            nc.vector.tensor_scalar(m.q_bias[0:64, 0, :], qb_cols[0:64, :], inv, None, ALU.mult)
            nc.vector.tensor_scalar(m.q_bias[64:128, 0, :], bps[64:128, 0:PAIRS], inv, None, ALU.mult)
            nc.vector.tensor_scalar(m.q_bias[0:64, 1, :], bps[0:64, 0:PAIRS], inv, None, ALU.mult)
            nc.vector.tensor_scalar(m.q_bias[64:128, 1, :], qb_cols[64:128, :], inv, None, ALU.mult)
            dve.wait_ge(g_hi, 1)
            nc.vector.tensor_tensor(m.w_l[:, :, 64:192], wps[:, :, :].rearrange("p a (b n) -> p (a b) n", n=P),
                                    m.w_h[:, :, 64:192], ALU.subtract)

        @block.gpsimd
        def _(pool):
            nc.gpsimd.memset(m.mhalf[:, :], -0.5)
            nc.gpsimd.memset(m.eps[:, :], LN_EPS)


def rel_attention_phase(nc, io, m):
    with ExitStack() as ctx:
        sb = lambda name, shape, dt: ctx.enter_context(nc.sbuf_tensor(name, shape, dt))
        sem = lambda name: ctx.enter_context(nc.semaphore(name))
        ps = lambda name: ctx.enter_context(nc.psum_tensor(name, [P, 512], F32))
        q32 = [sb(f"q32_{h}", [P, S], F32) for h in range(2)]
        q_h = [sb(f"q_h{h}", [P, S], F16) for h in range(2)]
        q_l = [sb(f"q_l{h}", [P, S], F16) for h in range(2)]
        k32 = sb("k32", [P, S], F32)
        v_h = sb("v_h", [P, QC, P], F16)
        v_l = sb("v_l", [P, QC, P], F16)
        PW = P * QC * (QC + 1) // 2
        prob = [sb(f"prob{h}", [P, PW], F32) for h in range(2)]
        pt_h = [sb(f"pt_h{h}", [P, PW], F16) for h in range(2)]
        pt_l = [sb(f"pt_l{h}", [P, PW], F16) for h in range(2)]
        o_h = sb("o_h", [P, S], F16)
        o_l = sb("o_l", [P, S], F16)
        nmax = [sb(f"nmax{h}", [P, QC], F32) for h in range(2)]
        sums = [sb(f"sums{h}", [P, QC], F32) for h in range(2)]
        rsum = [sb(f"rsum{h}", [P, QC], F32) for h in range(2)]
        y = sb("ln_y", [P, QC, D], F32)
        st = sb("ln_st", [P, QC, 6], F32)
        mv = sb("ln_mv", [P, QC, 2], F32)
        ve = sb("ln_ve", [P, QC], F32)
        rstd = sb("ln_rstd", [P, QC], F32)
        score_ps = [ps(f"score_ps{u}") for u in range(3)]
        pt_ps = [ps(f"pt_ps{u}") for u in range(2)]
        proj_ps, pv_ps, out_ps = ps("proj_ps"), ps("pv_ps"), ps("out_ps")

        pair = lambda name: [sem(f"{name}{h}") for h in range(2)]
        count = lambda n, u: 3 * n + u + 1
        q_mm, q_out, q_split = pair("q_mm"), pair("q_out"), pair("q_split")
        k_mm, k_out, k_split = sem("k_mm"), sem("k_out"), pair("k_split")
        v_mm, v_hi, v_lo = sem("v_mm"), sem("v_hi"), sem("v_lo")
        s_mm, max_done, exp_done = pair("s_mm"), pair("max_done"), pair("exp_done")
        p_ready = pair("p_ready")
        t_mm, pt_hi, pt_lo = pair("t_mm"), pair("pt_hi"), pair("pt_lo")
        pv_mm, o_hi, o_lo, out_mm, y_done = sem("pv_mm"), sem("o_hi"), sem("o_lo"), sem("out_mm"), sem("y_done")
        dve_steps, pool_steps = sem("ra_dve"), sem("ra_pool")
        ln_dve = sem("ra_lnd")

        UNIT_CHUNKS = [[(3, 0)], [(2, 0), (0, 384)], [(1, 0)]]
        P_OFF = [P * c * (c + 1) // 2 for c in range(QC)]
        T_UNITS = [[(0, 0)], [(1, 0), (3, 384)], [(2, 0)]]
        T_OFF, T_WIDTH = [0, 512, 1024], [512, 512, 256]
        J_OFF = {0: 0, 1: 512, 3: 896, 2: 1024}

        def schedule(eng, first_front, body, close, last):
            first_front()
            body(0, 0, 0, False, None)
            with eng.Fori(1, PAIRS - 1) as p:
                body(p, 0, p, False, p - 1)
            body(PAIRS - 1, 0, PAIRS - 1, True, PAIRS - 2)
            with eng.Fori(1, B) as b:
                body(PAIRS * b, b, 0, False, "close")
                with eng.Fori(1, PAIRS - 1) as p:
                    body(PAIRS * b + p, b, p, False, p - 1)
                body(PAIRS * b + PAIRS - 1, b, PAIRS - 1, True, PAIRS - 2)
            last()

        block = ctx.enter_context(nc.Block())

        @block.sync
        def _(sp):
            load = lambda dst, src: sp.dma_start(dst, src).then_inc(m.f0_loaded, 16)
            load(m.w1_raw[:, :, :], io["L0_ffn_W1"].rearrange("e d f -> d e f"))
            load(m.w2_raw[:, :, :, :], io["L0_ffn_W2"].rearrange("e (c p) d -> p e c d", p=P))
            load(m.wg_raw[:, :], io["L0_ffn_Wg"])
            load(m.bg_bc[:, :], io["L0_ffn_bg"].rearrange("(a e) -> a e", a=1).broadcast_to([P, E0]))
            load(m.b1_rows[:, :], io["L0_ffn_b1"].rearrange("e (c p) -> (e c) p", p=P))
            load(m.b2_rows[:, :], io["L0_ffn_b2"])
            load(m.iota8[:, :], io["c_iota8"])
            loads = 0

            def load(dst, src, scattered=False):
                nonlocal loads
                sp.dma_start(dst, src, allow_slow_non_contiguous=scattered).then_inc(m.a_loaded, 16)
                loads += 16

            for k, name in ((0, "wq"), (1, "wk"), (2, "wv"), (4, "wo")):
                load(m.a_w[:, k, :], io[f"L1_attn_{name}"])
            for dst, name in ((m.a_w[:, 3, :], "wfq"), (m.a_wfg[:, :], "wfg")):
                for g in range(4):
                    load(dst[32 * g:32 * g + 32, :], io[f"L1_attn_{name}"].rearrange("(g h d) n -> g d h n", h=4, d=D1)[g])
            for k, name in enumerate(("bq", "bk")):
                for g in range(4):
                    load(m.a_cols[32 * g:32 * g + 32, k:k + 1],
                         io[f"L1_attn_{name}"].rearrange("(g h d a) -> g d h a", h=4, d=D1, a=1)[g], scattered=True)
            for k, name in enumerate(("bfq", "bfg")):
                load(m.a_cols[:, 2 + k:3 + k], io[f"L1_attn_{name}"].rearrange("(p a) -> p a", a=1))
            for k, name in enumerate(("up", "uz")):
                load(m.a_cols[:, 4 + k:5 + k], io[f"L1_attn_{name}"].rearrange("h a d -> (h d) a"))
            for dst, name in ((m.a_bv, "bv"), (m.a_bo, "bo")):
                load(dst[:, :], io[f"L1_attn_{name}"].rearrange("(a d) -> a d", a=1).broadcast_to([P, D]))
            sp.wait_ge(m.f0_loaded, m.F0_LOADS)
            sp.wait_ge(m.a_loaded, loads)
            m.A_LOADS = loads

        @block.tensor
        def _(pe):
            def project_q(h, mth, bx, pw):
                w_hi, w_lo = (t[:, pw, 128 * h:128 * h + 128] if isinstance(pw, int)
                              else m_flat(t)[:, ds(pw * 512 + 128 * h, 128)] for t in (m.w_h, m.w_l))
                x_hi, x_lo = (t[:, ds(bx * S, S)] for t in (m.xt_h, m.xt_l))
                nc.tensor.matmul(proj_ps[:, :], w_hi, x_hi, start=True, stop=False)
                nc.tensor.matmul(proj_ps[:, :], w_lo, x_hi, start=False, stop=False)
                nc.tensor.matmul(proj_ps[:, :], w_hi, x_lo, start=False, stop=True).then_inc(q_mm[h], 1)

            def project_k(bx, pw):
                w_hi, w_lo = (m_flat(t)[:, ds(pw * 512 + 256, 128)] for t in (m.w_h, m.w_l))
                x_hi, x_lo = (t[:, ds(bx * S, S)] for t in (m.xt_h, m.xt_l))
                nc.tensor.matmul(proj_ps[:, :], w_hi, x_hi, start=True, stop=False)
                nc.tensor.matmul(proj_ps[:, :], w_lo, x_hi, start=False, stop=False)
                nc.tensor.matmul(proj_ps[:, :], w_hi, x_lo, start=False, stop=True).then_inc(k_mm, 1)

            def project_v(bx, pw):
                w_hi, w_lo = (m_flat(t)[:, ds(pw * 512 + 384, 128)] for t in (m.w_h, m.w_l))
                for c in range(QC):
                    x_hi, x_lo = (t[:, ds(bx * S + c * P, P)] for t in (m.xt_h, m.xt_l))
                    o = proj_ps[:, c * P:(c + 1) * P]
                    nc.tensor.matmul(o, x_hi, w_hi, start=True, stop=False)
                    nc.tensor.matmul(o, x_hi, w_lo, start=False, stop=False)
                    mm = nc.tensor.matmul(o, x_lo, w_hi, start=False, stop=True)
                mm.then_inc(v_mm, 1)

            def scores(h, n):
                pe.wait_ge(q_split[h], n + 1)
                pe.wait_ge(k_split[h], n + 1)
                for u in range(3):
                    if h == 1 or not (isinstance(n, int) and n == 0):
                        pe.wait_ge(exp_done[1 - h], count(n + h - 1, u))
                    for c, col in UNIT_CHUNKS[u]:
                        w = P * (c + 1)
                        o, qs = score_ps[u][:, col:col + w], slice(c * P, (c + 1) * P)
                        nc.tensor.matmul(o, q_h[h][:, qs], m.k_h[h][:, 0:w], start=True, stop=False)
                        nc.tensor.matmul(o, q_h[h][:, qs], m.k_l[h][:, 0:w], start=False, stop=False)
                        nc.tensor.matmul(o, q_l[h][:, qs], m.k_h[h][:, 0:w], start=False, stop=False)
                        mm = nc.tensor.matmul(o[:, w - P:w], m.ident_bf[:, :], m.causal[:, :], start=False, stop=True)
                    mm.then_inc(s_mm[h], 1)

            def transposes(h, n, u_list):
                for u in u_list:
                    if u == 0:
                        pe.wait_ge(p_ready[h], n + 1)
                    at = 3 * h + u
                    ph, pu = divmod(at - 2 if at >= 2 else at + 4, 3)
                    if at >= 2 or not (isinstance(n, int) and n == 0):
                        pe.wait_ge(pt_lo[ph], count(n if at >= 2 else n - 1, pu))
                    for j, col in T_UNITS[u]:
                        for c in range(j, QC):
                            mm = nc.tensor.transpose(pt_ps[at % 2][:, col + (c - j) * P:col + (c - j + 1) * P],
                                                     prob[h][:, P_OFF[c] + j * P:P_OFF[c] + (j + 1) * P], m.ident[:, :])
                    mm.then_inc(t_mm[h], 1)

            def weighted_values(n):
                for h in range(2):
                    pe.wait_ge(pt_lo[h], count(n, 2))
                pe.wait_ge(v_lo, n + 1)
                pe.wait_ge(o_lo, n)
                for j in range(QC):
                    for term in range(3):
                        pt, v = [(pt_h, v_h), (pt_h, v_l), (pt_l, v_h)][term]
                        for h in range(2):
                            mm = nc.tensor.matmul(pv_ps[64 * h:64 * h + 64, j * P:S], v[:, j, 64 * h:64 * h + 64],
                                                  pt[h][:, J_OFF[j]:J_OFF[j] + S - j * P],
                                                  start=(j == 0 and term == 0), stop=(j == QC - 1 and term == 2))
                mm.then_inc(pv_mm, 1)

            def open_output(b):
                pe.wait_ge(y_done, b)
                nc.tensor.matmul(out_ps[:, :], m.zeros[:, 0:P], m.zeros[:, :], start=True, stop=False, skip_group_check=True)

            def project_out(n, pw, end):
                pe.wait_ge(o_lo, n + 1)
                w_hi, w_lo = (m_flat(t)[:, ds(pw * P, P)] for t in (m.wo_h, m.wo_l))
                for c in range(QC):
                    cs = slice(c * P, (c + 1) * P)
                    for k, (a, w) in enumerate([(o_h, w_hi), (o_h, w_lo), (o_l, w_hi)]):
                        mm = nc.tensor.matmul(out_ps[:, cs], a[:, cs], w, start=False,
                                              stop=(end and c == QC - 1 and k == 2), skip_group_check=True)
                mm.then_inc(out_mm, 1)

            def first_front():
                project_q(0, 0, 0, 0)
                pe.wait_ge(q_out[0], 1)
                project_q(1, 0, 0, 0)
                pe.wait_ge(q_out[1], 1)
                project_k(0, 0)
                open_output(0)

            def body(n, b, p, wrap, lag):
                bx, pw = (b + 1, 0) if wrap else (b, p + 1)
                scores(0, n)
                if lag is not None:
                    transposes(1, n - 1, [0, 1, 2])
                pe.wait_ge(k_out, n + 1)
                project_q(0, n + 1, bx, pw)
                if lag is not None:
                    weighted_values(n - 1)
                pe.wait_ge(q_out[0], n + 2)
                project_v(b, p)
                if lag is not None:
                    closing = isinstance(lag, str)
                    project_out(n - 1, PAIRS - 1 if closing else lag, closing)
                    if closing:
                        open_output(b)
                scores(1, n)
                pe.wait_ge(v_lo, n + 1)
                project_q(1, n + 1, bx, pw)
                transposes(0, n, [0, 1])
                pe.wait_ge(q_out[1], n + 2)
                project_k(bx, pw)
                transposes(0, n, [2])

            def last():
                n = B * PAIRS - 1
                transposes(1, n, [0, 1, 2])
                weighted_values(n)
                project_out(n, PAIRS - 1, True)

            schedule(pe, first_front, body, None, last)

        @block.scalar
        def _(act):
            def exps(h, n):
                for u in range(3):
                    act.wait_ge(max_done[h], count(n, u))
                    if u == 0:
                        act.wait_ge(t_mm[h], 3 * n)
                    for c, col in UNIT_CHUNKS[u]:
                        w = P * (c + 1)
                        ins = nc.scalar.activation(prob[h][:, P_OFF[c]:P_OFF[c] + w], score_ps[u][:, col:col + w], ACT.Exp,
                                                   bias=nmax[h][:, c:c + 1], accum_out=sums[h][:, c:c + 1])
                    ins.then_inc(exp_done[h], 1)

            def pt_high(h, n):
                for u in range(3):
                    act.wait_ge(t_mm[h], count(n, u))
                    if u == 0:
                        act.wait_ge(pv_mm, n)
                    w = T_WIDTH[u]
                    nc.scalar.activation(pt_h[h][:, T_OFF[u]:T_OFF[u] + w], pt_ps[(3 * h + u) % 2][:, 0:w],
                                         ACT.Copy).then_inc(pt_hi[h], 1)

            def o_high(n):
                act.wait_ge(pv_mm, n + 1)
                act.wait_ge(out_mm, n)
                nc.scalar.activation(o_h[:, :], pv_ps[:, :], ACT.Copy).then_inc(o_hi, 1)

            def v_high(n, pv_behind):
                act.wait_ge(v_mm, n + 1)
                act.wait_ge(pv_mm, n)
                nc.scalar.activation(v_h[:, :, :].rearrange("p c n -> p (c n)"), proj_ps[:, :], ACT.Copy,
                                     scale=W_SCALE).then_inc(v_hi, 1)

            def k_copy(n):
                act.wait_ge(k_mm, n + 1)
                act.wait_ge(k_split[1], n)
                nc.scalar.activation(k32[:, :], proj_ps[:, :], ACT.Copy, scale=W_SCALE * QK_SCALE).then_inc(k_out, 1)

            def body(n, b, p, wrap, lag):
                exps(0, n)
                if lag is not None:
                    pt_high(1, n - 1)
                    o_high(n - 1)
                v_high(n, lag is not None)
                exps(1, n)
                pt_high(0, n)
                k_copy(n + 1)

            def last():
                n = B * PAIRS - 1
                pt_high(1, n)
                o_high(n)

            nc.scalar.preload_act_table(ACT.Exp)
            schedule(act, lambda: k_copy(0), body, None, last)

        @block.vector
        def _(dve):
            def maxima(h, n):
                for u in range(3):
                    dve.wait_ge(s_mm[h], count(n, u))
                    for c, col in UNIT_CHUNKS[u]:
                        ins = nc.vector.tensor_reduce(nmax[h][:, c:c + 1], score_ps[u][:, col:col + P * (c + 1)],
                                                      AX.X, ALU.max, negate=True)
                    ins.then_inc(max_done[h], 1)

            def normalise(h, n):
                dve.wait_ge(exp_done[h], count(n, 2))
                nc.vector.reciprocal(rsum[h][:, :], sums[h][:, :]).then_inc(dve_steps, 1)
                dve.wait_ge(dve_steps, 2 * n + h + 1)
                for c in range(QC):
                    pr = prob[h][:, P_OFF[c]:P_OFF[c] + P * (c + 1)]
                    ins = nc.vector.tensor_scalar(pr, pr, rsum[h][:, c:c + 1], P_SCALE, ALU.mult, ALU.mult)
                ins.then_inc(p_ready[h], 1)

            def pt_low(h, n):
                for u in range(3):
                    dve.wait_ge(pt_hi[h], count(n, u))
                    w = T_WIDTH[u]
                    nc.vector.tensor_tensor(pt_l[h][:, T_OFF[u]:T_OFF[u] + w], pt_ps[(3 * h + u) % 2][:, 0:w],
                                            pt_h[h][:, T_OFF[u]:T_OFF[u] + w], ALU.subtract).then_inc(pt_lo[h], 1)

            def q_evac(h, n, pw):
                dve.wait_ge(q_mm[h], n + 1)
                dve.wait_ge(q_split[h], n)
                nc.vector.scalar_tensor_tensor(q32[h][:, :], proj_ps[:, :], m_flat(m.q_bias)[:, ds(PAIRS * h + pw, 1)],
                                               m.q_mult[:, h, :], ALU.add, ALU.mult).then_inc(q_out[h], 1)

            def o_low(n):
                dve.wait_ge(o_hi, n + 1)
                nc.vector.tensor_tensor(o_l[:, :], pv_ps[:, :], o_h[:, :], ALU.subtract).then_inc(o_lo, 1)

            def v_low(n):
                dve.wait_ge(v_hi, n + 1)
                nc.vector.scalar_tensor_tensor(v_l[:, :, :].rearrange("p c n -> p (c n)"), proj_ps[:, :], W_SCALE,
                                               v_h[:, :, :].rearrange("p c n -> p (c n)"), ALU.mult, ALU.subtract).then_inc(v_lo, 1)

            def batch_sum(b):
                dve.wait_ge(ln_dve, 2 * b)
                xb = m_flat(m.x)[:, ds(b * S, S)]
                nc.vector.tensor_tensor(xb.rearrange("p (c d) -> p c d", d=D), xb.rearrange("p (c d) -> p c d", d=D),
                                        m.bo_bc[:, :].unsqueeze(1).to_broadcast([P, QC, D]), ALU.add).then_inc(ln_dve, 1)
                dve.wait_ge(out_mm, PAIRS * (b + 1))
                dve.wait_ge(ln_dve, 2 * b + 1)
                nc.vector.scalar_tensor_tensor(y[:, :, :].rearrange("p c d -> p (c d)"), out_ps[:, :], O_SCALE / P_SCALE,
                                               xb, ALU.mult, ALU.add).then_inc(y_done, 1)

            def batch_norm(b):
                dve.wait_ge(y_done, b + 1)
                xb = m_flat(m.x)[:, ds(b * S, S)]
                layer_norm_vector(nc, dve, m, b, y, st, mv, rstd, xb.rearrange("p (c d) -> p c d", d=D)).then_inc(ln_dve, 1)

            def body(n, b, p, wrap, lag):
                if lag is not None:
                    normalise(1, n - 1)
                maxima(0, n)
                if lag is not None:
                    pt_low(1, n - 1)
                q_evac(0, n + 1, 0 if wrap else p + 1)
                normalise(0, n)
                if lag is not None:
                    o_low(n - 1)
                v_low(n)
                if isinstance(lag, str):
                    batch_sum(b - 1)
                maxima(1, n)
                q_evac(1, n + 1, 0 if wrap else p + 1)
                pt_low(0, n)
                if isinstance(lag, str):
                    batch_norm(b - 1)

            def first_front():
                q_evac(0, 0, 0)
                q_evac(1, 0, 0)

            def last():
                n = B * PAIRS - 1
                normalise(1, n)
                pt_low(1, n)
                o_low(n)
                batch_sum(B - 1)
                batch_norm(B - 1)

            schedule(dve, first_front, body, None, last)

        @block.gpsimd
        def _(pool):
            def split(rows, src, hi, lo, chain_n):
                pool_gate(nc, m, rows)
                nc.gpsimd.affine_select(out=hi, in_=src, compare_op=ALU.is_ge, fill=0.0, base=0,
                                        pattern=[[1, S]], channel_multiplier=0).then_inc(pool_steps, 1)
                pool.wait_ge(pool_steps, chain_n)
                return nc.gpsimd.tensor_tensor(lo, src, hi, ALU.subtract)

            def split_q(h, n):
                pool.wait_ge(q_out[h], n + 1)
                pool.wait_ge(s_mm[h], 3 * n)
                if h == 0:
                    pool.wait_ge(k_split[1], n)
                split(slice(0, P), q32[h][:, :], q_h[h][:, :], q_l[h][:, :], 4 * n + 1 + h).then_inc(q_split[h], 1)

            def split_k(n):
                pool.wait_ge(k_out, n + 1)
                for h in range(2):
                    pool.wait_ge(s_mm[h], 3 * n)
                    pool.wait_ge(k_split[0] if h else q_split[1], n + 1)
                    r = slice(64 * h, 64 * h + 64)
                    split(r, k32[r, :], m.k_h[h][r, :], m.k_l[h][r, :], 4 * n + 3 + h).then_inc(k_split[h], 1)

            def front(n):
                split_q(0, n)
                split_q(1, n)
                split_k(n)

            def body(n, b, p, wrap, lag):
                front(n + 1)
                if isinstance(lag, str):
                    pool.wait_ge(k_split[1], n + 2)
                    layer_norm_gpsimd(nc, pool, m, b - 1, mv, ve, rstd)

            def last():
                pool.wait_ge(k_split[1], B * PAIRS + 1)
                layer_norm_gpsimd(nc, pool, m, B - 1, mv, ve, rstd)

            schedule(pool, lambda: front(0), body, None, last)


def moe_top2_phase(nc, io, m):
    with ExitStack() as ctx:
        sb = lambda name, shape, dt: ctx.enter_context(nc.sbuf_tensor(name, shape, dt))
        sem = lambda name: ctx.enter_context(nc.semaphore(name))
        FC = F0 // P
        w1_h, w1_l = (sb(n, [P, E0 * F0], F16) for n in ("w1_h", "w1_l"))
        w2_h, w2_l = (sb(n, [P, E0 * FC * D], F16) for n in ("w2_h", "w2_l"))
        wg_h, wg_l = (sb(n, [P, E0], F16) for n in ("wg_h", "wg_l"))
        b1_cols = sb("b1_cols", [P, E0 * FC], F32)
        logit = sb("logit", [P, NCH, E0], F32)
        lmax = sb("lmax", [P, NCH], F32)
        top = sb("top", [P, NCH, 8], F32)
        topi = sb("topi", [P, NCH, 8], U32)
        topf = sb("topf", [P, NCH, 8], F32)
        tsum = sb("tsum", [P, NCH], F32)
        pick = [sb(f"pick{k}", [P, NCH, E0], F32) for k in range(2)]
        comb = sb("comb", [P, NCH, E0], F32)
        comb_t = sb("comb_t", [E0, NT], F32)
        hid32 = [[sb(f"hid32_{k}{c}", [P, S], F32) for c in range(FC)] for k in range(2)]
        hid_h = [[sb(f"hid_h{k}{c}", [P, S], F16) for c in range(FC)] for k in range(2)]
        hid_l = [[sb(f"hid_l{k}{c}", [P, S], F16) for c in range(FC)] for k in range(2)]
        st = sb("f_st", [P, QC, 6], F32)
        mv = sb("f_mv", [P, QC, 2], F32)
        ve = sb("f_ve", [P, QC], F32)
        rstd = sb("f_rstd", [P, QC], F32)
        banks = [ctx.enter_context(nc.psum_tensor(f"fps{i}", [P, 512], F32)) for i in range(8)]
        hid_ps, y_ps, xt_ps = banks[0:4], banks[4:6], banks[6:8]

        xt_mm, xt_hi, xt_lo, lg_mm = sem("f_xt_mm"), sem("f_xt_hi"), sem("f_xt_lo"), sem("f_lg_mm")
        wg_split, b1_out = sem("f_wg_split"), sem("f_b1_out")
        w_split, b1_mm, shifted, exps_done = sem("f_w_split"), sem("f_b1_mm"), sem("f_shifted"), sem("f_exps")
        dsteps, comb_done, ct_mm, ct_out, b2_mm, b2_out = (sem(n) for n in ("f_steps", "f_comb", "f_ct_mm", "f_ct_out", "f_b2_mm", "f_b2_out"))
        h_mm, h_relu, h_hi, h_lo = ([sem(f"f_{n}{c}") for c in range(FC)] for n in ("h_mm", "h_relu", "h_hi", "h_lo"))
        y_out = [sem(f"f_y_out{k}") for k in range(2)]
        y_mm = sem("f_y_mm")

        def schedule(eng, unit, tile_end):
            with eng.Fori(0, B) as t:
                with eng.Fori(0, E0 // 2 - 1) as i:
                    for k in range(2):
                        unit(E0 * t + 2 * i + k, E0 // 2 * t + i, k, t, 2 * i + k + 1, t, 2 * i + k)
                half = E0 // 2 * t + E0 // 2 - 1
                unit(E0 * t + E0 - 2, half, 0, t, E0 - 1, t, E0 - 2)
                unit(E0 * t + E0 - 1, half, 1, t + 1, 0, t, E0 - 1)
                tile_end(t)

        block = ctx.enter_context(nc.Block())

        def router(pe, t):
            pe.wait_ge(xt_lo, t + 1)
            for c in range(QC):
                ch = t * QC + c
                o = y_ps[0][:, ch * E0:(ch + 1) * E0]
                xs = slice(ch * P, (ch + 1) * P)
                nc.tensor.matmul(o, m.xt_h[:, xs], wg_h[:, :], start=True, stop=False)
                nc.tensor.matmul(o, m.xt_h[:, xs], wg_l[:, :], start=False, stop=False)
                last = nc.tensor.matmul(o, m.xt_l[:, xs], wg_h[:, :], start=False, stop=True)
            last.then_inc(lg_mm, 1)

        @block.tensor
        def _(pe):
            for t in range(B):
                if t >= 2:
                    pe.wait_ge(xt_lo, t - 1)
                for c in range(QC):
                    last = nc.tensor.transpose(xt_ps[t % 2][:, c * P:(c + 1) * P], m.x[:, t * QC + c, :], m.ident[:, :])
                last.then_inc(xt_mm, 1)
                if t == 0:
                    pe.wait_ge(m.f0_loaded, m.F0_LOADS)
                    nc.tensor.transpose(hid_ps[0][:, 0:E0 * FC], m.b1_rows[:, :], m.ident[0:E0 * FC, 0:E0 * FC]).then_inc(b1_mm, 1)
                    pe.wait_ge(wg_split, 2)
                if t >= 1:
                    router(pe, t - 1)
            router(pe, B - 1)
            pe.wait_ge(comb_done, 1)
            for t in range(B):
                if t >= 2:
                    pe.wait_ge(ct_out, t - 1)
                for c in range(QC):
                    last = nc.tensor.transpose(xt_ps[t % 2][0:E0, c * P:(c + 1) * P], comb[:, t * QC + c, :], m.ident[:, :])
                last.then_inc(ct_mm, 1)
            for t in range(B):
                pe.wait_ge(ct_out, t + 1)
                if t >= 2:
                    pe.wait_ge(b2_out, t - 1)
                for c in range(QC):
                    ch = (t * QC + c) * P
                    last = nc.tensor.matmul(y_ps[t % 2][:, c * P:(c + 1) * P], comb_t[:, ch:ch + P], m.b2_rows[:, :],
                                            start=True, stop=True)
                last.then_inc(b2_mm, 1)

            def hidden(n, k, t, e):
                for c in range(FC):
                    w_hi, w_lo = (w[:, ds(e * F0 + c * P, P)] for w in (w1_h, w1_l))
                    x_hi, x_lo = (x[:, ds(t * S, S)] for x in (m.xt_h, m.xt_l))
                    o = hid_ps[2 * k + c][:, :]
                    nc.tensor.matmul(o, w_hi, x_hi, start=True, stop=False)
                    nc.tensor.matmul(o, w_lo, x_hi, start=False, stop=False)
                    nc.tensor.matmul(o, w_hi, x_lo, start=False, stop=True).then_inc(h_mm[c], 1)

            def unit(n, half, k, tn, en, t, e):
                hidden(n + 1, 1 - k, tn, en)
                for c in range(FC):
                    pe.wait_ge(h_lo[c], n + 1)
                pe.wait_ge(y_out[k], half)
                for c in range(QC):
                    cs = slice(c * P, (c + 1) * P)
                    for f in range(FC):
                        w_hi, w_lo = (w[:, ds((e * FC + f) * D, D)] for w in (w2_h, w2_l))
                        for j, (a, w) in enumerate([(hid_h, w_hi), (hid_h, w_lo), (hid_l, w_hi)]):
                            mm = nc.tensor.matmul(y_ps[k][:, cs], a[k][f][:, cs], w, start=(f == 0 and j == 0),
                                                  stop=(f == FC - 1 and j == 2))
                mm.then_inc(y_mm, 1)

            pe.wait_ge(b2_out, B)
            pe.wait_ge(w_split, 4)
            pe.wait_ge(b1_out, 1)
            hidden(0, 0, 0, 0)
            schedule(pe, unit, lambda t: None)

        @block.scalar
        def _(act):
            nc.scalar.preload_act_table(ACT.Exp)
            for t in range(B):
                act.wait_ge(xt_mm, t + 1)
                nc.scalar.activation(m.xt_h[:, t * S:(t + 1) * S], xt_ps[t % 2][:, :], ACT.Copy).then_inc(xt_hi, 1)
                if t == 0:
                    act.wait_ge(b1_mm, 1)
                    nc.scalar.activation(b1_cols[:, :], hid_ps[0][:, 0:E0 * FC], ACT.Copy).then_inc(b1_out, 1)
            act.wait_ge(shifted, 1)
            nc.scalar.activation(logit[:, :, :], logit[:, :, :], ACT.Exp).then_inc(exps_done, 1)
            for t in range(B):
                act.wait_ge(ct_mm, t + 1)
                nc.scalar.activation(comb_t[:, t * S:(t + 1) * S], xt_ps[t % 2][0:E0, :], ACT.Copy).then_inc(ct_out, 1)

            def relu(n, k, e):
                for c in range(FC):
                    act.wait_ge(h_mm[c], n + 1)
                    if not (isinstance(n, int) and n == 0):
                        act.wait_ge(h_lo[c], n - 1)
                    nc.scalar.activation(hid32[k][c][:, :], hid_ps[2 * k + c][:, :], ACT.Relu,
                                         bias=b1_cols[:, ds(e * FC + c, 1)]).then_inc(h_relu[c], 1)

            act.wait_ge(b1_out, 1)
            relu(0, 0, 0)
            schedule(act, lambda n, half, k, tn, en, t, e: relu(n + 1, 1 - k, en), lambda t: None)

        @block.vector
        def _(dve):
            steps = Steps(dve, dsteps)
            dve.wait_ge(m.f0_loaded, m.F0_LOADS)
            nc.vector.tensor_copy(wg_h[:, :], m.wg_raw[:, :]).then_inc(wg_split, 1)
            dve.wait_ge(wg_split, 1)
            nc.vector.tensor_tensor(wg_l[:, :], m.wg_raw[:, :], wg_h[:, :], ALU.subtract).then_inc(wg_split, 1)
            for t in range(B):
                dve.wait_ge(xt_hi, t + 1)
                nc.vector.tensor_tensor(m.xt_l[:, t * S:(t + 1) * S], xt_ps[t % 2][:, :], m.xt_h[:, t * S:(t + 1) * S],
                                        ALU.subtract).then_inc(xt_lo, 1)
            dve.wait_ge(lg_mm, B)
            lg_ps = y_ps[0][:, 0:NCH * E0].rearrange("p (c e) -> p c e", e=E0)
            steps.step(nc.vector.tensor_tensor(logit[:, :, :], lg_ps, m.bg_bc[:, :].unsqueeze(1).to_broadcast([P, NCH, E0]), ALU.add))
            steps.step(nc.vector.tensor_reduce(lmax[:, :], logit[:, :, :], AX.X, ALU.max))
            nc.vector.tensor_tensor(logit[:, :, :], logit[:, :, :], lmax[:, :].unsqueeze(2).to_broadcast([P, NCH, E0]),
                                    ALU.subtract).then_inc(shifted, 1)
            for hi, raw in ((w1_h, m.w1_raw), (w2_h, m.w2_raw)):
                nc.vector.tensor_copy(hi[:, :], m_flat(raw)).then_inc(w_split, 1)
            dve.wait_ge(exps_done, 1)
            for c in range(NCH):
                steps.done(nc.vector.max(top[:, c, :], logit[:, c, :]))
            steps.wait()
            for c in range(NCH):
                steps.done(nc.vector.max_index(topi[:, c, :], top[:, c, :], logit[:, c, :]))
            steps.step(nc.vector.tensor_tensor(tsum[:, :], top[:, :, 0], top[:, :, 1], ALU.add))
            steps.done(nc.vector.reciprocal(tsum[:, :], tsum[:, :]))
            steps.step(nc.vector.tensor_copy(topf[:, :, :], topi[:, :, :]))
            wide = lambda a: a.unsqueeze(2).to_broadcast([P, NCH, E0])
            for k in range(2):
                steps.done(nc.vector.tensor_tensor(pick[k][:, :, :], m.iota8[:, :].unsqueeze(1).to_broadcast([P, NCH, E0]),
                                                   wide(topf[:, :, k]), ALU.is_equal))
            steps.wait()
            for k in range(2):
                steps.done(nc.vector.tensor_tensor(pick[k][:, :, :], pick[k][:, :, :], wide(top[:, :, k]), ALU.mult))
            steps.wait()
            steps.step(nc.vector.tensor_tensor(comb[:, :, :], pick[0][:, :, :], pick[1][:, :, :], ALU.add))
            nc.vector.tensor_tensor(comb[:, :, :], comb[:, :, :], wide(tsum[:, :]), ALU.mult).then_inc(comb_done, 1)
            for lo, hi, raw in ((w1_l, w1_h, m.w1_raw), (w2_l, w2_h, m.w2_raw)):
                nc.vector.tensor_tensor(lo[:, :], m_flat(raw), hi[:, :], ALU.subtract).then_inc(w_split, 1)
            for t in range(B):
                dve.wait_ge(b2_mm, t + 1)
                xs = m.x[:, t * QC:(t + 1) * QC, :].rearrange("p c d -> p (c d)")
                nc.vector.tensor_tensor(xs, y_ps[t % 2][:, :], xs, ALU.add).then_inc(b2_out, 1)

            def high(n, k):
                for c in range(FC):
                    dve.wait_ge(h_relu[c], n + 1)
                    nc.vector.tensor_copy(hid_h[k][c][:, :], hid32[k][c][:, :]).then_inc(h_hi[c], 1)
                dve.wait_ge(h_hi[0], n + 1)
                nc.vector.tensor_tensor(hid_l[k][0][:, :], hid32[k][0][:, :], hid_h[k][0][:, :], ALU.subtract).then_inc(h_lo[0], 1)

            def unit(n, half, k, tn, en, t, e):
                high(n + 1, 1 - k)
                dve.wait_ge(y_mm, n + 1)
                for c in range(QC):
                    xc = m_flat(m.x)[:, ds(t * S + c * D, D)]
                    ins = nc.vector.scalar_tensor_tensor(xc, y_ps[k][:, c * D:(c + 1) * D],
                                                         m_flat(comb)[:, ds(t * (QC * E0) + c * E0 + e, 1)], xc, ALU.mult, ALU.add)
                ins.then_inc(y_out[k], 1)

            def tile_end(t):
                dve.wait_ge(y_out[1], E0 // 2 * (t + 1))
                vector_gate(nc, m)
                xt = m_flat(m.x)[:, ds(t * S, S)].rearrange("p (c d) -> p c d", d=D)
                layer_norm_vector(nc, dve, m, B + t, xt, st, mv, rstd, xt)

            high(0, 0)
            schedule(dve, unit, tile_end)

        @block.gpsimd
        def _(pool):
            def low(n, k):
                pool.wait_ge(h_hi[1], n + 1)
                nc.gpsimd.tensor_tensor(hid_l[k][1][:, :], hid32[k][1][:, :], hid_h[k][1][:, :], ALU.subtract).then_inc(h_lo[1], 1)

            def tile_end(t):
                layer_norm_gpsimd(nc, pool, m, B + t, mv, ve, rstd)

            low(0, 0)
            schedule(pool, lambda n, half, k, tn, en, t, e: low(n + 1, 1 - k), tile_end)


def gauss_attention_phase(nc, io, m):
    with ExitStack() as ctx:
        sb = lambda name, shape, dt: ctx.enter_context(nc.sbuf_tensor(name, shape, dt))
        sem = lambda name: ctx.enter_context(nc.semaphore(name))
        G = 4
        SC = 64.0
        K_SCALE = SC * D1 ** -0.5
        w_h, w_l = (sb(n, [P, 5, P], F16) for n in ("a_w_h", "a_w_l"))
        upz = sb("a_upz", [P, 2 * H1], F32)
        head_mask = sb("a_head_mask", [P, H1], F32)
        bk_s = sb("a_bk_s", [P, 1], F32)
        bf = sb("a_bf", [P, 1], F32)
        gbias = sb("a_gbias", [P, 1], F32)
        qsum = sb("a_qsum", [P, 1], F32)
        ident16 = sb("a_ident16", [P, P], F16)
        xs = sb("a_xs", [P, QC, D], F32)
        xt_h, xt_l = (sb(n, [P, S], F16) for n in ("a_xt_h", "a_xt_l"))
        q32, k32, c32, v32 = (sb(n, [P, S], F32) for n in ("a_q32", "a_k32", "a_c32", "a_v32"))
        q_h, q_l, k_h, k_l, coef_t = (sb(n, [P, S], F16) for n in ("a_q_h", "a_q_l", "a_k_h", "a_k_l", "a_coef_t"))
        epz = sb("a_epz", [P, QC, 2 * H1], F32)
        cent = sb("a_cent", [P, QC, H1], F32)
        ca, cb, cc = (sb(n, [P, QC, H1], F32) for n in ("a_ca", "a_cb", "a_cc"))
        coef = sb("a_coef", [P, QC, G, 8, G], F16)
        qop = sb("a_qop", [P, G, S], F16)
        kop = sb("a_kop", [P, G, G, S], F16)
        vaug = sb("a_vaug", [P, QC, H1, 32], F32)
        nm = [sb(f"a_nm{k}", [P, QC, G], F16) for k in range(2)]
        nm_t = [sb(f"a_nm_t{k}", [G, S], F16) for k in range(2)]
        pt = [[sb(f"a_pt{k}{r}", [P, 2, S], F32) for r in range(2)] for k in range(2)]
        pvs = sb("a_pvs", [P, S], F32)
        rsum = sb("a_rsum", [P, QC, G], F32)
        ctxt = sb("a_ctx", [P, QC, P], F32)
        ct_h, ct_l = (sb(n, [P, S], F16) for n in ("a_ct_h", "a_ct_l"))
        xres = sb("a_xres", [P, QC, D], F32)
        y = sb("a_y", [P, QC, D], F32)
        st = sb("a_st", [P, QC, 6], F32)
        mv = sb("a_mv", [P, QC, 2], F32)
        ve = sb("a_ve", [P, QC], F32)
        rstd = sb("a_rstd", [P, QC], F32)
        s_ps = [ctx.enter_context(nc.psum_tensor(f"a_s{k}", [P, S], F32)) for k in range(2)]
        st_ps = [ctx.enter_context(nc.psum_tensor(f"a_st{r}", [P, 2, S], F32)) for r in range(2)]
        pv_ps = ctx.enter_context(nc.psum_tensor("a_pv", [P, S], F32))
        misc = ctx.enter_context(nc.psum_tensor("a_misc", [P, S], F32))
        misc16 = misc[:, :].bitcast(F16)

        names = lambda *a: [sem("a_" + n) for n in a]
        wsplit, setup_done, kzero, kconst, vset = names("wsplit", "setup_done", "kzero", "kconst", "vset")
        misc_mm, misc_out = names("misc_mm", "misc_out")
        xs_in, xt_hi, ct_hi, q_split, k_split, pool_steps = names("xs_in", "xt_hi", "ct_hi", "q_split", "k_split", "pool_steps")
        cf_steps, coef_done, vaug_done, pvs_done, ctx_steps, xres_done = names(
            "cf_steps", "coef_done", "vaug_done", "pvs_done", "ctx_steps", "xres_done")
        ln_dve, pv_mm, parts_out = names("ln_dve", "pv_mm", "parts_out")
        s_mm, max_done, st_mm, exp_done = ([sem(f"a_{n}{k}") for k in range(2)] for n in ("s_mm", "max_done", "st_mm", "exp_done"))
        op_in = [sem(f"a_op_in{g}") for g in range(G)]
        nm_in = [sem(f"a_nm_in{g}") for g in range(G)]
        OP_LOADS = (1 + G) * 16
        PARTS = 7 * 16
        WSPLITS = 10
        q_dram = nc.dram_tensor("q_parts", (4, 32, G, S), F16).ap()
        k_dram = nc.dram_tensor("k_parts", (3, 32, G, S), F16).ap()

        PREP = ["XT", "Q", "K", "V", "GB", "F", "PZ", "CF"]
        USES = ["XT", "ctx0", "nm0", "ctx1", "Q", "nm1", "CT", "K", "OUT", "V", "GB", "ctx2", "F", "nm2", "PZ", "CF", "ctx3", "nm3"]
        BEHIND = ["ctx0", "ctx1", "CT", "OUT"]

        def uses(kind):
            drop = {"first": BEHIND, "middle": [], "last": PREP,
                    "tail": PREP + ["ctx2", "ctx3"] + [f"nm{g}" for g in range(G)]}[kind]
            return [u for u in USES if u not in drop]

        def use(kind, b, name):
            if kind == "prep0":
                return PREP.index(name)
            base = len(PREP)
            if kind != "first":
                base = base + len(uses("first")) + len(uses("middle")) * ((b if kind == "middle" else B - 1) - 1)
            if kind == "tail":
                base = base + len(uses("last"))
            return base + uses(kind).index(name)

        def schedule(eng, do):
            def step(name, *args):
                if name in do:
                    do[name](*args)

            def batch(kind, b):
                behind, ahead, own = kind != "first", kind in ("first", "middle"), kind != "tail"
                for at in range(4 * G if own else 11):
                    g, s = divmod(at, G)
                    step("slot", kind, b, at)
                    if own:
                        step("head", b, g, s)
                    if at == 1 and ahead:
                        step("XT", kind, b, b + 1)
                    if at >= 6 and own:
                        step("unit", b, (at - 6) // G, (at - 6) % G, kind == "first" and at == 6)
                    if at < 6 and behind:
                        step("unit", b - 1, (at + 10) // G, (at + 10) % G, False)
                    if kind == "tail" and at == 6:
                        step("value", b - 1, G - 1, QC - 1)
                    if s >= 2 and (at < 8 and behind or at >= 8 and own):
                        cb, cg = (b - 1, g + 2) if at < 8 else (b, g - 2)
                        step("group_end" if s == 2 else "ctx", kind, b, cb, cg)
                    if at == 7 and ahead:
                        step("Q", kind, b, b + 1)
                    if at == 11 and ahead:
                        step("F", kind, b, b + 1)
                    if s == 3 and own:
                        step("nm", kind, b, g)
                    if at == 8 and behind:
                        step("CT", kind, b, b - 1)
                    if at == 8 and ahead:
                        step("K", kind, b, b + 1)
                    if at == 9 and behind:
                        step("OUT", kind, b, b - 1)
                    if at == 9 and ahead:
                        step("V", kind, b, b + 1)
                        step("GB", kind, b, b + 1)
                    if at == 10 and behind:
                        step("norm", kind, b, b - 1)
                    if at == 12 and ahead:
                        step("PZ", kind, b, b + 1)
                    if at == 13 and ahead:
                        step("CF", kind, b, b + 1)

            step("setup")
            for name in PREP:
                step(name, "prep0", 0, 0)
            step("prepared")
            batch("first", 0)
            with eng.Fori(1, B - 1) as b:
                batch("middle", b)
            batch("last", B - 1)
            batch("tail", B)

        block = ctx.enter_context(nc.Block())

        @block.sync
        def _(sp):
            def setup():
                for dst, src in ((m.e_w1[:, :, :], io["L1_ffn_w1"].rearrange("e d f -> d e f")),
                                 (m.e_w2[:, :, :, :], io["L1_ffn_w2"].rearrange("e (c p) d -> p e c d", p=P)),
                                 (m.e_wg[:, :], io["L1_ffn_gate_w"])):
                    sp.dma_start(dst, src).then_inc(m.e_loaded, 16)
                sp.wait_ge(kzero, 1)
                for hh in range(G):
                    sp.dma_start(kop[96 + hh:P:G, hh, :, :],
                                 io["c_key_rows"].unsqueeze(1).to_broadcast([8, G, S])).then_inc(kconst, 16)
                sp.wait_ge(kconst, 16 * G)

            def spread(nb):
                sp.wait_ge(k_split, nb + 1)
                for g in range(G):
                    sp.wait_ge(op_in[g], OP_LOADS * nb)
                for n, src in ((0, q_h), (1, q_h), (2, q_l)):
                    sp.dma_start(q_dram[n].rearrange("r g n -> g r n"), src[:, :]).then_inc(parts_out, 16)
                for n, src in ((0, k_h), (1, k_l), (2, k_h)):
                    sp.dma_start(k_dram[n].rearrange("r g n -> g r n"), src[:, :]).then_inc(parts_out, 16)

            def spread_coef(kind, b, nb):
                sp.wait_ge(misc_out, use(kind, b, "CF") + 1)
                sp.dma_start(q_dram[3].rearrange("r g n -> g r n"), coef_t[:, :]).then_inc(parts_out, 16)
                sp.wait_ge(parts_out, PARTS * (nb + 1))

            def gather(nb, g):
                if not (isinstance(nb, int) and nb == 0):
                    sp.wait_ge(st_mm[1], 16 * (nb - 1) + 4 * g + 4)
                sp.dma_start(qop[:, g, :], q_dram[:, :, g, :].rearrange("t r n -> (t r) n")).then_inc(op_in[g], 16)
                for hh in range(G):
                    sp.dma_start(kop[hh:96:G, hh, g, :],
                                 k_dram.rearrange("t (d h) g n -> (t d) h g n", h=G)[:, hh, g, :]).then_inc(op_in[g], 16)

            def prepared():
                spread(0)
                spread_coef("prep0", 0, 0)
                for g in range(G):
                    gather(0, g)

            def slot(kind, b, at):
                if kind in ("middle", "last") and at in (1, 5):
                    gather(b, 2 + at // 4)
                if kind in ("first", "middle"):
                    if at == 10:
                        spread(b + 1)
                    if at == 14:
                        spread_coef(kind, b, b + 1)
                        gather(b + 1, 0)
                        gather(b + 1, 1)

            def minus_max(kind, b, g):
                sp.wait_ge(misc_out, use(kind, b, f"nm{g}") + 1)
                sp.dma_start(qop[P - G:P, g, :], nm_t[g % 2][:, :]).then_inc(nm_in[g], 16)

            schedule(sp, {"setup": setup, "prepared": prepared, "slot": slot, "nm": minus_max})
            for g in range(G):
                sp.wait_ge(nm_in[g], 16 * B)
            sp.wait_ge(m.e_loaded, 48)
            sp.wait_ge(m.e_loaded, 48)

        @block.tensor
        def _(pe):
            def shared(kind, b, name):
                pe.wait_ge(misc_out, use(kind, b, name))

            def setup():
                pe.wait_ge(wsplit, WSPLITS)

            def tokens_t(kind, b, nb):
                pe.wait_ge(xs_in, nb + 1)
                shared(kind, b, "XT")
                for c in range(QC):
                    mm = nc.tensor.transpose(misc[:, c * P:(c + 1) * P], xs[:, c, :], m.ident[:, :])
                mm.then_inc(misc_mm, 1)

            def features(name, k, xh, xl):
                def run(kind, b, nb):
                    if name == "F":
                        pe.wait_ge(q_split, nb + 1)
                    shared(kind, b, name)
                    nc.tensor.matmul(misc[:, :], w_h[:, k, :], xh[:, :], start=True, stop=False)
                    nc.tensor.matmul(misc[:, :], w_l[:, k, :], xh[:, :], start=False, stop=False)
                    nc.tensor.matmul(misc[:, :], w_h[:, k, :], xl[:, :], start=False, stop=True).then_inc(misc_mm, 1)
                return run

            def rows(name, k, xh, xl):
                def run(kind, b, nb):
                    shared(kind, b, name)
                    for c in range(QC):
                        cs = slice(c * P, (c + 1) * P)
                        nc.tensor.matmul(misc[:, cs], xh[:, cs], w_h[:, k, :], start=True, stop=False)
                        nc.tensor.matmul(misc[:, cs], xh[:, cs], w_l[:, k, :], start=False, stop=False)
                        mm = nc.tensor.matmul(misc[:, cs], xl[:, cs], w_h[:, k, :], start=False, stop=True)
                    mm.then_inc(misc_mm, 1)
                return run

            def gate_bias(kind, b, nb):
                shared(kind, b, "GB")
                nc.tensor.matmul(misc[:, 0:1], m.a_wfg[:, :], qsum[:, :], start=True, stop=True).then_inc(misc_mm, 1)

            def centre_width(kind, b, nb):
                shared(kind, b, "PZ")
                for c in range(QC):
                    mm = nc.tensor.matmul(misc[:, c * 2 * H1:(c + 1) * 2 * H1], c32[:, c * P:(c + 1) * P], upz[:, :],
                                          start=True, stop=True)
                mm.then_inc(misc_mm, 1)

            def coefficients_t(kind, b, nb):
                pe.wait_ge(coef_done, nb + 1)
                shared(kind, b, "CF")
                for c in range(QC):
                    mm = nc.tensor.transpose(misc16[:, c * P:(c + 1) * P],
                                             coef[:, c, :, :, :].rearrange("p g t h -> p (g t h)"), ident16[:, :])
                mm.then_inc(misc_mm, 1)

            def head_scores(b, g, hh):
                n = 16 * b + 4 * g + hh
                if hh == 0:
                    pe.wait_ge(op_in[g], OP_LOADS * (b + 1))
                for c in range(QC):
                    k = c % 2
                    pe.wait_ge(max_done[k], 2 * n + c // 2)
                    nc.tensor.matmul(s_ps[k][:, :], qop[:, g, c * P:(c + 1) * P], kop[:, hh, g, :], start=True,
                                     stop=True).then_inc(s_mm[k], 1)

            def unit(b, g, kc, first):
                if kc == 0:
                    pe.wait_ge(nm_in[g], 16 * (b + 1))
                for r in range(2):
                    pe.wait_ge(exp_done[r], 16 * b + 4 * g + kc)
                    for i in range(2):
                        mm = nc.tensor.matmul(st_ps[r][:, i, :], kop[:, 2 * r + i, g, kc * P:(kc + 1) * P], qop[:, g, :],
                                              start=True, stop=True)
                    mm.then_inc(st_mm[r], 1)
                if not first:
                    value(*((b, g, kc - 1) if kc else (b, g - 1, QC - 1) if g else (b - 1, G - 1, QC - 1)))

            def value(b, g, kc):
                for r in range(2):
                    pe.wait_ge(exp_done[r], 16 * b + 4 * g + kc + 1)
                if kc == 0:
                    pe.wait_ge(vaug_done, 4 * b + g + 1)
                    pe.wait_ge(pvs_done, 4 * b + g)
                for hh in range(G):
                    mm = nc.tensor.matmul(pv_ps[32 * hh:32 * hh + 32, :], vaug[:, kc, G * g + hh, :],
                                          pt[kc % 2][hh // 2][:, hh % 2, :], start=(kc == 0), stop=(kc == QC - 1))
                mm.then_inc(pv_mm, 1)

            def context(kind, b, cb, g):
                pe.wait_ge(pvs_done, 4 * cb + g + 1)
                shared(kind, b, f"ctx{(g + 2) % G}")
                for c in range(QC):
                    mm = nc.tensor.transpose(misc[:, c * P:(c + 1) * P], pvs[:, c * P:(c + 1) * P], m.ident[:, :])
                mm.then_inc(misc_mm, 1)

            def context_t(kind, b, cb):
                shared(kind, b, "CT")
                for c in range(QC):
                    mm = nc.tensor.transpose(misc[:, c * P:(c + 1) * P], ctxt[:, c, :], m.ident[:, :])
                mm.then_inc(misc_mm, 1)

            def maxima_t(kind, b, g):
                for k in range(2):
                    pe.wait_ge(max_done[k], 32 * b + 8 * g + 8)
                shared(kind, b, f"nm{g}")
                for c in range(QC):
                    mm = nc.tensor.transpose(misc16[0:G, c * P:(c + 1) * P], nm[g % 2][:, c, :], ident16[:, :])
                mm.then_inc(misc_mm, 1)

            schedule(pe, {"setup": setup, "XT": tokens_t, "Q": features("Q", 0, xt_h, xt_l), "K": features("K", 1, xt_h, xt_l),
                          "V": rows("V", 2, xt_h, xt_l), "GB": gate_bias, "F": features("F", 3, q_h, q_l),
                          "PZ": centre_width, "CF": coefficients_t, "head": head_scores, "unit": unit, "value": value,
                          "ctx": context, "nm": maxima_t, "CT": context_t, "OUT": rows("OUT", 4, ct_h, ct_l)})

        @block.scalar
        def _(act):
            def setup():
                nc.scalar.preload_act_table(ACT.Exp)
                act.wait_ge(m.a_loaded, m.A_LOADS)
                nc.scalar.activation(bk_s[:, :], m.a_cols[:, 1:2], ACT.Copy, scale=K_SCALE).then_inc(setup_done, 1)
                nc.scalar.activation(xs[:, :, :], m.x[:, 0:QC, :], ACT.Copy).then_inc(xs_in, 1)

            def slot(kind, b, at):
                if at == 0 and kind in ("first", "middle"):
                    act.wait_ge(misc_mm, use("prep0", 0, "XT") + 1 if kind == "first" else use(kind, b, "XT"))
                    nc.scalar.activation(xs[:, :, :].rearrange("p c d -> p (c d)"), m_flat(m.x)[:, ds((b + 1) * S, S)],
                                         ACT.Copy).then_inc(xs_in, 1)

            def used(kind, b, name):
                act.wait_ge(misc_mm, use(kind, b, name) + 1)

            def high(name, dst, signal):
                def run(kind, b, nb):
                    used(kind, b, name)
                    nc.scalar.activation(dst[:, :], misc[:, :], ACT.Copy).then_inc(signal, 1)
                return run

            def queries(kind, b, nb):
                act.wait_ge(q_split, nb)
                used(kind, b, "Q")
                nc.scalar.activation(q32[:, :], misc[:, :], ACT.Identity, bias=m.a_cols[:, 0:1],
                                     accum_out=qsum[:, :]).then_inc(misc_out, 1)

            def keys(kind, b, nb):
                act.wait_ge(k_split, nb)
                act.wait_ge(setup_done, 1)
                used(kind, b, "K")
                nc.scalar.activation(k32[:, :], misc[:, :], ACT.Identity, bias=bk_s[:, :], scale=K_SCALE).then_inc(misc_out, 1)

            def gates(kind, b, nb):
                used(kind, b, "F")
                nc.scalar.activation(c32[:, :], misc[:, :], ACT.Tanh, bias=gbias[:, :]).then_inc(misc_out, 1)

            def sigmoids(kind, b, nb):
                act.wait_ge(coef_done, nb)
                used(kind, b, "PZ")
                nc.scalar.activation(epz[:, :, :].rearrange("p c h -> p (c h)"), misc[:, 0:QC * 2 * H1], ACT.Exp,
                                     scale=-1.0).then_inc(misc_out, 1)

            def coefficients(kind, b, nb):
                act.wait_ge(parts_out, PARTS * nb)
                used(kind, b, "CF")
                nc.scalar.activation(coef_t[:, :], misc16[:, 0:S], ACT.Copy).then_inc(misc_out, 1)

            def unit(b, g, kc, first):
                n = 16 * b + 4 * g + kc
                for r in range(2):
                    act.wait_ge(st_mm[r], n + 1)
                    if not isinstance(n, int) or n >= 2:
                        act.wait_ge(pv_mm, n - 1)
                    nc.scalar.activation(pt[kc % 2][r][:, :, :], st_ps[r][:, :, :], ACT.Exp, scale=1.0 / SC).then_inc(exp_done[r], 1)

            def group_end(kind, b, cb, g):
                act.wait_ge(pv_mm, 16 * cb + 4 * g + 4)
                act.wait_ge(ctx_steps, 4 * cb + g)
                nc.scalar.activation(pvs[:, :], pv_ps[:, :], ACT.Copy).then_inc(pvs_done, 1)

            def maxima(kind, b, g):
                act.wait_ge(nm_in[(g + 2) % G], 16 * (b + 1) if g >= 2 else 16 * b)
                used(kind, b, f"nm{g}")
                nc.scalar.activation(nm_t[g % 2][:, :], misc16[0:G, 0:S], ACT.Copy).then_inc(misc_out, 1)

            schedule(act, {"setup": setup, "slot": slot, "XT": high("XT", xt_h, xt_hi), "Q": queries, "K": keys, "F": gates,
                           "PZ": sigmoids, "CF": coefficients, "unit": unit, "group_end": group_end, "nm": maxima,
                           "CT": high("CT", ct_h, ct_hi)})

        @block.vector
        def _(dve):
            def setup():
                steps = Steps(dve, ln_dve)
                nc.vector.memset(kop[:, :, :, :].rearrange("p a b n -> p (a b n)"), 0.0).then_inc(kzero, 1)
                nc.vector.memset(coef[:, :, :, :, :].rearrange("p c g t h -> p (c g t h)"), 0.0)
                nc.vector.tensor_copy(ident16[:, :], m.ident[:, :])
                dve.wait_ge(m.a_loaded, m.A_LOADS)
                for k in range(5):
                    view = (lambda t: t[:, k, :].rearrange("p (g d h) -> p g d h", g=G, h=G)) if k < 2 else (lambda t: t[:, k, :])
                    raw = m.a_w[:, k, :]
                    if k < 2:
                        raw = raw.rearrange("p (g h d) -> p g d h", g=G, h=G)
                    nc.vector.tensor_copy(view(w_h), raw).then_inc(wsplit, 1)
                    dve.wait_ge(wsplit, 2 * k + 1)
                    nc.vector.tensor_tensor(view(w_l), raw, view(w_h), ALU.subtract).then_inc(wsplit, 1)
                steps.step(nc.vector.tensor_reduce(head_mask[:, :], m.ident[:, :].rearrange("p (h d) -> p h d", d=D1), AX.X, ALU.add))
                for k in range(2):
                    steps.done(nc.vector.tensor_scalar(upz[:, k * H1:(k + 1) * H1], head_mask[:, :], m.a_cols[:, 4 + k:5 + k], None, ALU.mult))
                steps.step(nc.vector.tensor_tensor(bf[:, :], m.a_cols[:, 2:3], m.a_cols[:, 3:4], ALU.add))
                assert steps.k == SETUP_STEPS

            def used(kind, b, name):
                dve.wait_ge(misc_mm, use(kind, b, name) + 1)

            def low(name, hi, lo, signal):
                def run(kind, b, nb):
                    used(kind, b, name)
                    dve.wait_ge(signal, nb + 1)
                    nc.vector.tensor_tensor(lo[:, :], misc[:, :], hi[:, :], ALU.subtract).then_inc(misc_out, 1)
                return run

            def values(kind, b, nb):
                dve.wait_ge(vaug_done, G * nb)
                used(kind, b, "V")
                nc.vector.tensor_copy(v32[:, :], misc[:, :]).then_inc(misc_out, 1)

            def gate_bias(kind, b, nb):
                used(kind, b, "GB")
                nc.vector.scalar_tensor_tensor(gbias[:, :], misc[:, 0:1], 1.0 / S, bf[:, :], ALU.mult, ALU.add).then_inc(misc_out, 1)

            def polynomial(kind, b, nb):
                steps = Steps(dve, cf_steps, CF_STEPS * nb)
                dve.wait_ge(misc_out, use(kind, b, "PZ") + 1)
                steps.step(nc.vector.tensor_scalar(epz[:, :, :], epz[:, :, :], 1.0, None, ALU.add))
                steps.done(nc.vector.reciprocal(cent[:, :, :], epz[:, :, 0:H1]))
                steps.step(nc.vector.tensor_tensor(ca[:, :, :], epz[:, :, H1:], epz[:, :, H1:], ALU.mult))
                steps.done(nc.vector.tensor_scalar(cent[:, :, :], cent[:, :, :], float(S), -(S - 1) / 2, ALU.mult, ALU.add))
                steps.step(nc.vector.tensor_scalar(ca[:, :, :], ca[:, :, :], -2.0 * SC * 256 / (S * S), None, ALU.mult))
                steps.step(nc.vector.scalar_tensor_tensor(cb[:, :, :], ca[:, :, :], -1.0 / 8, cent[:, :, :], ALU.mult, ALU.mult))
                steps.step(nc.vector.scalar_tensor_tensor(cc[:, :, :], cb[:, :, :], -1.0 / 32, cent[:, :, :], ALU.mult, ALU.mult))
                by_group = lambda t: t[:, :, :].rearrange("p c (g h) -> p c g h", g=G)
                for slots, t in (((0, 1), ca), ((3,), cb), ((5,), cc)):
                    for n in slots:
                        steps.done(nc.vector.tensor_copy(coef[:, :, :, n, :], by_group(t)))
                steps.wait()
                for hi, lo, t in ((0, 2, ca), (3, 4, cb), (5, 6, cc)):
                    last = nc.vector.tensor_tensor(coef[:, :, :, lo, :], by_group(t), coef[:, :, :, hi, :], ALU.subtract)
                last.then_inc(coef_done, 1)
                assert steps.k == CF_STEPS

            def maxima(b, g, hh):
                n = 16 * b + 4 * g + hh
                if hh == 0:
                    dve.wait_ge(nm_in[(g + 2) % G], 16 * (b + 1) if g >= 2 else 16 * b)
                for c in range(QC):
                    dve.wait_ge(s_mm[c % 2], 2 * n + c // 2 + 1)
                    nc.vector.tensor_reduce(nm[g % 2][:, c, hh:hh + 1], s_ps[c % 2][:, :], AX.X, ALU.max,
                                            negate=True).then_inc(max_done[c % 2], 1)

            def context(kind, b, cb, g):
                used(kind, b, f"ctx{(g + 2) % G}")
                heads = misc[:, :].rearrange("p (c h e) -> p c h e", c=QC, e=32)
                nc.vector.reciprocal(rsum[:, :, :], heads[:, :, :, D1]).then_inc(ctx_steps, 1)
                dve.wait_ge(ctx_steps, 4 * cb + g + 1)
                nc.vector.tensor_tensor(ctxt[:, :, g * 32:g * 32 + 32].rearrange("p c (h d) -> p c h d", d=D1), heads[:, :, :, 0:D1],
                                        rsum[:, :, :].unsqueeze(3).to_broadcast([P, QC, G, D1]), ALU.mult).then_inc(misc_out, 1)

            def output(kind, b, cb):
                dve.wait_ge(xres_done, cb + 1)
                used(kind, b, "OUT")
                nc.vector.tensor_tensor(y[:, :, :].rearrange("p c d -> p (c d)"), misc[:, :],
                                        xres[:, :, :].rearrange("p c d -> p (c d)"), ALU.add).then_inc(misc_out, 1)
                dve.wait_ge(misc_out, use(kind, b, "OUT") + 1)
                for c in range(QC):
                    last = nc.vector.bn_stats(st[:, c, :], y[:, c, :])
                last.then_inc(m.stats_ready, 1)
                dve.wait_ge(m.stats_ready, 2 * B + cb + 1)
                vector_gate(nc, m)
                for c in range(QC):
                    last = nc.vector.bn_aggr(mv[:, c, :], st[:, c, :])
                last.then_inc(m.var_ready, 1)

            def norm(kind, b, cb):
                dve.wait_ge(m.rstd_ready, 2 * B + cb + 1)
                for c in range(QC):
                    last = nc.vector.tensor_scalar(m_flat(m.x)[:, ds(cb * S + c * D, D)], y[:, c, :], mv[:, c, 0:1],
                                                   rstd[:, c:c + 1], ALU.subtract, ALU.mult)
                last.then_inc(ln_dve, 1)

            SETUP_STEPS, CF_STEPS = 4, 11
            schedule(dve, {"setup": setup, "XT": low("XT", xt_h, xt_l, xt_hi), "V": values, "GB": gate_bias, "PZ": polynomial,
                           "head": maxima, "ctx": context, "CT": low("CT", ct_h, ct_l, ct_hi), "OUT": output, "norm": norm})

        @block.gpsimd
        def _(pool):
            def setup():
                steps = Steps(pool, vset)
                steps.step(nc.gpsimd.memset(vaug[:, :, :, :].rearrange("p c h e -> p (c h e)"), 0.0))
                steps.step(nc.gpsimd.memset(vaug[:, :, :, D1:D1 + 1].rearrange("p c h e -> p (c h) e"), 1.0))

            def split(name, src, hi, lo, done, at):
                def run(kind, b, nb):
                    pool.wait_ge(misc_out, use(kind, b, name) + 1)
                    pool.wait_ge(parts_out, PARTS * nb)
                    pool_gate(nc, m, slice(0, P))
                    nc.gpsimd.affine_select(out=hi[:, :], in_=src[:, :], compare_op=ALU.is_ge, fill=0.0, base=0,
                                            pattern=[[1, S]], channel_multiplier=0).then_inc(pool_steps, 1)
                    pool.wait_ge(pool_steps, 2 * nb + at)
                    nc.gpsimd.tensor_tensor(lo[:, :], src[:, :], hi[:, :], ALU.subtract).then_inc(done, 1)
                return run

            def values(nb, g):
                if not (isinstance(nb, int) and nb == 0):
                    pool.wait_ge(pv_mm, 16 * (nb - 1) + 4 * g + 4)
                by_head = lambda a: a.rearrange("p c (g h d) -> p c g h d", g=G, h=G)[:, :, g, :, :]
                bias = m.a_bv[:, :].unsqueeze(1).to_broadcast([P, QC, D])
                nc.gpsimd.tensor_tensor(vaug[:, :, G * g:G * g + G, 0:D1], by_head(v32[:, :].rearrange("p (c d) -> p c d", d=D)),
                                        by_head(bias), ALU.add).then_inc(vaug_done, 1)

            def first_values():
                pool.wait_ge(misc_out, use("prep0", 0, "V") + 1)
                for g in range(G):
                    values(0, g)

            def slot(kind, b, at):
                if kind in ("middle", "last") and at in (2, 6):
                    values(b, 2 + at // 4)
                if kind in ("first", "middle") and at in (10, 14):
                    if at == 10:
                        pool.wait_ge(misc_out, use(kind, b, "V") + 1)
                    values(b + 1, at // 4 - 2)
                if kind != "first" and at == 4:
                    xb = m_flat(m.x)[:, ds((b - 1) * S, S)].rearrange("p (c d) -> p c d", d=D)
                    nc.gpsimd.tensor_tensor(xres[:, :, :], xb, m.a_bo[:, :].unsqueeze(1).to_broadcast([P, QC, D]),
                                            ALU.add).then_inc(xres_done, 1)

            def output(kind, b, cb):
                layer_norm_gpsimd(nc, pool, m, 2 * B + cb, mv, ve, rstd)

            schedule(pool, {"setup": setup, "prepared": first_values, "slot": slot, "Q": split("Q", q32, q_h, q_l, q_split, 1),
                            "K": split("K", k32, k_h, k_l, k_split, 2), "OUT": output})


def moe_capacity_phase(nc, io, out, m):
    with ExitStack() as ctx:
        sb = lambda name, shape, dt: ctx.enter_context(nc.sbuf_tensor(name, shape, dt))
        sem = lambda name: ctx.enter_context(nc.semaphore("c_" + name))
        FC = F1 // P
        HALF = CAP // 2
        SLOTS = E1 * CAP
        OUT_OF_RANGE = float(1 << 20)
        wg_h, wg_l = (sb(n, [P, E1], F16) for n in ("cwg_h", "cwg_l"))
        logit, expo, held, onehot, onehot_pos = (sb(n, [P, NCH, E1], F32) for n in ("c_logit", "c_expo", "c_held", "c_onehot", "c_onehot_pos"))
        prefix = [sb(f"c_prefix{k}", [P, NCH, E1], F32) for k in range(2)]
        onehot16 = sb("c_onehot16", [P, NCH, E1], F16)
        lmax, esum, best, pos, over, away, slot = (sb(n, [P, NCH], F32) for n in ("c_lmax", "c_esum", "c_best", "c_pos", "c_over", "c_away", "c_slot"))
        to_slot, from_slot = (sb(n, [P, NCH], U32) for n in ("c_to_slot", "c_from_slot"))
        tri, ones = (sb(n, [P, P], F16) for n in ("tri_ones", "all_ones"))
        zeros = sb("c_zeros", [P, SLOTS], F32)
        xe = sb("c_xe", [HALF, 2 * E1, D], F32)
        xe_t = [sb(f"c_xe_t{k}", [P, CAP], F32) for k in range(2)]
        hid = [sb(f"c_hid{k}", [P, FC, CAP], F32) for k in range(2)]
        ye = sb("c_ye", [HALF, 2 * E1, D], F32)
        yg = sb("c_yg", [P, NCH, D], F32)
        y = sb("c_y", [P, QC, D], F32)
        res = [sb(f"c_res{k}", [P, QC, D], F32) for k in range(2)]
        st = sb("c_st", [P, QC, 6], F32)
        mv = sb("c_mv", [P, QC, 2], F32)
        ve = sb("c_ve", [P, QC], F32)
        rstd = sb("c_rstd", [P, QC], F32)
        bank = lambda name: ctx.enter_context(nc.psum_tensor(name, [P, 512], F32))
        xt_ps = [bank(f"c_xt_ps{k}") for k in range(2)]
        y_ps = [bank(f"c_y_ps{k}") for k in range(2)]
        hid_ps = [ctx.enter_context(nc.psum_tensor(f"c_hid_ps{k}", [P, 2, 512], F32)) for k in range(2)]
        slot_rows = nc.dram_tensor("slot_rows", (SLOTS, D), F32).ap()
        expert_rows = nc.dram_tensor("expert_rows", (SLOTS + 1, D), F32).ap()

        xt_mm, xt_hi, xt_lo, lg_mm, steps_done, shifted, exps_done, onehot_done, count_mm = (sem(n) for n in (
            "xt_mm", "xt_hi", "xt_lo", "lg_mm", "steps", "shifted", "exps", "onehot_done", "count_mm"))
        slots_done, tri_in, zeros_set, zeroed, scattered, xe_in, h_mm, relu_done, y_mm, y_out, stored = (sem(n) for n in (
            "slots_done", "tri_in", "zeros_set", "zeroed", "scattered", "xe_in", "h_mm", "relu_done", "y_mm", "y_out", "stored"))
        out_ready = sem("out_ready")
        gathered = [sem(f"gathered{k}") for k in range(2)]
        out_stored = [sem(f"out_stored{k}") for k in range(2)]
        block = ctx.enter_context(nc.Block())
        E_LOADS = 16

        @block.sync
        def _(sp):
            sp.dma_start(tri[:, :], io["c_tri"]).then_inc(tri_in, 16)
            sp.wait_ge(zeros_set, 1)
            sp.dma_start(slot_rows.rearrange("(p r) d -> p (r d)", p=P), zeros[:, :]).then_inc(zeroed, 16)
            sp.dma_start(expert_rows[SLOTS:SLOTS + 1, :], zeros[0:1, 0:D]).then_inc(zeroed, 16)
            sp.wait_ge(scattered, 16 * NCH)
            sp.dma_start(xe[:, :, :], slot_rows.rearrange("(t p) d -> p t d", p=HALF)).then_inc(xe_in, E_LOADS)
            for e in range(E1):
                sp.wait_ge(y_out, e + 1)
                sp.dma_start(expert_rows[e * CAP:(e + 1) * CAP, :].rearrange("(t p) d -> p t d", p=HALF),
                             ye[:, 2 * e:2 * e + 2, :]).then_inc(stored, 16)
            for t in range(B):
                sp.wait_ge(out_ready, t + 1)
                sp.dma_start(out[t].rearrange("(c p) d -> p c d", p=P), res[t % 2][:, :, :]).then_inc(out_stored[t % 2], 16)
            for k in range(2):
                sp.wait_ge(out_stored[k], 16 * (B // 2))
            sp.wait_ge(tri_in, 16)

        def router(pe, t):
            pe.wait_ge(xt_lo, t + 1)
            for c in range(QC):
                ch = t * QC + c
                o = y_ps[0][:, ch * E1:(ch + 1) * E1]
                xs = slice(ch * P, (ch + 1) * P)
                nc.tensor.matmul(o, m.xt_h[:, xs], wg_h[:, :], start=True, stop=False)
                nc.tensor.matmul(o, m.xt_h[:, xs], wg_l[:, :], start=False, stop=False)
                last = nc.tensor.matmul(o, m.xt_l[:, xs], wg_h[:, :], start=False, stop=True)
            last.then_inc(lg_mm, 1)

        @block.tensor
        def _(pe):
            for t in range(B):
                if t >= 2:
                    pe.wait_ge(xt_lo, t - 1)
                for c in range(QC):
                    last = nc.tensor.transpose(xt_ps[t % 2][:, c * P:(c + 1) * P], m.x[:, t * QC + c, :], m.ident[:, :])
                last.then_inc(xt_mm, 1)
                if t >= 1:
                    router(pe, t - 1)
            router(pe, B - 1)
            pe.wait_ge(tri_in, 16)
            pe.wait_ge(onehot_done, 1)
            o16 = onehot16[:, :, :].rearrange("p c e -> p (c e)")
            nc.tensor.matmul(y_ps[1][:, 0:NCH * E1], tri[:, :], o16, start=True, stop=True)
            nc.tensor.matmul(y_ps[1][:, NCH * E1:], ones[:, :], o16, start=True, stop=True).then_inc(count_mm, 1)
            pe.wait_ge(xe_in, E_LOADS)
            pe.wait_ge(m.e_loaded, 48)

            def rows_t(e):
                if e >= 2:
                    pe.wait_ge(xt_hi, B + e - 1)
                for j in range(2):
                    mm = nc.tensor.transpose(xt_ps[e % 2][:, j * HALF:(j + 1) * HALF], xe[:, 2 * e + j, :],
                                             m.ident[0:HALF, 0:HALF])
                mm.then_inc(xt_mm, 1)

            def hidden(e):
                pe.wait_ge(xt_hi, B + e + 1)
                if e >= 2:
                    pe.wait_ge(relu_done, e - 1)
                for f in range(FC):
                    mm = nc.tensor.matmul(hid_ps[e % 2][:, f // 2, (f % 2) * CAP:(f % 2 + 1) * CAP],
                                          m.e_w1[:, e, f * P:(f + 1) * P], xe_t[e % 2][:, :], start=True, stop=True)
                mm.then_inc(h_mm, 1)

            def output(e):
                pe.wait_ge(relu_done, e + 1)
                if e >= 2:
                    pe.wait_ge(y_out, e - 1)
                for j in range(2):
                    for f in range(FC):
                        mm = nc.tensor.matmul(y_ps[e % 2][0:HALF, j * D:(j + 1) * D],
                                              hid[e % 2][:, f, j * HALF:(j + 1) * HALF], m.e_w2[:, e, f, :],
                                              start=(f == 0), stop=(f == FC - 1))
                mm.then_inc(y_mm, 1)

            rows_t(0)
            rows_t(1)
            hidden(0)
            for e in range(E1):
                if e + 2 < E1:
                    rows_t(e + 2)
                if e + 1 < E1:
                    hidden(e + 1)
                output(e)

        @block.scalar
        def _(act):
            nc.scalar.preload_act_table(ACT.Exp)
            for t in range(B):
                act.wait_ge(xt_mm, t + 1)
                nc.scalar.activation(m.xt_h[:, t * S:(t + 1) * S], xt_ps[t % 2][:, :], ACT.Copy).then_inc(xt_hi, 1)
            act.wait_ge(shifted, 1)
            nc.scalar.activation(expo[:, :, :], logit[:, :, :], ACT.Exp).then_inc(exps_done, 1)

            def rows_t(e):
                act.wait_ge(xt_mm, B + e + 1)
                if e >= 2:
                    act.wait_ge(h_mm, e - 1)
                nc.scalar.activation(xe_t[e % 2][:, :], xt_ps[e % 2][:, 0:CAP], ACT.Copy).then_inc(xt_hi, 1)

            rows_t(0)
            rows_t(1)
            for e in range(E1):
                act.wait_ge(h_mm, e + 1)
                if e >= 2:
                    act.wait_ge(y_mm, e - 1)
                nc.scalar.activation(hid[e % 2][:, :, :].rearrange("p (b f) n -> p b (f n)", b=2), hid_ps[e % 2][:, :, 0:2 * CAP],
                                     ACT.Relu).then_inc(relu_done, 1)
                if e + 2 < E1:
                    rows_t(e + 2)

        @block.vector
        def _(dve):
            steps = Steps(dve, steps_done)
            wide = lambda a: a.unsqueeze(2).to_broadcast([P, NCH, E1])
            iota = m.iota8[:, :].unsqueeze(1).to_broadcast([P, NCH, E1])
            dve.wait_ge(m.e_loaded, 48)
            steps.done(nc.vector.memset(ones[:, :], 1.0))
            steps.step(nc.vector.tensor_copy(wg_h[:, :], m.e_wg[:, :]))
            steps.step(nc.vector.tensor_tensor(wg_l[:, :], m.e_wg[:, :], wg_h[:, :], ALU.subtract))
            for t in range(B):
                dve.wait_ge(xt_hi, t + 1)
                nc.vector.tensor_tensor(m.xt_l[:, t * S:(t + 1) * S], xt_ps[t % 2][:, :], m.xt_h[:, t * S:(t + 1) * S],
                                        ALU.subtract).then_inc(xt_lo, 1)
            dve.wait_ge(lg_mm, B)
            lg = y_ps[0][:, 0:NCH * E1].rearrange("p (c e) -> p c e", e=E1)
            steps.step(nc.vector.tensor_reduce(lmax[:, :], lg, AX.X, ALU.max))
            nc.vector.tensor_tensor(logit[:, :, :], lg, wide(lmax[:, :]), ALU.subtract).then_inc(shifted, 1)
            dve.wait_ge(exps_done, 1)
            steps.done(nc.vector.tensor_reduce(esum[:, :], expo[:, :, :], AX.X, ALU.add))
            steps.step(nc.vector.tensor_scalar(held[:, :, :], expo[:, :, :], 1.0, -float(E1), ALU.is_ge, ALU.mult))
            steps.step(nc.vector.tensor_tensor(held[:, :, :], held[:, :, :], iota, ALU.add))
            steps.step(nc.vector.tensor_reduce(best[:, :], held[:, :, :], AX.X, ALU.min))
            steps.step(nc.vector.tensor_tensor(onehot[:, :, :], held[:, :, :], wide(best[:, :]), ALU.is_equal))
            nc.vector.tensor_copy(onehot16[:, :, :], onehot[:, :, :]).then_inc(onehot_done, 1)
            steps.done(nc.vector.reciprocal(esum[:, :], esum[:, :]))
            steps.done(nc.vector.tensor_scalar(best[:, :], best[:, :], float(E1), None, ALU.add))
            dve.wait_ge(count_mm, 1)
            totals = y_ps[1][:, NCH * E1:].rearrange("p (c e) -> p c e", e=E1)
            steps.done(nc.vector.memset(prefix[0][:, 0:1, :], 0.0))
            steps.step(nc.vector.tensor_copy(prefix[0][:, 1:, :], totals[:, 0:NCH - 1, :]))
            k, d = 0, 1
            while d < NCH:
                a, b = prefix[k], prefix[1 - k]
                steps.done(nc.vector.tensor_copy(b[:, 0:d, :], a[:, 0:d, :]))
                steps.step(nc.vector.tensor_tensor(b[:, d:, :], a[:, d:, :], a[:, 0:NCH - d, :], ALU.add))
                k, d = 1 - k, 2 * d
            counts = y_ps[1][:, 0:NCH * E1].rearrange("p (c e) -> p c e", e=E1)
            steps.step(nc.vector.tensor_tensor(held[:, :, :], counts, prefix[k][:, :, :], ALU.add))
            steps.step(nc.vector.tensor_tensor(onehot_pos[:, :, :], held[:, :, :], onehot[:, :, :], ALU.mult))
            steps.step(nc.vector.tensor_reduce(pos[:, :], onehot_pos[:, :, :], AX.X, ALU.add))
            steps.done(nc.vector.scalar_tensor_tensor(slot[:, :], best[:, :], float(CAP), pos[:, :], ALU.mult, ALU.add))
            steps.done(nc.vector.tensor_scalar(over[:, :], pos[:, :], float(CAP), None, ALU.is_gt))
            steps.step(nc.vector.tensor_scalar(away[:, :], best[:, :], float(NT), OUT_OF_RANGE, ALU.mult, ALU.add))
            steps.step(nc.vector.tensor_tensor(over[:, :], over[:, :], away[:, :], ALU.mult))
            steps.step(nc.vector.scalar_tensor_tensor(slot[:, :], slot[:, :], -1.0, over[:, :], ALU.add, ALU.add))
            nc.vector.tensor_copy(to_slot[:, :], slot[:, :]).then_inc(slots_done, 1)
            nc.vector.tensor_scalar(from_slot[:, :], slot[:, :], float(SLOTS), None, ALU.min).then_inc(slots_done, 1)
            for e in range(E1):
                dve.wait_ge(y_mm, e + 1)
                nc.vector.tensor_copy(ye[:, 2 * e:2 * e + 2, :], y_ps[e % 2][0:HALF, 0:2 * D].rearrange("p (j d) -> p j d", d=D)).then_inc(y_out, 1)
            for t in range(B):
                k = t % 2
                dve.wait_ge(gathered[k], 16 * QC * (t // 2 + 1))
                if t >= 1:
                    dve.wait_ge(out_ready, t)
                for c in range(QC):
                    ch = t * QC + c
                    steps.done(nc.vector.scalar_tensor_tensor(y[:, c, :], yg[:, ch, :], esum[:, ch:ch + 1], m.x[:, ch, :], ALU.mult, ALU.add))
                steps.wait()
                if t >= 2:
                    dve.wait_ge(out_stored[k], 16 * (t // 2))
                layer_norm_vector(nc, dve, m, 3 * B + t, y, st, mv, rstd, res[k]).then_inc(out_ready, 1)

        @block.gpsimd
        def _(pool):
            nc.gpsimd.memset(zeros[:, :], 0.0).then_inc(zeros_set, 1)
            pool.wait_ge(zeroed, 32)
            pool.wait_ge(slots_done, 2)
            for ch in range(NCH):
                nc.gpsimd.indirect_dma_start(out=slot_rows[:, :], out_offset=bass.IndirectOffsetOnAxis(ap=to_slot[:, ch:ch + 1], axis=0),
                                             in_=m.x[:, ch, :], in_offset=None, bounds_check=SLOTS - 1,
                                             oob_is_err=False).then_inc(scattered, 16)
            pool.wait_ge(stored, 16 * E1)

            def gather(t):
                for ch in range(t * QC, (t + 1) * QC):
                    nc.gpsimd.indirect_dma_start(out=yg[:, ch, :], out_offset=None, in_=expert_rows[:, :],
                                                 in_offset=bass.IndirectOffsetOnAxis(ap=from_slot[:, ch:ch + 1], axis=0),
                                                 bounds_check=SLOTS, oob_is_err=False).then_inc(gathered[t % 2], 16)

            gather(0)
            gather(1)
            for t in range(B):
                layer_norm_gpsimd(nc, pool, m, 3 * B + t, mv, ve, rstd)
                if t + 2 < B:
                    gather(t + 2)


def m_flat(t):
    a = t[tuple(slice(None) for _ in t.shape)]
    names = "abcd"[:len(t.shape) - 1]
    return a if len(names) == 1 else a.rearrange(f"p {' '.join(names)} -> p ({' '.join(names)})")


class Memory:
    pass


def build(nc, io, out):
    ctx = ExitStack()
    with ctx:
        sb = lambda name, shape, dt: ctx.enter_context(nc.sbuf_tensor(name, shape, dt))
        m = Memory()
        m.x = sb("x_tok", [P, NCH, D], F32)
        m.ident = sb("ident", [P, P], F32)
        m.mhalf = sb("mhalf", [P, QC], F32)
        m.eps = sb("ln_eps", [P, QC], F32)
        m.gate_v = sb("gate_v", [P, 1], F32)
        m.gate = sb("gate", [P, QC], F32)
        m.x_loaded = [ctx.enter_context(nc.semaphore(f"x_loaded{b}")) for b in range(B)]
        m.var_ready, m.rstd_ready, m.ln_pool = (ctx.enter_context(nc.semaphore(n)) for n in ("var_ready", "rstd_ready", "ln_pool"))
        m.stats_ready = ctx.enter_context(nc.semaphore("stats_ready"))
        m.xt_h = sb("xt_h", [P, NT + S], F16)
        m.xt_l = sb("xt_l", [P, NT + S], F16)
        m.w1_raw = sb("w1_raw", [P, E0, F0], F32)
        m.w2_raw = sb("w2_raw", [P, E0, F0 // P, D], F32)
        m.wg_raw = sb("wg_raw", [P, E0], F32)
        m.bg_bc = sb("bg_bc", [P, E0], F32)
        m.b1_rows = sb("b1_rows", [E0 * F0 // P, P], F32)
        m.b2_rows = sb("b2_rows", [E0, D], F32)
        m.iota8 = sb("iota8", [P, E0], F32)
        m.f0_loaded = ctx.enter_context(nc.semaphore("f0_loaded"))
        m.F0_LOADS = 7 * 16
        m.a_w = sb("a_w_raw", [P, 5, D], F32)
        m.a_wfg = sb("a_wfg", [P, D], F32)
        m.a_cols = sb("a_cols", [P, 6], F32)
        m.a_bv = sb("a_bv", [P, D], F32)
        m.a_bo = sb("a_bo", [P, D], F32)
        m.e_w1 = sb("e_w1", [P, E1, F1], F32)
        m.e_w2 = sb("e_w2", [P, E1, F1 // P, D], F32)
        m.e_wg = sb("e_wg", [P, E1], F32)
        m.e_loaded = ctx.enter_context(nc.semaphore("e_loaded"))
        m.a_loaded = ctx.enter_context(nc.semaphore("a_loaded"))
        with ExitStack() as c0:
            sb0 = lambda name, shape, dt: c0.enter_context(nc.sbuf_tensor(name, shape, dt))
            m.w_h = sb0("w_h", [P, PAIRS, 512], F16)
            m.w_l = sb0("w_l", [P, PAIRS, 512], F16)
            m.wo_h = sb0("wo_h", [P, PAIRS, D], F16)
            m.wo_l = sb0("wo_l", [P, PAIRS, D], F16)
            m.k_h = [sb0(f"k_h{h}", [P, S], F16) for h in range(2)]
            m.k_l = [sb0(f"k_l{h}", [P, S], F16) for h in range(2)]
            m.q_mult = sb0("q_mult", [P, 2, S], F32)
            m.q_bias = sb0("q_bias", [P, 2, PAIRS], F32)
            m.bo_bc = sb0("bo_bc", [P, D], F32)
            m.causal = sb0("causal", [P, P], BF16)
            m.ident_bf = sb0("ident_bf", [P, P], BF16)
            m.zeros = sb0("zeros", [P, S], F16)
            setup_phase(nc, io, m)
            rel_attention_phase(nc, io, m)
        moe_top2_phase(nc, io, m)
        gauss_attention_phase(nc, io, m)
        moe_capacity_phase(nc, io, out, m)


_INPUTS = [
    "L0_attn_input", "L0_attn_qkv", "L0_attn_q_bias", "L0_attn_positional", "L0_attn_out_kernel", "L0_attn_out_bias",
    "L0_ffn_Wg", "L0_ffn_bg", "L0_ffn_W1", "L0_ffn_b1", "L0_ffn_W2", "L0_ffn_b2",
    "L1_attn_wq", "L1_attn_bq", "L1_attn_wk", "L1_attn_bk", "L1_attn_wv", "L1_attn_bv", "L1_attn_wo", "L1_attn_bo",
    "L1_attn_wfq", "L1_attn_bfq", "L1_attn_wfg", "L1_attn_bfg", "L1_attn_up", "L1_attn_uz",
    "L1_ffn_gate_w", "L1_ffn_w1", "L1_ffn_w2",
]


def kernel(**inputs):
    import concourse.bacc as bacc
    from concourse.bass_utils import run_bass_kernel_spmd

    nc = bacc.Bacc("TRN2", target_bir_lowering=False, num_devices=1)
    arrays, io = {}, {}
    for name in _INPUTS:
        arrays[f"in_{name}_dram"] = np.ascontiguousarray(inputs[name])
    for name, table in shape_constants().items():
        arrays[f"in_{name}_dram"] = table
    for dram, a in arrays.items():
        io[dram[3:-5]] = nc.dram_tensor(dram, a.shape, mybir.dt.from_np(a.dtype), kind="ExternalInput").ap()
    out = nc.dram_tensor("out_0_dram", (B, S, D), F32, kind="ExternalOutput").ap()
    build(nc, io, out)
    r = run_bass_kernel_spmd(nc, [arrays], core_ids=[0])
    return r.results[0]["out_0_dram"]
```

```python
from contextlib import ExitStack

import numpy as np

import concourse.bass as bass
from concourse import mybir

F32 = mybir.dt.float32
F16 = mybir.dt.float16
BF16 = mybir.dt.bfloat16
U32 = mybir.dt.uint32
ALU = mybir.AluOpType
ACT = mybir.ActivationFunctionType
AX = mybir.AxisListType
ds = bass.ds

P = 128
B, S, D = 8, 512, 128
NT = B * S
NCH = NT // P
QC = S // P
LN_EPS = 1e-5

H0, HD, FREQS, MAX_PERIOD = 16, 64, 32, 1250
PAIRS = H0 // 2
W_SCALE = (3.0 * D * HD * H0) ** -0.25
O_SCALE = (H0 * HD * D) ** -0.25
QK_SCALE = HD ** -0.25
P_SCALE = 64.0

E0, F0 = 8, 2 * D

H1 = 16
D1 = D // H1

E1, F1, CAP = 8, 512, 160


def shape_constants():
    pos = np.arange(S, dtype=np.float64)
    idx = np.arange(FREQS)
    ang = pos[None, :] * (MAX_PERIOD ** (-(idx // 2 * 2) / FREQS))[:, None]
    sin, cos = np.sin(ang), np.cos(ang)
    odd = (idx % 2 == 1)[:, None]
    alpha, beta = np.where(odd, cos, sin), np.where(odd, sin, -cos)
    t_scale = W_SCALE * np.sqrt(2.0) * FREQS ** -0.5 * HD ** -0.5
    rel = np.concatenate([alpha, beta]) * t_scale
    plain = np.full((HD, S), W_SCALE * QK_SCALE)
    q_mult = np.stack([np.concatenate([plain, rel]), np.concatenate([rel, plain])], 1)
    k_tab = np.tile(np.concatenate([cos, sin]), (2, 1))
    qi, ki = np.arange(P)[:, None], np.arange(P)[None, :]
    causal = np.where(ki <= qi, 0.0, -1e30)
    j = (np.arange(S) - (S - 1) / 2) / 16
    j2_h = (j * j).astype(np.float16)
    j2_l = (j * j - j2_h).astype(np.float16)
    one = np.ones(S)
    key_rows = np.stack([-j2_h / 8, -j2_l / 8, -j2_h / 8, j / 2, j / 2, -one / 2, -one / 2, one])
    return {
        "c_tri": np.triu(np.ones((P, P))).astype(np.float16),
        "c_key_rows": key_rows.astype(np.float16),
        "c_q_mult": q_mult.astype(np.float32),
        "c_k_tab": k_tab.astype(np.float32),
        "c_causal": causal.astype(np.float32),
        "c_ident": np.eye(P, dtype=np.float32),
        "c_iota8": np.tile(np.arange(8, dtype=np.float32), (P, 1)),
    }


class Steps:

    def __init__(self, eng, sem, base=0):
        self.eng, self.sem, self.base, self.k = eng, sem, base, 0

    def done(self, ins):
        ins.then_inc(self.sem, 1)
        self.k += 1

    def wait(self):
        self.eng.wait_ge(self.sem, self.base + self.k)

    def step(self, ins):
        self.done(ins)
        self.wait()


def vector_gate(nc, m):
    return nc.vector.memset(m.gate_v[:, :], 0.0)


def layer_norm_stats(nc, dve, m, n, y, st, mv):
    for c in range(QC):
        last = nc.vector.bn_stats(st[:, c, :], y[:, c, :])
    last.then_inc(m.stats_ready, 1)
    dve.wait_ge(m.stats_ready, n + 1)
    vector_gate(nc, m)
    for c in range(QC):
        last = nc.vector.bn_aggr(mv[:, c, :], st[:, c, :])
    last.then_inc(m.var_ready, 1)


def layer_norm_apply(nc, dve, m, n, y, mv, rstd, out):
    dve.wait_ge(m.rstd_ready, n + 1)
    for c in range(QC):
        last = nc.vector.tensor_scalar(out[:, c, :], y[:, c, :], mv[:, c, 0:1], rstd[:, c:c + 1],
                                       ALU.subtract, ALU.mult)
    return last


def pool_gate(nc, m, rows):
    nc.gpsimd.tensor_tensor(m.gate[rows, 0:1], m.mhalf[rows, 0:1], m.mhalf[rows, 1:2], ALU.add)


def layer_norm_gpsimd(nc, pool, m, n, mv, ve, rstd):
    steps = Steps(pool, m.ln_pool, n)
    pool.wait_ge(m.var_ready, n + 1)
    steps.step(nc.gpsimd.tensor_tensor(ve[:, :], mv[:, :, 1], m.eps[:, :], ALU.add))
    nc.gpsimd.tensor_tensor(rstd[:, :], ve[:, :], m.mhalf[:, :], ALU.pow).then_inc(m.rstd_ready, 1)


def setup_phase(nc, io, m):
    with ExitStack() as ctx:
        sb = lambda name, shape, dt: ctx.enter_context(nc.sbuf_tensor(name, shape, dt))
        sem = lambda name: ctx.enter_context(nc.semaphore(name))
        w_raw = sb("w_raw", [P, 3, H0, HD], F32)
        wo_raw = sb("wo_raw", [P, PAIRS, D], F32)
        posit = sb("posit", [FREQS, H0 * HD], F32)
        qb_rows = sb("qb_rows", [PAIRS, P], F32)
        qb_cols = sb("qb_cols", [P, PAIRS], F32)
        wq_t = sb("wq_t", [P, PAIRS, P], F32)
        pos_t = sb("pos_t", [P, PAIRS, P], F32)
        tab32 = sb("tab32", [P, S], F32)
        mask32 = sb("mask32", [P, P], F32)
        tp = [ctx.enter_context(nc.psum_tensor(f"tp{i}", [P, 512], F32)) for i in range(2)]
        wps = ctx.enter_context(nc.psum_tensor("wps", [P, 2, 512], F32))
        pps = ctx.enter_context(nc.psum_tensor("pps", [P, 512], F32))
        bps = ctx.enter_context(nc.psum_tensor("bps", [P, 512], F32))

        x_in, ident_in, w_in, misc_in = sem("x_in"), sem("ident_in"), sem("w_in"), sem("misc_in")
        xt_mm, xt_hi, xt_lo = sem("xt_mm"), sem("xt_hi"), sem("xt_lo")
        wt_mm, wt_out, g_mm, g_hi, dve_steps = sem("wt_mm"), sem("wt_out"), sem("g_mm"), sem("g_hi"), sem("su_steps")
        act_done = sem("act_done")
        block = ctx.enter_context(nc.Block())

        @block.sync
        def _(sp):
            sp.dma_start(m.ident[:, :], io["c_ident"]).then_inc(ident_in, 16)
            for b in range(B):
                sp.dma_start(m.x[:, b * QC:(b + 1) * QC, :],
                             io["L0_attn_input"][b].rearrange("(c p) d -> p c d", p=P)).then_inc(m.x_loaded[b], 16)

        @block.scalar
        def _(act):
            act.dma_start(w_raw[:, :, :, :], io["L0_attn_qkv"]).then_inc(w_in, 16)
            act.dma_start(posit[:, :], io["L0_attn_positional"].rearrange("f n h -> f (n h)")).then_inc(misc_in, 16)
            act.dma_start(qb_rows[:, :], io["L0_attn_q_bias"].rearrange("(a n) h -> a (n h)", n=2)).then_inc(misc_in, 16)
            act.dma_start(wo_raw[:, :, :], io["L0_attn_out_kernel"].rearrange("(a p) d -> p a d", p=P)).then_inc(misc_in, 16)
            act.dma_start(tab32[:, :], io["c_k_tab"]).then_inc(misc_in, 16)
            act.dma_start(m.q_mult[:, :, :], io["c_q_mult"]).then_inc(misc_in, 16)
            act.dma_start(mask32[:, :], io["c_causal"]).then_inc(misc_in, 16)
            act.dma_start(m.bo_bc[:, :], io["L0_attn_out_bias"].rearrange("(a d) -> a d", a=1).broadcast_to([P, D])).then_inc(misc_in, 16)
            for b in range(B):
                act.wait_ge(xt_mm, b + 1)
                nc.scalar.activation(m.xt_h[:, b * S:(b + 1) * S], tp[b % 2][:, :], ACT.Copy).then_inc(xt_hi, 1)
            act.wait_ge(wt_mm, 1)
            nc.scalar.activation(wq_t[:, :, :].rearrange("p a b -> p (a b)").rearrange("p (a b) -> p a b", a=2), wps[:, :, :], ACT.Copy).then_inc(act_done, 1)
            act.wait_ge(g_mm, 2)
            nc.scalar.activation(m.w_h[:, :, 64:192], wps[:, :, :].rearrange("p a (b n) -> p (a b) n", n=P),
                                 ACT.Copy).then_inc(g_hi, 1)

        @block.tensor
        def _(pe):
            pe.wait_ge(ident_in, 16)
            for b in range(B):
                pe.wait_ge(m.x_loaded[b], 16)
                if b >= 2:
                    pe.wait_ge(xt_lo, b - 1)
                for c in range(QC):
                    last = nc.tensor.transpose(tp[b % 2][:, c * P:(c + 1) * P], m.x[:, b * QC + c, :], m.ident[:, :])
                last.then_inc(xt_mm, 1)
            pe.wait_ge(w_in, 16)
            for a in range(PAIRS):
                last = nc.tensor.transpose(wps[:, a // 4, (a % 4) * P:(a % 4 + 1) * P],
                                           w_raw[:, 0, 2 * a:2 * a + 2, :].rearrange("p n h -> p (n h)"), m.ident[:, :])
            last.then_inc(wt_mm, 1)
            pe.wait_ge(misc_in, 112)
            for a in range(PAIRS):
                last = nc.tensor.transpose(pps[:, a * FREQS:(a + 1) * FREQS], posit[:, a * P:(a + 1) * P],
                                           m.ident[0:FREQS, 0:FREQS])
            last = nc.tensor.transpose(pps[:, 256:256 + PAIRS], qb_rows[:, :], m.ident[0:PAIRS, 0:PAIRS])
            last.then_inc(wt_mm, 1)
            pe.wait_ge(act_done, 1)
            pe.wait_ge(wt_out, 1)
            for a in range(PAIRS):
                nc.tensor.matmul(bps[0:64, a:a + 1], pos_t[:, a, 64:128], qb_cols[:, a:a + 1], start=True, stop=True)
                last = nc.tensor.matmul(bps[64:128, a:a + 1], pos_t[:, a, 0:64], qb_cols[:, a:a + 1], start=True, stop=True)
            last.then_inc(g_mm, 1)
            for a in range(PAIRS):
                last = nc.tensor.matmul(wps[:, a // 4, (a % 4) * P:(a % 4 + 1) * P], wq_t[:, a, :], pos_t[:, a, :],
                                        start=True, stop=True)
            last.then_inc(g_mm, 1)

        @block.vector
        def _(dve):
            steps = Steps(dve, dve_steps)
            steps.done(nc.vector.memset(pos_t[:, :, :], 0.0))
            steps.done(nc.vector.memset(m.zeros[:, :], 0.0))
            steps.done(nc.vector.memset(m.xt_h[:, NT:NT + S], 0.0))
            steps.done(nc.vector.memset(m.xt_l[:, NT:NT + S], 0.0))
            for b in range(B):
                dve.wait_ge(xt_hi, b + 1)
                nc.vector.tensor_tensor(m.xt_l[:, b * S:(b + 1) * S], tp[b % 2][:, :], m.xt_h[:, b * S:(b + 1) * S],
                                        ALU.subtract).then_inc(xt_lo, 1)
            dve.wait_ge(w_in, 16)
            parts = [(0, 64, w_raw[:, 0, 0::2, :]), (192, 256, w_raw[:, 0, 1::2, :]),
                     (256, 384, w_raw[:, 1, :, :].rearrange("p (a n) h -> p a (n h)", n=2)),
                     (384, 512, w_raw[:, 2, :, :].rearrange("p (a n) h -> p a (n h)", n=2))]
            for lo, hi, src in parts:
                steps.done(nc.vector.tensor_copy(m.w_h[:, :, lo:hi], src))
            steps.wait()
            for lo, hi, src in parts:
                steps.done(nc.vector.tensor_tensor(m.w_l[:, :, lo:hi], src, m.w_h[:, :, lo:hi], ALU.subtract))
            dve.wait_ge(misc_in, 112)
            dve.wait_ge(wt_mm, 2)
            for h in range(2):
                r = slice(64 * h, 64 * h + 64)
                for k in range(2):
                    steps.done(nc.vector.tensor_copy(pos_t[r, :, 64 * h + 32 * k:64 * h + 32 * k + 32],
                                                     pps[r, 0:256].rearrange("p (a f) -> p a f", f=FREQS)))
            nc.vector.tensor_copy(qb_cols[:, :], pps[:, 256:256 + PAIRS]).then_inc(wt_out, 1)
            steps.done(nc.vector.tensor_copy(m.wo_h[:, :, :], wo_raw[:, :, :]))
            for h in range(2):
                steps.done(nc.vector.tensor_copy(m.k_h[h][:, :], tab32[:, :]))
            steps.done(nc.vector.tensor_copy(m.causal[:, :], mask32[:, :]))
            steps.done(nc.vector.tensor_copy(m.ident_bf[:, :], m.ident[:, :]))
            steps.wait()
            nc.vector.tensor_tensor(m.wo_l[:, :, :], wo_raw[:, :, :], m.wo_h[:, :, :], ALU.subtract)
            for h in range(2):
                nc.vector.tensor_tensor(m.k_l[h][:, :], tab32[:, :], m.k_h[h][:, :], ALU.subtract)
            dve.wait_ge(g_mm, 1)
            dve.wait_ge(wt_out, 1)
            inv = 1.0 / W_SCALE
            nc.vector.tensor_scalar(m.q_bias[0:64, 0, :], qb_cols[0:64, :], inv, None, ALU.mult)
            nc.vector.tensor_scalar(m.q_bias[64:128, 0, :], bps[64:128, 0:PAIRS], inv, None, ALU.mult)
            nc.vector.tensor_scalar(m.q_bias[0:64, 1, :], bps[0:64, 0:PAIRS], inv, None, ALU.mult)
            nc.vector.tensor_scalar(m.q_bias[64:128, 1, :], qb_cols[64:128, :], inv, None, ALU.mult)
            dve.wait_ge(g_hi, 1)
            nc.vector.tensor_tensor(m.w_l[:, :, 64:192], wps[:, :, :].rearrange("p a (b n) -> p (a b) n", n=P),
                                    m.w_h[:, :, 64:192], ALU.subtract)

        @block.gpsimd
        def _(pool):
            nc.gpsimd.memset(m.mhalf[:, :], -0.5)
            nc.gpsimd.memset(m.eps[:, :], LN_EPS)


def rel_attention_phase(nc, io, m):
    with ExitStack() as ctx:
        sb = lambda name, shape, dt: ctx.enter_context(nc.sbuf_tensor(name, shape, dt))
        sem = lambda name: ctx.enter_context(nc.semaphore(name))
        ps = lambda name: ctx.enter_context(nc.psum_tensor(name, [P, 512], F32))
        q32 = [sb(f"q32_{h}", [P, S], F32) for h in range(2)]
        q_h = [sb(f"q_h{h}", [P, S], F16) for h in range(2)]
        q_l = [sb(f"q_l{h}", [P, S], F16) for h in range(2)]
        k32 = sb("k32", [P, S], F32)
        v_h = sb("v_h", [P, QC, P], F16)
        v_l = sb("v_l", [P, QC, P], F16)
        PW = P * QC * (QC + 1) // 2
        prob = [sb(f"prob{h}", [P, PW], F32) for h in range(2)]
        pt_h = [sb(f"pt_h{h}", [P, PW], F16) for h in range(2)]
        pt_l = [sb(f"pt_l{h}", [P, PW], F16) for h in range(2)]
        o_h = sb("o_h", [P, S], F16)
        o_l = sb("o_l", [P, S], F16)
        nmax = [sb(f"nmax{h}", [P, QC], F32) for h in range(2)]
        sums = [sb(f"sums{h}", [P, QC], F32) for h in range(2)]
        rsum = [sb(f"rsum{h}", [P, QC], F32) for h in range(2)]
        y = sb("ln_y", [P, QC, D], F32)
        st = sb("ln_st", [P, QC, 6], F32)
        mv = sb("ln_mv", [P, QC, 2], F32)
        ve = sb("ln_ve", [P, QC], F32)
        rstd = sb("ln_rstd", [P, QC], F32)
        score_ps = [ps(f"score_ps{u}") for u in range(3)]
        pt_ps = [ps(f"pt_ps{u}") for u in range(2)]
        proj_ps, pv_ps, out_ps = ps("proj_ps"), ps("pv_ps"), ps("out_ps")

        pair = lambda name: [sem(f"{name}{h}") for h in range(2)]
        count = lambda n, u: 3 * n + u + 1
        q_mm, q_out, q_split = pair("q_mm"), pair("q_out"), pair("q_split")
        k_mm, k_out, k_split = sem("k_mm"), sem("k_out"), pair("k_split")
        v_mm, v_hi, v_lo = sem("v_mm"), sem("v_hi"), sem("v_lo")
        s_mm, max_done, exp_done = pair("s_mm"), pair("max_done"), pair("exp_done")
        p_ready = pair("p_ready")
        t_mm, pt_hi, pt_lo = pair("t_mm"), pair("pt_hi"), pair("pt_lo")
        pv_mm, o_hi, o_lo, out_mm, y_done = sem("pv_mm"), sem("o_hi"), sem("o_lo"), sem("out_mm"), sem("y_done")
        dve_steps, pool_steps = sem("ra_dve"), sem("ra_pool")
        ln_dve, bias_in, r_ready = sem("ra_lnd"), sem("bias_in"), sem("r_ready")

        UNIT_CHUNKS = [[(3, 0)], [(2, 0), (0, 384)], [(1, 0)]]
        P_OFF = [P * c * (c + 1) // 2 for c in range(QC)]
        T_UNITS = [[(0, 0)], [(1, 0), (3, 384)], [(2, 0)]]
        T_OFF, T_WIDTH = [0, 512, 1024], [512, 512, 256]
        J_OFF = {0: 0, 1: 512, 3: 896, 2: 1024}

        CLOSE = "close"

        def schedule(eng, first_front, body, close, last):
            first_front()
            body(0, 0, 0, False, False, None)
            body(1, 0, 1, False, True, None)
            with eng.Fori(2, PAIRS - 1) as p:
                body(p, 0, p, False, True, p - 2)
            body(PAIRS - 1, 0, PAIRS - 1, True, True, PAIRS - 3)
            with eng.Fori(1, B) as b:
                body(PAIRS * b, b, 0, False, True, PAIRS - 2)
                body(PAIRS * b + 1, b, 1, False, True, CLOSE)
                with eng.Fori(2, PAIRS - 1) as p:
                    body(PAIRS * b + p, b, p, False, True, p - 2)
                body(PAIRS * b + PAIRS - 1, b, PAIRS - 1, True, True, PAIRS - 3)
            last()

        block = ctx.enter_context(nc.Block())

        @block.sync
        def _(sp):
            load = lambda dst, src: sp.dma_start(dst, src).then_inc(m.f0_loaded, 16)
            load(m.w1_raw[:, :, :], io["L0_ffn_W1"].rearrange("e d f -> d e f"))
            load(m.w2_raw[:, :, :, :], io["L0_ffn_W2"].rearrange("e (c p) d -> p e c d", p=P))
            load(m.wg_raw[:, :], io["L0_ffn_Wg"])
            load(m.bg_bc[:, :], io["L0_ffn_bg"].rearrange("(a e) -> a e", a=1).broadcast_to([P, E0]))
            load(m.b1_rows[:, :], io["L0_ffn_b1"].rearrange("e (c p) -> (e c) p", p=P))
            load(m.b2_rows[:, :], io["L0_ffn_b2"])
            load(m.iota8[:, :], io["c_iota8"])
            loads = 0

            def load(dst, src, scattered=False):
                nonlocal loads
                sp.dma_start(dst, src, allow_slow_non_contiguous=scattered).then_inc(m.a_loaded, 16)
                loads += 16

            for k, name in ((0, "wq"), (1, "wk"), (2, "wv"), (4, "wo")):
                load(m.a_w[:, k, :], io[f"L1_attn_{name}"])
            for dst, name in ((m.a_w[:, 3, :], "wfq"), (m.a_wfg[:, :], "wfg")):
                for g in range(4):
                    load(dst[32 * g:32 * g + 32, :], io[f"L1_attn_{name}"].rearrange("(g h d) n -> g d h n", h=4, d=D1)[g])
            for k, name in enumerate(("bq", "bk")):
                for g in range(4):
                    load(m.a_cols[32 * g:32 * g + 32, k:k + 1],
                         io[f"L1_attn_{name}"].rearrange("(g h d a) -> g d h a", h=4, d=D1, a=1)[g], scattered=True)
            for k, name in enumerate(("bfq", "bfg")):
                load(m.a_cols[:, 2 + k:3 + k], io[f"L1_attn_{name}"].rearrange("(p a) -> p a", a=1))
            for k, name in enumerate(("up", "uz")):
                load(m.a_cols[:, 4 + k:5 + k], io[f"L1_attn_{name}"].rearrange("h a d -> (h d) a"))
            for dst, name in ((m.a_bv, "bv"), (m.a_bo, "bo")):
                load(dst[:, :], io[f"L1_attn_{name}"].rearrange("(a d) -> a d", a=1).broadcast_to([P, D]))
            sp.wait_ge(m.f0_loaded, m.F0_LOADS)
            sp.wait_ge(m.a_loaded, loads)
            m.A_LOADS = loads

        @block.tensor
        def _(pe):
            def project_q(h, mth, bx, pw):
                w_hi, w_lo = (t[:, pw, 128 * h:128 * h + 128] if isinstance(pw, int)
                              else m_flat(t)[:, ds(pw * 512 + 128 * h, 128)] for t in (m.w_h, m.w_l))
                x_hi, x_lo = (t[:, ds(bx * S, S)] for t in (m.xt_h, m.xt_l))
                nc.tensor.matmul(proj_ps[:, :], w_hi, x_hi, start=True, stop=False)
                nc.tensor.matmul(proj_ps[:, :], w_lo, x_hi, start=False, stop=False)
                nc.tensor.matmul(proj_ps[:, :], w_hi, x_lo, start=False, stop=True).then_inc(q_mm[h], 1)

            def project_k(bx, pw):
                w_hi, w_lo = (m_flat(t)[:, ds(pw * 512 + 256, 128)] for t in (m.w_h, m.w_l))
                x_hi, x_lo = (t[:, ds(bx * S, S)] for t in (m.xt_h, m.xt_l))
                nc.tensor.matmul(proj_ps[:, :], w_hi, x_hi, start=True, stop=False)
                nc.tensor.matmul(proj_ps[:, :], w_lo, x_hi, start=False, stop=False)
                nc.tensor.matmul(proj_ps[:, :], w_hi, x_lo, start=False, stop=True).then_inc(k_mm, 1)

            def project_v(bx, pw):
                w_hi, w_lo = (m_flat(t)[:, ds(pw * 512 + 384, 128)] for t in (m.w_h, m.w_l))
                for c in range(QC):
                    x_hi, x_lo = (t[:, ds(bx * S + c * P, P)] for t in (m.xt_h, m.xt_l))
                    o = proj_ps[:, c * P:(c + 1) * P]
                    nc.tensor.matmul(o, x_hi, w_hi, start=True, stop=False)
                    nc.tensor.matmul(o, x_hi, w_lo, start=False, stop=False)
                    mm = nc.tensor.matmul(o, x_lo, w_hi, start=False, stop=True)
                mm.then_inc(v_mm, 1)

            def scores(h, n):
                pe.wait_ge(q_split[h], n + 1)
                pe.wait_ge(k_split[h], n + 1)
                for u in range(3):
                    if h == 1 or not (isinstance(n, int) and n == 0):
                        pe.wait_ge(exp_done[1 - h], count(n + h - 1, u))
                    for c, col in UNIT_CHUNKS[u]:
                        w = P * (c + 1)
                        o, qs = score_ps[u][:, col:col + w], slice(c * P, (c + 1) * P)
                        nc.tensor.matmul(o, q_h[h][:, qs], m.k_h[h][:, 0:w], start=True, stop=False)
                        nc.tensor.matmul(o, q_h[h][:, qs], m.k_l[h][:, 0:w], start=False, stop=False)
                        nc.tensor.matmul(o, q_l[h][:, qs], m.k_h[h][:, 0:w], start=False, stop=False)
                        mm = nc.tensor.matmul(o[:, w - P:w], m.ident_bf[:, :], m.causal[:, :], start=False, stop=True)
                    mm.then_inc(s_mm[h], 1)

            def transposes(h, n, u_list):
                for u in u_list:
                    if u == 0:
                        pe.wait_ge(p_ready[h], n + 1)
                    at = 3 * h + u
                    ph, pu = divmod(at - 2 if at >= 2 else at + 4, 3)
                    if at >= 2 or not (isinstance(n, int) and n == 0):
                        pe.wait_ge(pt_lo[ph], count(n if at >= 2 else n - 1, pu))
                    for j, col in T_UNITS[u]:
                        for c in range(j, QC):
                            mm = nc.tensor.transpose(pt_ps[at % 2][:, col + (c - j) * P:col + (c - j + 1) * P],
                                                     prob[h][:, P_OFF[c] + j * P:P_OFF[c] + (j + 1) * P], m.ident[:, :])
                    mm.then_inc(t_mm[h], 1)

            def weighted_values(n):
                for h in range(2):
                    pe.wait_ge(pt_lo[h], count(n, 2))
                pe.wait_ge(v_lo, n + 1)
                pe.wait_ge(o_lo, n)
                for j in range(QC):
                    for term in range(3):
                        pt, v = [(pt_h, v_h), (pt_h, v_l), (pt_l, v_h)][term]
                        for h in range(2):
                            mm = nc.tensor.matmul(pv_ps[64 * h:64 * h + 64, j * P:S], v[:, j, 64 * h:64 * h + 64],
                                                  pt[h][:, J_OFF[j]:J_OFF[j] + S - j * P],
                                                  start=(j == 0 and term == 0), stop=(j == QC - 1 and term == 2))
                mm.then_inc(pv_mm, 1)

            def open_output(b):
                pe.wait_ge(y_done, b)
                nc.tensor.matmul(out_ps[:, :], m.zeros[:, 0:P], m.zeros[:, :], start=True, stop=False, skip_group_check=True)

            def project_out(n, pw, end):
                pe.wait_ge(o_lo, n + 1)
                w_hi, w_lo = (m_flat(t)[:, ds(pw * P, P)] for t in (m.wo_h, m.wo_l))
                for c in range(QC):
                    cs = slice(c * P, (c + 1) * P)
                    for k, (a, w) in enumerate([(o_h, w_hi), (o_h, w_lo), (o_l, w_hi)]):
                        mm = nc.tensor.matmul(out_ps[:, cs], a[:, cs], w, start=False,
                                              stop=(end and c == QC - 1 and k == 2), skip_group_check=True)
                mm.then_inc(out_mm, 1)

            def first_front():
                project_k(0, 0)
                pe.wait_ge(k_out, 1)
                project_q(0, 0, 0, 0)
                pe.wait_ge(q_out[0], 1)
                project_q(1, 0, 0, 0)
                open_output(0)

            def body(n, b, p, wrap, lag, out):
                bx, pw = (b + 1, 0) if wrap else (b, p + 1)
                pe.wait_ge(q_out[1], n + 1)
                project_k(bx, pw)
                scores(0, n)
                if out is not None:
                    project_out(n - 2, PAIRS - 1 if out is CLOSE else out, out is CLOSE)
                if lag:
                    transposes(1, n - 1, [0, 1])
                pe.wait_ge(k_out, n + 2)
                project_q(0, n + 1, bx, pw)
                if lag:
                    transposes(1, n - 1, [2])
                pe.wait_ge(q_out[0], n + 2)
                project_v(b, p)
                if lag:
                    weighted_values(n - 1)
                scores(1, n)
                transposes(0, n, [0, 1])
                pe.wait_ge(v_lo, n + 1)
                project_q(1, n + 1, bx, pw)
                transposes(0, n, [2])
                if out is CLOSE:
                    open_output(b)

            def last():
                n = B * PAIRS - 1
                transposes(1, n, [0, 1, 2])
                weighted_values(n)
                project_out(n - 1, PAIRS - 2, False)
                project_out(n, PAIRS - 1, True)

            schedule(pe, first_front, body, None, last)

        @block.scalar
        def _(act):
            def exps(h, n, u_list):
                for u in u_list:
                    act.wait_ge(max_done[h], count(n, u))
                    if u == 0:
                        act.wait_ge(t_mm[h], 3 * n)
                    for c, col in UNIT_CHUNKS[u]:
                        w = P * (c + 1)
                        ins = nc.scalar.activation(prob[h][:, P_OFF[c]:P_OFF[c] + w], score_ps[u][:, col:col + w], ACT.Exp,
                                                   bias=nmax[h][:, c:c + 1], accum_out=sums[h][:, c:c + 1])
                    ins.then_inc(exp_done[h], 1)

            def pt_high(h, n, u_list):
                for u in u_list:
                    act.wait_ge(t_mm[h], count(n, u))
                    if u == 0:
                        act.wait_ge(pv_mm, n)
                    w = T_WIDTH[u]
                    nc.scalar.activation(pt_h[h][:, T_OFF[u]:T_OFF[u] + w], pt_ps[(3 * h + u) % 2][:, 0:w],
                                         ACT.Copy).then_inc(pt_hi[h], 1)

            def normalise(n):
                act.wait_ge(r_ready, n + 1)
                for c in range(QC):
                    pr = prob[0][:, P_OFF[c]:P_OFF[c] + P * (c + 1)]
                    ins = nc.scalar.activation(pr, pr, ACT.Copy, scale=rsum[0][:, c:c + 1])
                ins.then_inc(p_ready[0], 1)

            def o_high(n):
                act.wait_ge(pv_mm, n + 1)
                if not (isinstance(n, int) and n < 1):
                    act.wait_ge(out_mm, n)
                nc.scalar.activation(o_h[:, :], pv_ps[:, :], ACT.Copy).then_inc(o_hi, 1)

            def v_high(n, pv_behind):
                act.wait_ge(v_mm, n + 1)
                act.wait_ge(pv_mm, n)
                nc.scalar.activation(v_h[:, :, :].rearrange("p c n -> p (c n)"), proj_ps[:, :], ACT.Copy,
                                     scale=W_SCALE).then_inc(v_hi, 1)

            def k_copy(n):
                act.wait_ge(k_mm, n + 1)
                act.wait_ge(k_split[1], n)
                nc.scalar.activation(k32[:, :], proj_ps[:, :], ACT.Copy, scale=W_SCALE * QK_SCALE).then_inc(k_out, 1)

            def body(n, b, p, wrap, lag, out):
                k_copy(n + 1)
                exps(0, n, [0])
                if lag:
                    pt_high(1, n - 1, [0, 1])
                exps(0, n, [1])
                if lag:
                    pt_high(1, n - 1, [2])
                exps(0, n, [2])
                normalise(n)
                if lag:
                    o_high(n - 1)
                v_high(n, lag is not None)
                pt_high(0, n, [0])
                exps(1, n, [0])
                pt_high(0, n, [1])
                exps(1, n, [1])
                pt_high(0, n, [2])
                exps(1, n, [2])

            def last():
                n = B * PAIRS - 1
                pt_high(1, n, [0, 1, 2])
                o_high(n)

            nc.scalar.preload_act_table(ACT.Exp)
            schedule(act, lambda: k_copy(0), body, None, last)

        @block.vector
        def _(dve):
            def maxima(h, n):
                for u in range(3):
                    dve.wait_ge(s_mm[h], count(n, u))
                    for c, col in UNIT_CHUNKS[u]:
                        ins = nc.vector.tensor_reduce(nmax[h][:, c:c + 1], score_ps[u][:, col:col + P * (c + 1)],
                                                      AX.X, ALU.max, negate=True)
                    ins.then_inc(max_done[h], 1)

            def reciprocals(h, n):
                dve.wait_ge(exp_done[h], count(n, 2))
                nc.vector.reciprocal(rsum[h][:, :], sums[h][:, :]).then_inc(dve_steps, 1)
                dve.wait_ge(dve_steps, 2 * n + h + 1)

            def scaled_reciprocals(n):
                reciprocals(0, n)
                nc.vector.tensor_scalar(rsum[0][:, :], rsum[0][:, :], P_SCALE, None, ALU.mult).then_inc(r_ready, 1)

            def normalise(n):
                h = 1
                reciprocals(h, n)
                for c in range(QC):
                    pr = prob[h][:, P_OFF[c]:P_OFF[c] + P * (c + 1)]
                    ins = nc.vector.tensor_scalar(pr, pr, rsum[h][:, c:c + 1], P_SCALE, ALU.mult, ALU.mult)
                ins.then_inc(p_ready[h], 1)

            def pt_low(h, n, u_list):
                for u in u_list:
                    dve.wait_ge(pt_hi[h], count(n, u))
                    w = T_WIDTH[u]
                    nc.vector.tensor_tensor(pt_l[h][:, T_OFF[u]:T_OFF[u] + w], pt_ps[(3 * h + u) % 2][:, 0:w],
                                            pt_h[h][:, T_OFF[u]:T_OFF[u] + w], ALU.subtract).then_inc(pt_lo[h], 1)

            def q_evac(h, n, pw):
                dve.wait_ge(q_mm[h], n + 1)
                dve.wait_ge(q_split[h], n)
                nc.vector.scalar_tensor_tensor(q32[h][:, :], proj_ps[:, :], m_flat(m.q_bias)[:, ds(PAIRS * h + pw, 1)],
                                               m.q_mult[:, h, :], ALU.add, ALU.mult).then_inc(q_out[h], 1)

            def o_low(n):
                dve.wait_ge(o_hi, n + 1)
                nc.vector.tensor_tensor(o_l[:, :], pv_ps[:, :], o_h[:, :], ALU.subtract).then_inc(o_lo, 1)

            def v_low(n):
                dve.wait_ge(v_hi, n + 1)
                nc.vector.scalar_tensor_tensor(v_l[:, :, :].rearrange("p c n -> p (c n)"), proj_ps[:, :], W_SCALE,
                                               v_h[:, :, :].rearrange("p c n -> p (c n)"), ALU.mult, ALU.subtract).then_inc(v_lo, 1)

            def add_bias(b):
                xb = m_flat(m.x)[:, ds(b * S, S)].rearrange("p (c d) -> p c d", d=D)
                nc.vector.tensor_tensor(xb, xb, m.bo_bc[:, :].unsqueeze(1).to_broadcast([P, QC, D]), ALU.add).then_inc(bias_in, 1)

            def batch_sum(b):
                dve.wait_ge(out_mm, PAIRS * (b + 1))
                dve.wait_ge(bias_in, b + 1)
                nc.vector.scalar_tensor_tensor(y[:, :, :].rearrange("p c d -> p (c d)"), out_ps[:, :], O_SCALE / P_SCALE,
                                               m_flat(m.x)[:, ds(b * S, S)], ALU.mult, ALU.add).then_inc(y_done, 1)

            def batch_stats(b):
                dve.wait_ge(y_done, b + 1)
                layer_norm_stats(nc, dve, m, b, y, st, mv)

            def batch_norm(b):
                layer_norm_apply(nc, dve, m, b, y, mv, rstd,
                                 m_flat(m.x)[:, ds(b * S, S)].rearrange("p (c d) -> p c d", d=D)).then_inc(ln_dve, 1)

            def body(n, b, p, wrap, lag, out):
                maxima(0, n)
                if lag:
                    pt_low(1, n - 1, [0])
                q_evac(0, n + 1, 0 if wrap else p + 1)
                if lag:
                    pt_low(1, n - 1, [1, 2])
                behind = wrap and not (isinstance(b, int) and b == 0)
                if behind:
                    batch_stats(b - 1)
                scaled_reciprocals(n)
                if out is CLOSE:
                    dve.wait_ge(ln_dve, b)
                    batch_sum(b - 1)
                maxima(1, n)
                v_low(n)
                pt_low(0, n, [0])
                q_evac(1, n + 1, 0 if wrap else p + 1)
                pt_low(0, n, [1])
                if lag:
                    o_low(n - 1)
                pt_low(0, n, [2])
                normalise(n)
                if wrap:
                    add_bias(b)
                if behind:
                    batch_norm(b - 1)

            def first_front():
                vector_gate(nc, m).then_inc(ln_dve, 1)
                q_evac(0, 0, 0)
                q_evac(1, 0, 0)

            def last():
                n = B * PAIRS - 1
                pt_low(1, n, [0, 1, 2])
                o_low(n)
                batch_sum(B - 1)
                batch_stats(B - 1)
                batch_norm(B - 1)

            schedule(dve, first_front, body, None, last)

        @block.gpsimd
        def _(pool):
            def split(rows, src, hi, lo, chain_n):
                pool_gate(nc, m, rows)
                nc.gpsimd.affine_select(out=hi, in_=src, compare_op=ALU.is_ge, fill=0.0, base=0,
                                        pattern=[[1, S]], channel_multiplier=0).then_inc(pool_steps, 1)
                pool.wait_ge(pool_steps, chain_n)
                return nc.gpsimd.tensor_tensor(lo, src, hi, ALU.subtract)

            def split_q(h, n):
                pool.wait_ge(q_out[h], n + 1)
                pool.wait_ge(s_mm[h], 3 * n)
                pool.wait_ge(k_split[h], n + 1)
                split(slice(0, P), q32[h][:, :], q_h[h][:, :], q_l[h][:, :], 4 * n + 2 + 2 * h).then_inc(q_split[h], 1)

            def split_k(h, n):
                if h == 0:
                    pool.wait_ge(k_out, n + 1)
                pool.wait_ge(s_mm[h], 3 * n)
                pool.wait_ge(q_split[1 - h], n + h)
                r = slice(64 * h, 64 * h + 64)
                split(r, k32[r, :], m.k_h[h][r, :], m.k_l[h][r, :], 4 * n + 1 + 2 * h).then_inc(k_split[h], 1)

            def front(n):
                for h in range(2):
                    split_k(h, n)
                    split_q(h, n)

            def body(n, b, p, wrap, lag, out):
                front(n + 1)
                if wrap and not (isinstance(b, int) and b == 0):
                    layer_norm_gpsimd(nc, pool, m, b - 1, mv, ve, rstd)

            def last():
                layer_norm_gpsimd(nc, pool, m, B - 1, mv, ve, rstd)

            schedule(pool, lambda: front(0), body, None, last)


def moe_top2_phase(nc, io, m):
    with ExitStack() as ctx:
        sb = lambda name, shape, dt: ctx.enter_context(nc.sbuf_tensor(name, shape, dt))
        sem = lambda name: ctx.enter_context(nc.semaphore(name))
        FC = F0 // P
        w1_h, w1_l = (sb(n, [P, E0 * F0], F16) for n in ("w1_h", "w1_l"))
        w2_h, w2_l = (sb(n, [P, E0 * FC * D], F16) for n in ("w2_h", "w2_l"))
        wg_h, wg_l = (sb(n, [P, E0], F16) for n in ("wg_h", "wg_l"))
        b1_cols = sb("b1_cols", [P, E0 * FC], F32)
        logit = sb("logit", [P, NCH, E0], F32)
        lmax = sb("lmax", [P, NCH], F32)
        top = sb("top", [P, NCH, 8], F32)
        topi = sb("topi", [P, NCH, 8], U32)
        topf = sb("topf", [P, NCH, 8], F32)
        tsum = sb("tsum", [P, NCH], F32)
        pick = [sb(f"pick{k}", [P, NCH, E0], F32) for k in range(2)]
        comb = sb("comb", [P, NCH, E0], F32)
        comb_t = sb("comb_t", [E0, NT], F32)
        hid32 = [[sb(f"hid32_{k}{c}", [P, S], F32) for c in range(FC)] for k in range(2)]
        hid_h = [[sb(f"hid_h{k}{c}", [P, S], F16) for c in range(FC)] for k in range(2)]
        hid_l = [[sb(f"hid_l{k}{c}", [P, S], F16) for c in range(FC)] for k in range(2)]
        st = sb("f_st", [P, QC, 6], F32)
        mv = sb("f_mv", [P, QC, 2], F32)
        ve = sb("f_ve", [P, QC], F32)
        rstd = sb("f_rstd", [P, QC], F32)
        banks = [ctx.enter_context(nc.psum_tensor(f"fps{i}", [P, 512], F32)) for i in range(8)]
        hid_ps, y_ps, xt_ps = banks[0:4], banks[4:6], banks[6:8]

        xt_mm, xt_hi, xt_lo, lg_mm = sem("f_xt_mm"), sem("f_xt_hi"), sem("f_xt_lo"), sem("f_lg_mm")
        wg_split, b1_out = sem("f_wg_split"), sem("f_b1_out")
        w_split, b1_mm, shifted, exps_done = sem("f_w_split"), sem("f_b1_mm"), sem("f_shifted"), sem("f_exps")
        dsteps, comb_done, ct_mm, ct_out, b2_mm, b2_out = (sem(n) for n in ("f_steps", "f_comb", "f_ct_mm", "f_ct_out", "f_b2_mm", "f_b2_out"))
        h_mm, h_relu, h_hi, h_lo = ([sem(f"f_{n}{c}") for c in range(FC)] for n in ("h_mm", "h_relu", "h_hi", "h_lo"))
        y_out = [sem(f"f_y_out{k}") for k in range(2)]
        y_mm = sem("f_y_mm")

        def schedule(eng, unit, tile_end):
            with eng.Fori(0, B) as t:
                with eng.Fori(0, E0 // 2 - 1) as i:
                    for k in range(2):
                        unit(E0 * t + 2 * i + k, E0 // 2 * t + i, k, t, 2 * i + k + 1, t, 2 * i + k)
                half = E0 // 2 * t + E0 // 2 - 1
                unit(E0 * t + E0 - 2, half, 0, t, E0 - 1, t, E0 - 2)
                unit(E0 * t + E0 - 1, half, 1, t + 1, 0, t, E0 - 1)
                tile_end(t)

        block = ctx.enter_context(nc.Block())

        def router(pe, t):
            pe.wait_ge(xt_lo, t + 1)
            for c in range(QC):
                ch = t * QC + c
                o = y_ps[0][:, ch * E0:(ch + 1) * E0]
                xs = slice(ch * P, (ch + 1) * P)
                nc.tensor.matmul(o, m.xt_h[:, xs], wg_h[:, :], start=True, stop=False)
                nc.tensor.matmul(o, m.xt_h[:, xs], wg_l[:, :], start=False, stop=False)
                last = nc.tensor.matmul(o, m.xt_l[:, xs], wg_h[:, :], start=False, stop=True)
            last.then_inc(lg_mm, 1)

        @block.tensor
        def _(pe):
            for t in range(B):
                if t >= 2:
                    pe.wait_ge(xt_lo, t - 1)
                for c in range(QC):
                    last = nc.tensor.transpose(xt_ps[t % 2][:, c * P:(c + 1) * P], m.x[:, t * QC + c, :], m.ident[:, :])
                last.then_inc(xt_mm, 1)
                if t == 0:
                    pe.wait_ge(m.f0_loaded, m.F0_LOADS)
                    nc.tensor.transpose(hid_ps[0][:, 0:E0 * FC], m.b1_rows[:, :], m.ident[0:E0 * FC, 0:E0 * FC]).then_inc(b1_mm, 1)
                    pe.wait_ge(wg_split, 2)
                if t >= 1:
                    router(pe, t - 1)
            router(pe, B - 1)
            pe.wait_ge(comb_done, 1)
            for t in range(B):
                if t >= 2:
                    pe.wait_ge(ct_out, t - 1)
                for c in range(QC):
                    last = nc.tensor.transpose(xt_ps[t % 2][0:E0, c * P:(c + 1) * P], comb[:, t * QC + c, :], m.ident[:, :])
                last.then_inc(ct_mm, 1)
            for t in range(B):
                pe.wait_ge(ct_out, t + 1)
                if t >= 2:
                    pe.wait_ge(b2_out, t - 1)
                for c in range(QC):
                    ch = (t * QC + c) * P
                    last = nc.tensor.matmul(y_ps[t % 2][:, c * P:(c + 1) * P], comb_t[:, ch:ch + P], m.b2_rows[:, :],
                                            start=True, stop=True)
                last.then_inc(b2_mm, 1)

            def hidden(n, k, t, e):
                for c in range(FC):
                    w_hi, w_lo = (w[:, ds(e * F0 + c * P, P)] for w in (w1_h, w1_l))
                    x_hi, x_lo = (x[:, ds(t * S, S)] for x in (m.xt_h, m.xt_l))
                    o = hid_ps[2 * k + c][:, :]
                    nc.tensor.matmul(o, w_hi, x_hi, start=True, stop=False)
                    nc.tensor.matmul(o, w_lo, x_hi, start=False, stop=False)
                    nc.tensor.matmul(o, w_hi, x_lo, start=False, stop=True).then_inc(h_mm[c], 1)

            def unit(n, half, k, tn, en, t, e):
                hidden(n + 1, 1 - k, tn, en)
                for c in range(FC):
                    pe.wait_ge(h_lo[c], n + 1)
                pe.wait_ge(y_out[k], half + 1)
                for c in range(QC):
                    cs = slice(c * P, (c + 1) * P)
                    for f in range(FC):
                        w_hi, w_lo = (w[:, ds((e * FC + f) * D, D)] for w in (w2_h, w2_l))
                        for j, (a, w) in enumerate([(hid_h, w_hi), (hid_h, w_lo), (hid_l, w_hi)]):
                            mm = nc.tensor.matmul(y_ps[k][:, cs], a[k][f][:, cs], w, start=(f == 0 and j == 0),
                                                  stop=(f == FC - 1 and j == 2))
                mm.then_inc(y_mm, 1)

            pe.wait_ge(b2_out, B)
            pe.wait_ge(w_split, 4)
            pe.wait_ge(b1_out, 1)
            hidden(0, 0, 0, 0)
            schedule(pe, unit, lambda t: None)

        @block.scalar
        def _(act):
            nc.scalar.preload_act_table(ACT.Exp)
            for t in range(B):
                act.wait_ge(xt_mm, t + 1)
                nc.scalar.activation(m.xt_h[:, t * S:(t + 1) * S], xt_ps[t % 2][:, :], ACT.Copy).then_inc(xt_hi, 1)
                if t == 0:
                    act.wait_ge(b1_mm, 1)
                    nc.scalar.activation(b1_cols[:, :], hid_ps[0][:, 0:E0 * FC], ACT.Copy).then_inc(b1_out, 1)
            act.wait_ge(shifted, 1)
            nc.scalar.activation(logit[:, :, :], logit[:, :, :], ACT.Exp).then_inc(exps_done, 1)
            for t in range(B):
                act.wait_ge(ct_mm, t + 1)
                nc.scalar.activation(comb_t[:, t * S:(t + 1) * S], xt_ps[t % 2][0:E0, :], ACT.Copy).then_inc(ct_out, 1)

            def relu(n, k, e):
                for c in range(FC):
                    act.wait_ge(h_mm[c], n + 1)
                    nc.scalar.activation(hid32[k][c][:, :], hid_ps[2 * k + c][:, :], ACT.Relu,
                                         bias=b1_cols[:, ds(e * FC + c, 1)]).then_inc(h_relu[c], 1)

            act.wait_ge(b1_out, 1)
            relu(0, 0, 0)
            schedule(act, lambda n, half, k, tn, en, t, e: relu(n + 1, 1 - k, en), lambda t: None)

        @block.vector
        def _(dve):
            steps = Steps(dve, dsteps)
            dve.wait_ge(m.f0_loaded, m.F0_LOADS)
            nc.vector.tensor_copy(wg_h[:, :], m.wg_raw[:, :]).then_inc(wg_split, 1)
            dve.wait_ge(wg_split, 1)
            nc.vector.tensor_tensor(wg_l[:, :], m.wg_raw[:, :], wg_h[:, :], ALU.subtract).then_inc(wg_split, 1)
            for t in range(B):
                dve.wait_ge(xt_hi, t + 1)
                nc.vector.tensor_tensor(m.xt_l[:, t * S:(t + 1) * S], xt_ps[t % 2][:, :], m.xt_h[:, t * S:(t + 1) * S],
                                        ALU.subtract).then_inc(xt_lo, 1)
            dve.wait_ge(lg_mm, B)
            lg_ps = y_ps[0][:, 0:NCH * E0].rearrange("p (c e) -> p c e", e=E0)
            steps.step(nc.vector.tensor_tensor(logit[:, :, :], lg_ps, m.bg_bc[:, :].unsqueeze(1).to_broadcast([P, NCH, E0]), ALU.add))
            steps.step(nc.vector.tensor_reduce(lmax[:, :], logit[:, :, :], AX.X, ALU.max))
            nc.vector.tensor_tensor(logit[:, :, :], logit[:, :, :], lmax[:, :].unsqueeze(2).to_broadcast([P, NCH, E0]),
                                    ALU.subtract).then_inc(shifted, 1)
            for hi, raw in ((w1_h, m.w1_raw), (w2_h, m.w2_raw)):
                nc.vector.tensor_copy(hi[:, :], m_flat(raw)).then_inc(w_split, 1)
            dve.wait_ge(exps_done, 1)
            for c in range(NCH):
                steps.done(nc.vector.max(top[:, c, :], logit[:, c, :]))
            steps.wait()
            for c in range(NCH):
                steps.done(nc.vector.max_index(topi[:, c, :], top[:, c, :], logit[:, c, :]))
            steps.step(nc.vector.tensor_tensor(tsum[:, :], top[:, :, 0], top[:, :, 1], ALU.add))
            steps.done(nc.vector.reciprocal(tsum[:, :], tsum[:, :]))
            steps.step(nc.vector.tensor_copy(topf[:, :, :], topi[:, :, :]))
            wide = lambda a: a.unsqueeze(2).to_broadcast([P, NCH, E0])
            for k in range(2):
                steps.done(nc.vector.tensor_tensor(pick[k][:, :, :], m.iota8[:, :].unsqueeze(1).to_broadcast([P, NCH, E0]),
                                                   wide(topf[:, :, k]), ALU.is_equal))
            steps.wait()
            for k in range(2):
                steps.done(nc.vector.tensor_tensor(pick[k][:, :, :], pick[k][:, :, :], wide(top[:, :, k]), ALU.mult))
            steps.wait()
            steps.step(nc.vector.tensor_tensor(comb[:, :, :], pick[0][:, :, :], pick[1][:, :, :], ALU.add))
            nc.vector.tensor_tensor(comb[:, :, :], comb[:, :, :], wide(tsum[:, :]), ALU.mult).then_inc(comb_done, 1)
            for lo, hi, raw in ((w1_l, w1_h, m.w1_raw), (w2_l, w2_h, m.w2_raw)):
                nc.vector.tensor_tensor(lo[:, :], m_flat(raw), hi[:, :], ALU.subtract).then_inc(w_split, 1)
            for t in range(B):
                dve.wait_ge(b2_mm, t + 1)
                xs = m.x[:, t * QC:(t + 1) * QC, :].rearrange("p c d -> p (c d)")
                nc.vector.tensor_tensor(xs, y_ps[t % 2][:, :], xs, ALU.add).then_inc(b2_out, 1)

            def high(n, k):
                for c in range(FC):
                    dve.wait_ge(h_relu[c], n + 1)
                    nc.vector.tensor_copy(hid_h[k][c][:, :], hid32[k][c][:, :]).then_inc(h_hi[c], 1)
                dve.wait_ge(h_hi[0], n + 1)
                nc.vector.tensor_tensor(hid_l[k][0][:, :], hid32[k][0][:, :], hid_h[k][0][:, :], ALU.subtract).then_inc(h_lo[0], 1)

            def unit(n, half, k, tn, en, t, e):
                high(n + 1, 1 - k)
                dve.wait_ge(y_mm, n + 1)
                for c in range(QC):
                    xc = m_flat(m.x)[:, ds(t * S + c * D, D)]
                    ins = nc.vector.scalar_tensor_tensor(xc, y_ps[k][:, c * D:(c + 1) * D],
                                                         m_flat(comb)[:, ds(t * (QC * E0) + c * E0 + e, 1)], xc, ALU.mult, ALU.add)
                ins.then_inc(y_out[k], 1)

            def tile_end(t):
                dve.wait_ge(y_out[1], E0 // 2 * (t + 1) + 1)
                vector_gate(nc, m)
                xt = m_flat(m.x)[:, ds(t * S, S)].rearrange("p (c d) -> p c d", d=D)
                layer_norm_stats(nc, dve, m, B + t, xt, st, mv)
                layer_norm_apply(nc, dve, m, B + t, xt, mv, rstd, xt)

            nc.vector.memset(m.gate_v[:, :], 0.0).then_inc(y_out[0], 1)
            nc.vector.memset(m.gate_v2[:, :], 0.0).then_inc(y_out[1], 1)
            high(0, 0)
            schedule(dve, unit, tile_end)

        @block.gpsimd
        def _(pool):
            def low(n, k):
                pool.wait_ge(h_hi[1], n + 1)
                nc.gpsimd.tensor_tensor(hid_l[k][1][:, :], hid32[k][1][:, :], hid_h[k][1][:, :], ALU.subtract).then_inc(h_lo[1], 1)

            def tile_end(t):
                layer_norm_gpsimd(nc, pool, m, B + t, mv, ve, rstd)

            low(0, 0)
            schedule(pool, lambda n, half, k, tn, en, t, e: low(n + 1, 1 - k), tile_end)


def gauss_attention_phase(nc, io, m):
    with ExitStack() as ctx:
        sb = lambda name, shape, dt: ctx.enter_context(nc.sbuf_tensor(name, shape, dt))
        sem = lambda name: ctx.enter_context(nc.semaphore(name))
        G = 4
        SC = 64.0
        K_SCALE = SC * D1 ** -0.5
        w_h, w_l = (sb(n, [P, 5, P], F16) for n in ("a_w_h", "a_w_l"))
        upz = sb("a_upz", [P, 2 * H1], F32)
        head_mask = sb("a_head_mask", [P, H1], F32)
        bk_s = sb("a_bk_s", [P, 1], F32)
        bf = sb("a_bf", [P, 1], F32)
        gbias = sb("a_gbias", [P, 1], F32)
        qsum = sb("a_qsum", [P, 1], F32)
        ident16 = sb("a_ident16", [P, P], F16)
        xs = sb("a_xs", [P, QC, D], F32)
        xt_h, xt_l = (sb(n, [P, S], F16) for n in ("a_xt_h", "a_xt_l"))
        q32, k32, c32, v32 = (sb(n, [P, S], F32) for n in ("a_q32", "a_k32", "a_c32", "a_v32"))
        q_h, q_l, k_h, k_l, coef_t = (sb(n, [P, S], F16) for n in ("a_q_h", "a_q_l", "a_k_h", "a_k_l", "a_coef_t"))
        epz = sb("a_epz", [P, QC, 2 * H1], F32)
        cent = sb("a_cent", [P, QC, H1], F32)
        ca, cb, cc = (sb(n, [P, QC, H1], F32) for n in ("a_ca", "a_cb", "a_cc"))
        coef = sb("a_coef", [P, QC, G, 8, G], F16)
        qop = sb("a_qop", [P, G, S], F16)
        kop = sb("a_kop", [P, G, G, S], F16)
        vaug = sb("a_vaug", [P, QC, H1, 32], F32)
        nm = [sb(f"a_nm{k}", [P, QC, G], F16) for k in range(2)]
        nm_t = [sb(f"a_nm_t{k}", [G, S], F16) for k in range(2)]
        pt = [[sb(f"a_pt{k}{r}", [P, 2, S], F32) for r in range(2)] for k in range(2)]
        pvs = sb("a_pvs", [P, S], F32)
        rsum = sb("a_rsum", [P, QC, G], F32)
        ctxt = sb("a_ctx", [P, QC, P], F32)
        ct_h, ct_l = (sb(n, [P, S], F16) for n in ("a_ct_h", "a_ct_l"))
        xres = sb("a_xres", [P, QC, D], F32)
        y = sb("a_y", [P, QC, D], F32)
        st = sb("a_st", [P, QC, 6], F32)
        mv = sb("a_mv", [P, QC, 2], F32)
        ve = sb("a_ve", [P, QC], F32)
        rstd = sb("a_rstd", [P, QC], F32)
        s_ps = [ctx.enter_context(nc.psum_tensor(f"a_s{k}", [P, S], F32)) for k in range(2)]
        st_ps = [ctx.enter_context(nc.psum_tensor(f"a_st{r}", [P, 2, S], F32)) for r in range(2)]
        pv_ps = ctx.enter_context(nc.psum_tensor("a_pv", [P, S], F32))
        misc = ctx.enter_context(nc.psum_tensor("a_misc", [P, S], F32))
        misc16 = misc[:, :].bitcast(F16)

        names = lambda *a: [sem("a_" + n) for n in a]
        wsplit, setup_done, kzero, kconst, vset = names("wsplit", "setup_done", "kzero", "kconst", "vset")
        misc_mm, misc_out = names("misc_mm", "misc_out")
        xs_in, xt_hi, ct_hi, q_split, k_split, pool_steps = names("xs_in", "xt_hi", "ct_hi", "q_split", "k_split", "pool_steps")
        cf_steps, coef_done, vaug_done, pvs_done, ctx_steps, xres_done = names(
            "cf_steps", "coef_done", "vaug_done", "pvs_done", "ctx_steps", "xres_done")
        ln_dve, pv_mm, parts_out, cent_done, cf_pool = names("ln_dve", "pv_mm", "parts_out", "cent_done", "cf_pool")
        s_mm, max_done, st_mm, exp_done = ([sem(f"a_{n}{k}") for k in range(2)] for n in ("s_mm", "max_done", "st_mm", "exp_done"))
        op_in = [sem(f"a_op_in{g}") for g in range(G)]
        nm_in = [sem(f"a_nm_in{g}") for g in range(G)]
        OP_LOADS = (1 + G) * 16
        PARTS = 7 * 16
        WSPLITS = 10
        q_dram = nc.dram_tensor("q_parts", (4, 32, G, S), F16).ap()
        k_dram = nc.dram_tensor("k_parts", (3, 32, G, S), F16).ap()

        PREP = ["XT", "Q", "K", "V", "GB", "F", "PZ", "CF"]
        MIDDLE = {4: "nm0", 8: "nm1", 9: "CT", 10: "OUT", 12: "nm2"}
        END = {0: "ctx1", 1: "XT", 2: "Q", 4: "ctx2", 5: "K", 6: "GB", 7: "F", 8: "ctx3", 9: "PZ", 11: "CF", 12: "ctx0",
               13: "V", 15: "nm3"}
        SLOTS = 4 * G
        BEHIND = ["ctx1", "ctx2", "ctx3", "CT", "OUT"]
        PARTS_OF = {"first": ("ahead", "own"), "middle": ("ahead", "own", "behind"), "last": ("own", "behind"), "tail": ("behind",)}

        def part_of(name):
            return "ahead" if name in PREP else "behind" if name in BEHIND else "own"

        def uses(kind):
            order = [t[at] for at in range(SLOTS) for t in (MIDDLE, END) if at in t]
            return [u for u in order if part_of(u) in PARTS_OF[kind]]

        def use(kind, b, name):
            if kind == "prep0":
                return PREP.index(name)
            base = len(PREP)
            if kind != "first":
                base = base + len(uses("first")) + len(uses("middle")) * ((b if kind == "middle" else B - 1) - 1)
            if kind == "tail":
                base = base + len(uses("last"))
            return base + uses(kind).index(name)

        def schedule(eng, do):
            def step(name, *args):
                if name in do:
                    do[name](*args)

            def shared_use(name, kind, b):
                part = part_of(name)
                if part in PARTS_OF[kind]:
                    batch = {"ahead": b + 1, "own": b, "behind": b - 1}[part]
                    if name[-1] in "0123":
                        step(name[:-1], kind, b, batch, int(name[-1]))
                    else:
                        step(name, kind, b, batch)

            def batch(kind, b):
                behind, own = kind != "first", kind != "tail"
                for at in range(SLOTS if own else 12):
                    g, s = divmod(at, G)
                    step("slot", kind, b, at)
                    head = (b, g, s) if own else None
                    unit = ((b, (at - 6) // G, (at - 6) % G, kind == "first" and at == 6) if at >= 6 and own
                            else (b - 1, (at + 10) // G, (at + 10) % G, False) if at < 6 and behind else None)
                    for half, table in ((0, MIDDLE), (1, END)):
                        step("scores", half, head, unit)
                        if half and kind == "tail" and at == 6:
                            step("value", b - 1, G - 1, QC - 1)
                        if half and s == 2 and (at < 8 and behind or at >= 8 and own):
                            step("group_end", *((b - 1, g + 2) if at < 8 else (b, g - 2)))
                        if at in table:
                            shared_use(table[at], kind, b)
                    if at == 11 and behind:
                        step("norm", b - 1)

            step("setup")
            for name in PREP:
                step(name, "prep0", 0, 0)
            step("prepared")
            batch("first", 0)
            with eng.Fori(1, B - 1) as b:
                batch("middle", b)
            batch("last", B - 1)
            batch("tail", B)

        block = ctx.enter_context(nc.Block())

        @block.sync
        def _(sp):
            def setup():
                for dst, src in ((m.e_w1[:, :, :], io["L1_ffn_w1"].rearrange("e d f -> d e f")),
                                 (m.e_w2[:, :, :, :], io["L1_ffn_w2"].rearrange("e (c p) d -> p e c d", p=P)),
                                 (m.e_wg[:, :], io["L1_ffn_gate_w"])):
                    sp.dma_start(dst, src).then_inc(m.e_loaded, 16)
                sp.wait_ge(kzero, 1)
                for hh in range(G):
                    sp.dma_start(kop[96 + hh:P:G, hh, :, :],
                                 io["c_key_rows"].unsqueeze(1).to_broadcast([8, G, S])).then_inc(kconst, 16)
                sp.wait_ge(kconst, 16 * G)

            def spread(nb):
                sp.wait_ge(k_split, nb + 1)
                for g in range(G):
                    sp.wait_ge(op_in[g], OP_LOADS * nb)
                for n, src in ((0, q_h), (1, q_h), (2, q_l)):
                    sp.dma_start(q_dram[n].rearrange("r g n -> g r n"), src[:, :]).then_inc(parts_out, 16)
                for n, src in ((0, k_h), (1, k_l), (2, k_h)):
                    sp.dma_start(k_dram[n].rearrange("r g n -> g r n"), src[:, :]).then_inc(parts_out, 16)

            def spread_coef(kind, b, nb):
                sp.wait_ge(misc_out, use(kind, b, "CF") + 1)
                sp.dma_start(q_dram[3].rearrange("r g n -> g r n"), coef_t[:, :]).then_inc(parts_out, 16)
                sp.wait_ge(parts_out, PARTS * (nb + 1))

            def gather(nb, g):
                if not (isinstance(nb, int) and nb == 0):
                    sp.wait_ge(st_mm[1], 16 * (nb - 1) + 4 * g + 4)
                sp.dma_start(qop[:, g, :], q_dram[:, :, g, :].rearrange("t r n -> (t r) n")).then_inc(op_in[g], 16)
                for hh in range(G):
                    sp.dma_start(kop[hh:96:G, hh, g, :],
                                 k_dram.rearrange("t (d h) g n -> (t d) h g n", h=G)[:, hh, g, :]).then_inc(op_in[g], 16)

            def prepared():
                spread(0)
                spread_coef("prep0", 0, 0)
                for g in range(G):
                    gather(0, g)

            def slot(kind, b, at):
                if kind in ("middle", "last") and at in (1, 5):
                    gather(b, 2 + at // 4)
                if kind in ("first", "middle"):
                    if at == 8:
                        spread(b + 1)
                    if at == 13:
                        spread_coef(kind, b, b + 1)
                        gather(b + 1, 0)
                        gather(b + 1, 1)

            def minus_max(kind, b, _, g):
                sp.wait_ge(misc_out, use(kind, b, f"nm{g}") + 1)
                sp.dma_start(qop[P - G:P, g, :], nm_t[g % 2][:, :]).then_inc(nm_in[g], 16)

            schedule(sp, {"setup": setup, "prepared": prepared, "slot": slot, "nm": minus_max})
            for g in range(G):
                sp.wait_ge(nm_in[g], 16 * B)
            sp.wait_ge(m.e_loaded, 48)
            sp.wait_ge(m.e_loaded, 48)

        @block.tensor
        def _(pe):
            def shared(kind, b, name):
                pe.wait_ge(misc_out, use(kind, b, name))

            def setup():
                pe.wait_ge(wsplit, WSPLITS)

            def tokens_t(kind, b, nb):
                pe.wait_ge(xs_in, nb + 1)
                shared(kind, b, "XT")
                for c in range(QC):
                    mm = nc.tensor.transpose(misc[:, c * P:(c + 1) * P], xs[:, c, :], m.ident[:, :])
                mm.then_inc(misc_mm, 1)

            def features(name, k, xh, xl):
                def run(kind, b, nb):
                    if name == "F":
                        pe.wait_ge(q_split, nb + 1)
                    shared(kind, b, name)
                    nc.tensor.matmul(misc[:, :], w_h[:, k, :], xh[:, :], start=True, stop=False)
                    nc.tensor.matmul(misc[:, :], w_l[:, k, :], xh[:, :], start=False, stop=False)
                    nc.tensor.matmul(misc[:, :], w_h[:, k, :], xl[:, :], start=False, stop=True).then_inc(misc_mm, 1)
                return run

            def rows(name, k, xh, xl):
                def run(kind, b, nb):
                    shared(kind, b, name)
                    for c in range(QC):
                        cs = slice(c * P, (c + 1) * P)
                        nc.tensor.matmul(misc[:, cs], xh[:, cs], w_h[:, k, :], start=True, stop=False)
                        nc.tensor.matmul(misc[:, cs], xh[:, cs], w_l[:, k, :], start=False, stop=False)
                        mm = nc.tensor.matmul(misc[:, cs], xl[:, cs], w_h[:, k, :], start=False, stop=True)
                    mm.then_inc(misc_mm, 1)
                return run

            def gate_bias(kind, b, nb):
                shared(kind, b, "GB")
                nc.tensor.matmul(misc[:, 0:1], m.a_wfg[:, :], qsum[:, :], start=True, stop=True).then_inc(misc_mm, 1)

            def centre_width(kind, b, nb):
                shared(kind, b, "PZ")
                for c in range(QC):
                    mm = nc.tensor.matmul(misc[:, c * 2 * H1:(c + 1) * 2 * H1], c32[:, c * P:(c + 1) * P], upz[:, :],
                                          start=True, stop=True)
                mm.then_inc(misc_mm, 1)

            def coefficients_t(kind, b, nb):
                pe.wait_ge(coef_done, nb + 1)
                shared(kind, b, "CF")
                for c in range(QC):
                    mm = nc.tensor.transpose(misc16[:, c * P:(c + 1) * P],
                                             coef[:, c, :, :, :].rearrange("p g t h -> p (g t h)"), ident16[:, :])
                mm.then_inc(misc_mm, 1)

            def head_scores(b, g, hh, c):
                if hh == 0 and c == 0:
                    pe.wait_ge(op_in[g], OP_LOADS * (b + 1))
                k = c % 2
                pe.wait_ge(max_done[k], 2 * (16 * b + 4 * g + hh) + c // 2)
                nc.tensor.matmul(s_ps[k][:, :], qop[:, g, c * P:(c + 1) * P], kop[:, hh, g, :], start=True,
                                 stop=True).then_inc(s_mm[k], 1)

            def scores(half, head, unit):
                for c in range(2 * half, 2 * half + 2):
                    if head:
                        head_scores(*head, c)
                    if not unit:
                        continue
                    b, g, kc, first = unit
                    if c == 0 and kc == 0:
                        pe.wait_ge(nm_in[g], 16 * (b + 1))
                    if c % 2 == 0:
                        r = c // 2
                        pe.wait_ge(exp_done[r], 16 * b + 4 * g + kc)
                        for i in range(2):
                            mm = nc.tensor.matmul(st_ps[r][:, i, :], kop[:, 2 * r + i, g, kc * P:(kc + 1) * P], qop[:, g, :],
                                                  start=True, stop=True)
                        mm.then_inc(st_mm[r], 1)
                if unit and half and not first:
                    value(*((b, g, kc - 1) if kc else (b, g - 1, QC - 1) if g else (b - 1, G - 1, QC - 1)))

            def value(b, g, kc):
                for r in range(2):
                    pe.wait_ge(exp_done[r], 16 * b + 4 * g + kc + 1)
                if kc == 0:
                    pe.wait_ge(vaug_done, 4 * b + g + 1)
                    pe.wait_ge(pvs_done, 4 * b + g)
                for hh in range(G):
                    mm = nc.tensor.matmul(pv_ps[32 * hh:32 * hh + 32, :], vaug[:, kc, G * g + hh, :],
                                          pt[kc % 2][hh // 2][:, hh % 2, :], start=(kc == 0), stop=(kc == QC - 1))
                mm.then_inc(pv_mm, 1)

            def context(kind, b, cb, g):
                pe.wait_ge(pvs_done, 4 * cb + g + 1)
                shared(kind, b, f"ctx{g}")
                for c in range(QC):
                    mm = nc.tensor.transpose(misc[:, c * P:(c + 1) * P], pvs[:, c * P:(c + 1) * P], m.ident[:, :])
                mm.then_inc(misc_mm, 1)

            def context_t(kind, b, cb):
                shared(kind, b, "CT")
                for c in range(QC):
                    mm = nc.tensor.transpose(misc[:, c * P:(c + 1) * P], ctxt[:, c, :], m.ident[:, :])
                mm.then_inc(misc_mm, 1)

            def maxima_t(kind, b, _, g):
                for k in range(2):
                    pe.wait_ge(max_done[k], 32 * b + 8 * g + 8)
                shared(kind, b, f"nm{g}")
                for c in range(QC):
                    mm = nc.tensor.transpose(misc16[0:G, c * P:(c + 1) * P], nm[g % 2][:, c, :], ident16[:, :])
                mm.then_inc(misc_mm, 1)

            schedule(pe, {"setup": setup, "XT": tokens_t, "Q": features("Q", 0, xt_h, xt_l), "K": features("K", 1, xt_h, xt_l),
                          "V": rows("V", 2, xt_h, xt_l), "GB": gate_bias, "F": features("F", 3, q_h, q_l),
                          "PZ": centre_width, "CF": coefficients_t, "scores": scores, "value": value,
                          "ctx": context, "nm": maxima_t, "CT": context_t, "OUT": rows("OUT", 4, ct_h, ct_l)})

        @block.scalar
        def _(act):
            def setup():
                nc.scalar.preload_act_table(ACT.Exp)
                act.wait_ge(m.a_loaded, m.A_LOADS)
                nc.scalar.activation(bk_s[:, :], m.a_cols[:, 1:2], ACT.Copy, scale=K_SCALE).then_inc(setup_done, 1)
                nc.scalar.activation(xs[:, :, :], m.x[:, 0:QC, :], ACT.Copy).then_inc(xs_in, 1)

            def slot(kind, b, at):
                if at == 0 and kind in ("first", "middle"):
                    nc.scalar.activation(xs[:, :, :].rearrange("p c d -> p (c d)"), m_flat(m.x)[:, ds((b + 1) * S, S)],
                                         ACT.Copy).then_inc(xs_in, 1)

            def used(kind, b, name):
                act.wait_ge(misc_mm, use(kind, b, name) + 1)

            def high(name, dst, signal):
                def run(kind, b, nb):
                    used(kind, b, name)
                    nc.scalar.activation(dst[:, :], misc[:, :], ACT.Copy).then_inc(signal, 1)
                return run

            def queries(kind, b, nb):
                act.wait_ge(q_split, nb)
                used(kind, b, "Q")
                nc.scalar.activation(q32[:, :], misc[:, :], ACT.Identity, bias=m.a_cols[:, 0:1],
                                     accum_out=qsum[:, :]).then_inc(misc_out, 1)

            def keys(kind, b, nb):
                act.wait_ge(k_split, nb)
                act.wait_ge(setup_done, 1)
                used(kind, b, "K")
                nc.scalar.activation(k32[:, :], misc[:, :], ACT.Identity, bias=bk_s[:, :], scale=K_SCALE).then_inc(misc_out, 1)

            def gates(kind, b, nb):
                used(kind, b, "F")
                nc.scalar.activation(c32[:, :], misc[:, :], ACT.Tanh, bias=gbias[:, :]).then_inc(misc_out, 1)

            def sigmoids(kind, b, nb):
                act.wait_ge(coef_done, nb)
                used(kind, b, "PZ")
                nc.scalar.activation(epz[:, :, :].rearrange("p c h -> p (c h)"), misc[:, 0:QC * 2 * H1], ACT.Exp,
                                     scale=-1.0).then_inc(misc_out, 1)

            def coefficients(kind, b, nb):
                act.wait_ge(parts_out, PARTS * nb)
                used(kind, b, "CF")
                nc.scalar.activation(coef_t[:, :], misc16[:, 0:S], ACT.Copy).then_inc(misc_out, 1)

            def exponentials(r, head, unit):
                if not unit:
                    return
                b, g, kc, _ = unit
                n = 16 * b + 4 * g + kc
                act.wait_ge(st_mm[r], n + 1)
                if not isinstance(n, int) or n >= 2:
                    act.wait_ge(pv_mm, n - 1)
                nc.scalar.activation(pt[kc % 2][r][:, :, :], st_ps[r][:, :, :], ACT.Exp, scale=1.0 / SC).then_inc(exp_done[r], 1)

            def group_end(cb, g):
                act.wait_ge(pv_mm, 16 * cb + 4 * g + 4)
                act.wait_ge(ctx_steps, 4 * cb + g)
                nc.scalar.activation(pvs[:, :], pv_ps[:, :], ACT.Copy).then_inc(pvs_done, 1)

            def maxima(kind, b, _, g):
                act.wait_ge(nm_in[(g + 2) % G], 16 * (b + 1) if g >= 2 else 16 * b)
                used(kind, b, f"nm{g}")
                nc.scalar.activation(nm_t[g % 2][:, :], misc16[0:G, 0:S], ACT.Copy).then_inc(misc_out, 1)

            schedule(act, {"setup": setup, "slot": slot, "XT": high("XT", xt_h, xt_hi), "Q": queries, "K": keys, "F": gates,
                           "PZ": sigmoids, "CF": coefficients, "scores": exponentials, "group_end": group_end, "nm": maxima,
                           "CT": high("CT", ct_h, ct_hi)})

        @block.vector
        def _(dve):
            def setup():
                steps = Steps(dve, ln_dve)
                nc.vector.memset(kop[:, :, :, :].rearrange("p a b n -> p (a b n)"), 0.0).then_inc(kzero, 1)
                nc.vector.memset(coef[:, :, :, :, :].rearrange("p c g t h -> p (c g t h)"), 0.0)
                nc.vector.tensor_copy(ident16[:, :], m.ident[:, :])
                dve.wait_ge(m.a_loaded, m.A_LOADS)
                for k in range(5):
                    view = (lambda t: t[:, k, :].rearrange("p (g d h) -> p g d h", g=G, h=G)) if k < 2 else (lambda t: t[:, k, :])
                    raw = m.a_w[:, k, :]
                    if k < 2:
                        raw = raw.rearrange("p (g h d) -> p g d h", g=G, h=G)
                    nc.vector.tensor_copy(view(w_h), raw).then_inc(wsplit, 1)
                    dve.wait_ge(wsplit, 2 * k + 1)
                    nc.vector.tensor_tensor(view(w_l), raw, view(w_h), ALU.subtract).then_inc(wsplit, 1)
                steps.step(nc.vector.tensor_reduce(head_mask[:, :], m.ident[:, :].rearrange("p (h d) -> p h d", d=D1), AX.X, ALU.add))
                for k in range(2):
                    steps.done(nc.vector.tensor_scalar(upz[:, k * H1:(k + 1) * H1], head_mask[:, :], m.a_cols[:, 4 + k:5 + k], None, ALU.mult))
                steps.step(nc.vector.tensor_tensor(bf[:, :], m.a_cols[:, 2:3], m.a_cols[:, 3:4], ALU.add))
                assert steps.k == SETUP_STEPS

            def used(kind, b, name):
                dve.wait_ge(misc_mm, use(kind, b, name) + 1)

            def low(name, hi, lo, signal):
                def run(kind, b, nb):
                    used(kind, b, name)
                    dve.wait_ge(signal, nb + 1)
                    nc.vector.tensor_tensor(lo[:, :], misc[:, :], hi[:, :], ALU.subtract).then_inc(misc_out, 1)
                return run

            def values(kind, b, nb):
                dve.wait_ge(vaug_done, G * nb)
                used(kind, b, "V")
                nc.vector.tensor_copy(v32[:, :], misc[:, :]).then_inc(misc_out, 1)

            def gate_bias(kind, b, nb):
                used(kind, b, "GB")
                nc.vector.scalar_tensor_tensor(gbias[:, :], misc[:, 0:1], 1.0 / S, bf[:, :], ALU.mult, ALU.add).then_inc(misc_out, 1)

            def centres(kind, b, nb):
                steps = Steps(dve, cf_steps, 2 * nb)
                dve.wait_ge(coef_done, nb)
                dve.wait_ge(misc_out, use(kind, b, "PZ") + 1)
                steps.step(nc.vector.tensor_scalar(epz[:, :, :], epz[:, :, :], 1.0, None, ALU.add))
                steps.step(nc.vector.reciprocal(cent[:, :, :], epz[:, :, 0:H1]))
                nc.vector.tensor_scalar(cent[:, :, :], cent[:, :, :], S / 32.0, -(S - 1) / 64, ALU.mult, ALU.add).then_inc(cent_done, 1)

            def maxima(half, head, unit):
                if not head:
                    return
                b, g, hh = head
                n = 16 * b + 4 * g + hh
                if hh == 0 and half == 0:
                    dve.wait_ge(nm_in[(g + 2) % G], 16 * (b + 1) if g >= 2 else 16 * b)
                for c in range(2 * half, 2 * half + 2):
                    dve.wait_ge(s_mm[c % 2], 2 * n + c // 2 + 1)
                    nc.vector.tensor_reduce(nm[g % 2][:, c, hh:hh + 1], s_ps[c % 2][:, :], AX.X, ALU.max,
                                            negate=True).then_inc(max_done[c % 2], 1)

            def context(kind, b, cb, g):
                used(kind, b, f"ctx{g}")
                heads = misc[:, :].rearrange("p (c h e) -> p c h e", c=QC, e=32)
                nc.vector.reciprocal(rsum[:, :, :], heads[:, :, :, D1]).then_inc(ctx_steps, 1)
                dve.wait_ge(ctx_steps, 4 * cb + g + 1)
                nc.vector.tensor_tensor(ctxt[:, :, g * 32:g * 32 + 32].rearrange("p c (h d) -> p c h d", d=D1), heads[:, :, :, 0:D1],
                                        rsum[:, :, :].unsqueeze(3).to_broadcast([P, QC, G, D1]), ALU.mult).then_inc(misc_out, 1)

            def output(kind, b, cb):
                dve.wait_ge(xres_done, cb + 1)
                used(kind, b, "OUT")
                nc.vector.tensor_tensor(y[:, :, :].rearrange("p c d -> p (c d)"), misc[:, :],
                                        xres[:, :, :].rearrange("p c d -> p (c d)"), ALU.add).then_inc(misc_out, 1)
                dve.wait_ge(misc_out, use(kind, b, "OUT") + 1)
                layer_norm_stats(nc, dve, m, 2 * B + cb, y, st, mv)

            def norm(cb):
                layer_norm_apply(nc, dve, m, 2 * B + cb, y, mv, rstd,
                                 m_flat(m.x)[:, ds(cb * S, S)].rearrange("p (c d) -> p c d", d=D)).then_inc(ln_dve, 1)

            SETUP_STEPS = 4
            schedule(dve, {"setup": setup, "XT": low("XT", xt_h, xt_l, xt_hi), "V": values, "GB": gate_bias, "PZ": centres,
                           "scores": maxima, "ctx": context, "CT": low("CT", ct_h, ct_l, ct_hi), "OUT": output, "norm": norm})

        @block.gpsimd
        def _(pool):
            def setup():
                steps = Steps(pool, vset)
                steps.step(nc.gpsimd.memset(vaug[:, :, :, :].rearrange("p c h e -> p (c h e)"), 0.0))
                steps.step(nc.gpsimd.memset(vaug[:, :, :, D1:D1 + 1].rearrange("p c h e -> p (c h) e"), 1.0))

            def split(name, src, hi, lo, done, at):
                def run(kind, b, nb):
                    pool.wait_ge(misc_out, use(kind, b, name) + 1)
                    pool.wait_ge(parts_out, PARTS * nb)
                    pool_gate(nc, m, slice(0, P))
                    nc.gpsimd.affine_select(out=hi[:, :], in_=src[:, :], compare_op=ALU.is_ge, fill=0.0, base=0,
                                            pattern=[[1, S]], channel_multiplier=0).then_inc(pool_steps, 1)
                    pool.wait_ge(pool_steps, 2 * nb + at)
                    nc.gpsimd.tensor_tensor(lo[:, :], src[:, :], hi[:, :], ALU.subtract).then_inc(done, 1)
                return run

            def values(nb, g):
                if not (isinstance(nb, int) and nb == 0):
                    pool.wait_ge(pv_mm, 16 * (nb - 1) + 4 * g + 4)
                by_head = lambda a: a.rearrange("p c (g h d) -> p c g h d", g=G, h=G)[:, :, g, :, :]
                bias = m.a_bv[:, :].unsqueeze(1).to_broadcast([P, QC, D])
                nc.gpsimd.tensor_tensor(vaug[:, :, G * g:G * g + G, 0:D1], by_head(v32[:, :].rearrange("p (c d) -> p c d", d=D)),
                                        by_head(bias), ALU.add).then_inc(vaug_done, 1)

            def first_values():
                pool.wait_ge(misc_out, use("prep0", 0, "V") + 1)
                for g in range(G):
                    values(0, g)

            def slot(kind, b, at):
                if kind in ("middle", "last") and at in (2, 6):
                    values(b, 2 + at // 4)
                if kind in ("first", "middle") and at == 15:
                    pool.wait_ge(misc_out, use(kind, b, "V") + 1)
                    values(b + 1, 0)
                    values(b + 1, 1)
                if kind != "first" and at == 4:
                    xb = m_flat(m.x)[:, ds((b - 1) * S, S)].rearrange("p (c d) -> p c d", d=D)
                    nc.gpsimd.tensor_tensor(xres[:, :, :], xb, m.a_bo[:, :].unsqueeze(1).to_broadcast([P, QC, D]),
                                            ALU.add).then_inc(xres_done, 1)

            def polynomial(kind, b, nb):
                steps = Steps(pool, cf_pool, 3 * nb)
                by_group = lambda t: t.rearrange("p c (g h) -> p c g h", g=G)
                z, c = epz[:, :, H1:], cent[:, :, :]
                pool.wait_ge(cent_done, nb + 1)
                for (x, y_, total, slots) in ((z, z, ca, (0, 1)), (ca[:, :, :], c, cb, (3,)), (cb[:, :, :], c, cc, (5,))):
                    for n in slots:
                        nc.gpsimd.tensor_tensor(coef[:, :, :, n, :], by_group(x), by_group(y_), ALU.mult)
                    steps.step(nc.gpsimd.tensor_tensor(total[:, :, :], x, y_, ALU.mult))
                for hi, lo, t in ((0, 2, ca), (3, 4, cb), (5, 6, cc)):
                    last = nc.gpsimd.tensor_tensor(coef[:, :, :, lo, :], by_group(t[:, :, :]), coef[:, :, :, hi, :], ALU.subtract)
                last.then_inc(coef_done, 1)

            def output(kind, b, cb):
                layer_norm_gpsimd(nc, pool, m, 2 * B + cb, mv, ve, rstd)

            schedule(pool, {"setup": setup, "prepared": first_values, "slot": slot, "Q": split("Q", q32, q_h, q_l, q_split, 1),
                            "K": split("K", k32, k_h, k_l, k_split, 2), "PZ": polynomial, "OUT": output})


def moe_capacity_phase(nc, io, out, m):
    with ExitStack() as ctx:
        sb = lambda name, shape, dt: ctx.enter_context(nc.sbuf_tensor(name, shape, dt))
        sem = lambda name: ctx.enter_context(nc.semaphore("c_" + name))
        FC = F1 // P
        HALF = CAP // 2
        SLOTS = E1 * CAP
        OUT_OF_RANGE = float(1 << 20)
        wg_h, wg_l = (sb(n, [P, E1], F16) for n in ("cwg_h", "cwg_l"))
        logit, expo, held, onehot, onehot_pos = (sb(n, [P, NCH, E1], F32) for n in ("c_logit", "c_expo", "c_held", "c_onehot", "c_onehot_pos"))
        prefix = [sb(f"c_prefix{k}", [P, NCH, E1], F32) for k in range(2)]
        onehot16 = sb("c_onehot16", [P, NCH, E1], F16)
        lmax, esum, best, pos, over, away, slot = (sb(n, [P, NCH], F32) for n in ("c_lmax", "c_esum", "c_best", "c_pos", "c_over", "c_away", "c_slot"))
        to_slot, from_slot = (sb(n, [P, NCH], U32) for n in ("c_to_slot", "c_from_slot"))
        tri, ones = (sb(n, [P, P], F16) for n in ("tri_ones", "all_ones"))
        zeros = sb("c_zeros", [P, SLOTS], F32)
        xe = sb("c_xe", [HALF, 2 * E1, D], F32)
        xe_t = [sb(f"c_xe_t{k}", [P, CAP], F32) for k in range(2)]
        hid = [sb(f"c_hid{k}", [P, FC, CAP], F32) for k in range(2)]
        ye = sb("c_ye", [HALF, 2 * E1, D], F32)
        yg = sb("c_yg", [P, NCH, D], F32)
        y = sb("c_y", [P, QC, D], F32)
        res = [sb(f"c_res{k}", [P, QC, D], F32) for k in range(2)]
        st = sb("c_st", [P, QC, 6], F32)
        mv = sb("c_mv", [P, QC, 2], F32)
        ve = sb("c_ve", [P, QC], F32)
        rstd = sb("c_rstd", [P, QC], F32)
        bank = lambda name: ctx.enter_context(nc.psum_tensor(name, [P, 512], F32))
        xt_ps = [bank(f"c_xt_ps{k}") for k in range(2)]
        y_ps = [bank(f"c_y_ps{k}") for k in range(2)]
        hid_ps = [ctx.enter_context(nc.psum_tensor(f"c_hid_ps{k}", [P, 2, 512], F32)) for k in range(2)]
        slot_rows = nc.dram_tensor("slot_rows", (SLOTS, D), F32).ap()
        expert_rows = nc.dram_tensor("expert_rows", (SLOTS + 1, D), F32).ap()

        xt_mm, xt_hi, xt_lo, lg_mm, steps_done, shifted, exps_done, onehot_done, count_mm = (sem(n) for n in (
            "xt_mm", "xt_hi", "xt_lo", "lg_mm", "steps", "shifted", "exps", "onehot_done", "count_mm"))
        slots_done, tri_in, zeros_set, zeroed, scattered, xe_in, h_mm, relu_done, y_mm, y_out, stored = (sem(n) for n in (
            "slots_done", "tri_in", "zeros_set", "zeroed", "scattered", "xe_in", "h_mm", "relu_done", "y_mm", "y_out", "stored"))
        out_ready = sem("out_ready")
        gathered = [sem(f"gathered{k}") for k in range(2)]
        out_stored = [sem(f"out_stored{k}") for k in range(2)]
        block = ctx.enter_context(nc.Block())
        E_LOADS = 16

        @block.sync
        def _(sp):
            sp.dma_start(tri[:, :], io["c_tri"]).then_inc(tri_in, 16)
            sp.wait_ge(zeros_set, 1)
            sp.dma_start(slot_rows.rearrange("(p r) d -> p (r d)", p=P), zeros[:, :]).then_inc(zeroed, 16)
            sp.dma_start(expert_rows[SLOTS:SLOTS + 1, :], zeros[0:1, 0:D]).then_inc(zeroed, 16)
            sp.wait_ge(scattered, 16 * NCH)
            sp.dma_start(xe[:, :, :], slot_rows.rearrange("(t p) d -> p t d", p=HALF)).then_inc(xe_in, E_LOADS)
            for e in range(E1):
                sp.wait_ge(y_out, e + 1)
                sp.dma_start(expert_rows[e * CAP:(e + 1) * CAP, :].rearrange("(t p) d -> p t d", p=HALF),
                             ye[:, 2 * e:2 * e + 2, :]).then_inc(stored, 16)
            for t in range(B):
                sp.wait_ge(out_ready, t + 1)
                sp.dma_start(out[t].rearrange("(c p) d -> p c d", p=P), res[t % 2][:, :, :]).then_inc(out_stored[t % 2], 16)
            for k in range(2):
                sp.wait_ge(out_stored[k], 16 * (B // 2))
            sp.wait_ge(tri_in, 16)

        def router(pe, t):
            pe.wait_ge(xt_lo, t + 1)
            for c in range(QC):
                ch = t * QC + c
                o = y_ps[0][:, ch * E1:(ch + 1) * E1]
                xs = slice(ch * P, (ch + 1) * P)
                nc.tensor.matmul(o, m.xt_h[:, xs], wg_h[:, :], start=True, stop=False)
                nc.tensor.matmul(o, m.xt_h[:, xs], wg_l[:, :], start=False, stop=False)
                last = nc.tensor.matmul(o, m.xt_l[:, xs], wg_h[:, :], start=False, stop=True)
            last.then_inc(lg_mm, 1)

        @block.tensor
        def _(pe):
            for t in range(B):
                if t >= 2:
                    pe.wait_ge(xt_lo, t - 1)
                for c in range(QC):
                    last = nc.tensor.transpose(xt_ps[t % 2][:, c * P:(c + 1) * P], m.x[:, t * QC + c, :], m.ident[:, :])
                last.then_inc(xt_mm, 1)
                if t >= 1:
                    router(pe, t - 1)
            router(pe, B - 1)
            pe.wait_ge(tri_in, 16)
            pe.wait_ge(onehot_done, 1)
            o16 = onehot16[:, :, :].rearrange("p c e -> p (c e)")
            nc.tensor.matmul(y_ps[1][:, 0:NCH * E1], tri[:, :], o16, start=True, stop=True)
            nc.tensor.matmul(y_ps[1][:, NCH * E1:], ones[:, :], o16, start=True, stop=True).then_inc(count_mm, 1)
            pe.wait_ge(xe_in, E_LOADS)
            pe.wait_ge(m.e_loaded, 48)

            def rows_t(e):
                if e >= 2:
                    pe.wait_ge(xt_hi, B + e - 1)
                for j in range(2):
                    mm = nc.tensor.transpose(xt_ps[e % 2][:, j * HALF:(j + 1) * HALF], xe[:, 2 * e + j, :],
                                             m.ident[0:HALF, 0:HALF])
                mm.then_inc(xt_mm, 1)

            def hidden(e):
                pe.wait_ge(xt_hi, B + e + 1)
                if e >= 2:
                    pe.wait_ge(relu_done, e - 1)
                for f in range(FC):
                    mm = nc.tensor.matmul(hid_ps[e % 2][:, f // 2, (f % 2) * CAP:(f % 2 + 1) * CAP],
                                          m.e_w1[:, e, f * P:(f + 1) * P], xe_t[e % 2][:, :], start=True, stop=True)
                mm.then_inc(h_mm, 1)

            def output(e):
                pe.wait_ge(relu_done, e + 1)
                if e >= 2:
                    pe.wait_ge(y_out, e - 1)
                for j in range(2):
                    for f in range(FC):
                        mm = nc.tensor.matmul(y_ps[e % 2][0:HALF, j * D:(j + 1) * D],
                                              hid[e % 2][:, f, j * HALF:(j + 1) * HALF], m.e_w2[:, e, f, :],
                                              start=(f == 0), stop=(f == FC - 1))
                mm.then_inc(y_mm, 1)

            rows_t(0)
            rows_t(1)
            hidden(0)
            for e in range(E1):
                if e + 2 < E1:
                    rows_t(e + 2)
                if e + 1 < E1:
                    hidden(e + 1)
                output(e)

        @block.scalar
        def _(act):
            nc.scalar.preload_act_table(ACT.Exp)
            for t in range(B):
                act.wait_ge(xt_mm, t + 1)
                nc.scalar.activation(m.xt_h[:, t * S:(t + 1) * S], xt_ps[t % 2][:, :], ACT.Copy).then_inc(xt_hi, 1)
            act.wait_ge(shifted, 1)
            nc.scalar.activation(expo[:, :, :], logit[:, :, :], ACT.Exp).then_inc(exps_done, 1)

            def rows_t(e):
                act.wait_ge(xt_mm, B + e + 1)
                if e >= 2:
                    act.wait_ge(h_mm, e - 1)
                nc.scalar.activation(xe_t[e % 2][:, :], xt_ps[e % 2][:, 0:CAP], ACT.Copy).then_inc(xt_hi, 1)

            rows_t(0)
            rows_t(1)
            for e in range(E1):
                act.wait_ge(h_mm, e + 1)
                if e >= 2:
                    act.wait_ge(y_mm, e - 1)
                nc.scalar.activation(hid[e % 2][:, :, :].rearrange("p (b f) n -> p b (f n)", b=2), hid_ps[e % 2][:, :, 0:2 * CAP],
                                     ACT.Relu).then_inc(relu_done, 1)
                if e + 2 < E1:
                    rows_t(e + 2)

        @block.vector
        def _(dve):
            steps = Steps(dve, steps_done)
            wide = lambda a: a.unsqueeze(2).to_broadcast([P, NCH, E1])
            iota = m.iota8[:, :].unsqueeze(1).to_broadcast([P, NCH, E1])
            dve.wait_ge(m.e_loaded, 48)
            steps.done(nc.vector.memset(ones[:, :], 1.0))
            steps.step(nc.vector.tensor_copy(wg_h[:, :], m.e_wg[:, :]))
            steps.step(nc.vector.tensor_tensor(wg_l[:, :], m.e_wg[:, :], wg_h[:, :], ALU.subtract))
            for t in range(B):
                dve.wait_ge(xt_hi, t + 1)
                nc.vector.tensor_tensor(m.xt_l[:, t * S:(t + 1) * S], xt_ps[t % 2][:, :], m.xt_h[:, t * S:(t + 1) * S],
                                        ALU.subtract).then_inc(xt_lo, 1)
            dve.wait_ge(lg_mm, B)
            lg = y_ps[0][:, 0:NCH * E1].rearrange("p (c e) -> p c e", e=E1)
            steps.step(nc.vector.tensor_reduce(lmax[:, :], lg, AX.X, ALU.max))
            nc.vector.tensor_tensor(logit[:, :, :], lg, wide(lmax[:, :]), ALU.subtract).then_inc(shifted, 1)
            dve.wait_ge(exps_done, 1)
            steps.done(nc.vector.tensor_reduce(esum[:, :], expo[:, :, :], AX.X, ALU.add))
            steps.step(nc.vector.tensor_scalar(held[:, :, :], expo[:, :, :], 1.0, -float(E1), ALU.is_ge, ALU.mult))
            steps.step(nc.vector.tensor_tensor(held[:, :, :], held[:, :, :], iota, ALU.add))
            steps.step(nc.vector.tensor_reduce(best[:, :], held[:, :, :], AX.X, ALU.min))
            steps.step(nc.vector.tensor_tensor(onehot[:, :, :], held[:, :, :], wide(best[:, :]), ALU.is_equal))
            nc.vector.tensor_copy(onehot16[:, :, :], onehot[:, :, :]).then_inc(onehot_done, 1)
            steps.done(nc.vector.reciprocal(esum[:, :], esum[:, :]))
            steps.done(nc.vector.tensor_scalar(best[:, :], best[:, :], float(E1), None, ALU.add))
            dve.wait_ge(count_mm, 1)
            totals = y_ps[1][:, NCH * E1:].rearrange("p (c e) -> p c e", e=E1)
            steps.done(nc.vector.memset(prefix[0][:, 0:1, :], 0.0))
            steps.step(nc.vector.tensor_copy(prefix[0][:, 1:, :], totals[:, 0:NCH - 1, :]))
            k, d = 0, 1
            while d < NCH:
                a, b = prefix[k], prefix[1 - k]
                steps.done(nc.vector.tensor_copy(b[:, 0:d, :], a[:, 0:d, :]))
                steps.step(nc.vector.tensor_tensor(b[:, d:, :], a[:, d:, :], a[:, 0:NCH - d, :], ALU.add))
                k, d = 1 - k, 2 * d
            counts = y_ps[1][:, 0:NCH * E1].rearrange("p (c e) -> p c e", e=E1)
            steps.step(nc.vector.tensor_tensor(held[:, :, :], counts, prefix[k][:, :, :], ALU.add))
            steps.step(nc.vector.tensor_tensor(onehot_pos[:, :, :], held[:, :, :], onehot[:, :, :], ALU.mult))
            steps.step(nc.vector.tensor_reduce(pos[:, :], onehot_pos[:, :, :], AX.X, ALU.add))
            steps.done(nc.vector.scalar_tensor_tensor(slot[:, :], best[:, :], float(CAP), pos[:, :], ALU.mult, ALU.add))
            steps.done(nc.vector.tensor_scalar(over[:, :], pos[:, :], float(CAP), None, ALU.is_gt))
            steps.step(nc.vector.tensor_scalar(away[:, :], best[:, :], float(NT), OUT_OF_RANGE, ALU.mult, ALU.add))
            steps.step(nc.vector.tensor_tensor(over[:, :], over[:, :], away[:, :], ALU.mult))
            steps.step(nc.vector.scalar_tensor_tensor(slot[:, :], slot[:, :], -1.0, over[:, :], ALU.add, ALU.add))
            nc.vector.tensor_copy(to_slot[:, :], slot[:, :]).then_inc(slots_done, 1)
            nc.vector.tensor_scalar(from_slot[:, :], slot[:, :], float(SLOTS), None, ALU.min).then_inc(slots_done, 1)
            for e in range(E1):
                dve.wait_ge(y_mm, e + 1)
                nc.vector.tensor_copy(ye[:, 2 * e:2 * e + 2, :], y_ps[e % 2][0:HALF, 0:2 * D].rearrange("p (j d) -> p j d", d=D)).then_inc(y_out, 1)
            for t in range(B):
                k = t % 2
                dve.wait_ge(gathered[k], 16 * QC * (t // 2 + 1))
                if t >= 1:
                    dve.wait_ge(out_ready, t)
                for c in range(QC):
                    ch = t * QC + c
                    steps.done(nc.vector.scalar_tensor_tensor(y[:, c, :], yg[:, ch, :], esum[:, ch:ch + 1], m.x[:, ch, :], ALU.mult, ALU.add))
                steps.wait()
                if t >= 2:
                    dve.wait_ge(out_stored[k], 16 * (t // 2))
                layer_norm_stats(nc, dve, m, 3 * B + t, y, st, mv)
                layer_norm_apply(nc, dve, m, 3 * B + t, y, mv, rstd, res[k]).then_inc(out_ready, 1)

        @block.gpsimd
        def _(pool):
            nc.gpsimd.memset(zeros[:, :], 0.0).then_inc(zeros_set, 1)
            pool.wait_ge(zeroed, 32)
            pool.wait_ge(slots_done, 2)
            for ch in range(NCH):
                nc.gpsimd.indirect_dma_start(out=slot_rows[:, :], out_offset=bass.IndirectOffsetOnAxis(ap=to_slot[:, ch:ch + 1], axis=0),
                                             in_=m.x[:, ch, :], in_offset=None, bounds_check=SLOTS - 1,
                                             oob_is_err=False).then_inc(scattered, 16)
            pool.wait_ge(stored, 16 * E1)

            def gather(t):
                for ch in range(t * QC, (t + 1) * QC):
                    nc.gpsimd.indirect_dma_start(out=yg[:, ch, :], out_offset=None, in_=expert_rows[:, :],
                                                 in_offset=bass.IndirectOffsetOnAxis(ap=from_slot[:, ch:ch + 1], axis=0),
                                                 bounds_check=SLOTS, oob_is_err=False).then_inc(gathered[t % 2], 16)

            gather(0)
            gather(1)
            for t in range(B):
                layer_norm_gpsimd(nc, pool, m, 3 * B + t, mv, ve, rstd)
                if t + 2 < B:
                    gather(t + 2)


def m_flat(t):
    a = t[tuple(slice(None) for _ in t.shape)]
    names = "abcd"[:len(t.shape) - 1]
    return a if len(names) == 1 else a.rearrange(f"p {' '.join(names)} -> p ({' '.join(names)})")


class Memory:
    pass


def build(nc, io, out):
    ctx = ExitStack()
    with ctx:
        sb = lambda name, shape, dt: ctx.enter_context(nc.sbuf_tensor(name, shape, dt))
        m = Memory()
        m.x = sb("x_tok", [P, NCH, D], F32)
        m.ident = sb("ident", [P, P], F32)
        m.mhalf = sb("mhalf", [P, QC], F32)
        m.eps = sb("ln_eps", [P, QC], F32)
        m.gate_v = sb("gate_v", [P, 1], F32)
        m.gate_v2 = sb("gate_v2", [P, 1], F32)
        m.gate = sb("gate", [P, QC], F32)
        m.x_loaded = [ctx.enter_context(nc.semaphore(f"x_loaded{b}")) for b in range(B)]
        m.var_ready, m.rstd_ready, m.ln_pool = (ctx.enter_context(nc.semaphore(n)) for n in ("var_ready", "rstd_ready", "ln_pool"))
        m.stats_ready = ctx.enter_context(nc.semaphore("stats_ready"))
        m.xt_h = sb("xt_h", [P, NT + S], F16)
        m.xt_l = sb("xt_l", [P, NT + S], F16)
        m.w1_raw = sb("w1_raw", [P, E0, F0], F32)
        m.w2_raw = sb("w2_raw", [P, E0, F0 // P, D], F32)
        m.wg_raw = sb("wg_raw", [P, E0], F32)
        m.bg_bc = sb("bg_bc", [P, E0], F32)
        m.b1_rows = sb("b1_rows", [E0 * F0 // P, P], F32)
        m.b2_rows = sb("b2_rows", [E0, D], F32)
        m.iota8 = sb("iota8", [P, E0], F32)
        m.f0_loaded = ctx.enter_context(nc.semaphore("f0_loaded"))
        m.F0_LOADS = 7 * 16
        m.a_w = sb("a_w_raw", [P, 5, D], F32)
        m.a_wfg = sb("a_wfg", [P, D], F32)
        m.a_cols = sb("a_cols", [P, 6], F32)
        m.a_bv = sb("a_bv", [P, D], F32)
        m.a_bo = sb("a_bo", [P, D], F32)
        m.e_w1 = sb("e_w1", [P, E1, F1], F32)
        m.e_w2 = sb("e_w2", [P, E1, F1 // P, D], F32)
        m.e_wg = sb("e_wg", [P, E1], F32)
        m.e_loaded = ctx.enter_context(nc.semaphore("e_loaded"))
        m.a_loaded = ctx.enter_context(nc.semaphore("a_loaded"))
        with ExitStack() as c0:
            sb0 = lambda name, shape, dt: c0.enter_context(nc.sbuf_tensor(name, shape, dt))
            m.w_h = sb0("w_h", [P, PAIRS, 512], F16)
            m.w_l = sb0("w_l", [P, PAIRS, 512], F16)
            m.wo_h = sb0("wo_h", [P, PAIRS, D], F16)
            m.wo_l = sb0("wo_l", [P, PAIRS, D], F16)
            m.k_h = [sb0(f"k_h{h}", [P, S], F16) for h in range(2)]
            m.k_l = [sb0(f"k_l{h}", [P, S], F16) for h in range(2)]
            m.q_mult = sb0("q_mult", [P, 2, S], F32)
            m.q_bias = sb0("q_bias", [P, 2, PAIRS], F32)
            m.bo_bc = sb0("bo_bc", [P, D], F32)
            m.causal = sb0("causal", [P, P], BF16)
            m.ident_bf = sb0("ident_bf", [P, P], BF16)
            m.zeros = sb0("zeros", [P, S], F16)
            setup_phase(nc, io, m)
            rel_attention_phase(nc, io, m)
        moe_top2_phase(nc, io, m)
        gauss_attention_phase(nc, io, m)
        moe_capacity_phase(nc, io, out, m)


_INPUTS = [
    "L0_attn_input", "L0_attn_qkv", "L0_attn_q_bias", "L0_attn_positional", "L0_attn_out_kernel", "L0_attn_out_bias",
    "L0_ffn_Wg", "L0_ffn_bg", "L0_ffn_W1", "L0_ffn_b1", "L0_ffn_W2", "L0_ffn_b2",
    "L1_attn_wq", "L1_attn_bq", "L1_attn_wk", "L1_attn_bk", "L1_attn_wv", "L1_attn_bv", "L1_attn_wo", "L1_attn_bo",
    "L1_attn_wfq", "L1_attn_bfq", "L1_attn_wfg", "L1_attn_bfg", "L1_attn_up", "L1_attn_uz",
    "L1_ffn_gate_w", "L1_ffn_w1", "L1_ffn_w2",
]


def kernel(**inputs):
    import concourse.bacc as bacc
    from concourse.bass_utils import run_bass_kernel_spmd

    nc = bacc.Bacc("TRN2", target_bir_lowering=False, num_devices=1)
    arrays, io = {}, {}
    for name in _INPUTS:
        arrays[f"in_{name}_dram"] = np.ascontiguousarray(inputs[name])
    for name, table in shape_constants().items():
        arrays[f"in_{name}_dram"] = table
    for dram, a in arrays.items():
        io[dram[3:-5]] = nc.dram_tensor(dram, a.shape, mybir.dt.from_np(a.dtype), kind="ExternalInput").ap()
    out = nc.dram_tensor("out_0_dram", (B, S, D), F32, kind="ExternalOutput").ap()
    build(nc, io, out)
    r = run_bass_kernel_spmd(nc, [arrays], core_ids=[0])
    return r.results[0]["out_0_dram"]
```

```python
from contextlib import ExitStack

import numpy as np

import concourse.bass as bass
from concourse import mybir

F32 = mybir.dt.float32
F16 = mybir.dt.float16
BF16 = mybir.dt.bfloat16
U32 = mybir.dt.uint32
ALU = mybir.AluOpType
ACT = mybir.ActivationFunctionType
AX = mybir.AxisListType
ds = bass.ds

P = 128
B, S, D = 8, 512, 128
NT = B * S
NCH = NT // P
QC = S // P
LN_EPS = 1e-5

H0, HD, FREQS, MAX_PERIOD = 16, 64, 32, 1250
PAIRS = H0 // 2
W_SCALE = (3.0 * D * HD * H0) ** -0.25
O_SCALE = (H0 * HD * D) ** -0.25
QK_SCALE = HD ** -0.25
P_SCALE = 64.0

E0, F0 = 8, 2 * D

H1 = 16
D1 = D // H1

E1, F1, CAP = 8, 512, 160


def shape_constants():
    pos = np.arange(S, dtype=np.float64)
    idx = np.arange(FREQS)
    ang = pos[None, :] * (MAX_PERIOD ** (-(idx // 2 * 2) / FREQS))[:, None]
    sin, cos = np.sin(ang), np.cos(ang)
    odd = (idx % 2 == 1)[:, None]
    alpha, beta = np.where(odd, cos, sin), np.where(odd, sin, -cos)
    t_scale = W_SCALE * np.sqrt(2.0) * FREQS ** -0.5 * HD ** -0.5
    rel = np.concatenate([alpha, beta]) * t_scale
    plain = np.full((HD, S), W_SCALE * QK_SCALE)
    q_mult = np.stack([np.concatenate([plain, rel]), np.concatenate([rel, plain])], 1)
    k_tab = np.tile(np.concatenate([cos, sin]), (2, 1))
    qi, ki = np.arange(P)[:, None], np.arange(P)[None, :]
    causal = np.where(ki <= qi, 0.0, -1e30)
    j = (np.arange(S) - (S - 1) / 2) / 16
    j2_h = (j * j).astype(np.float16)
    j2_l = (j * j - j2_h).astype(np.float16)
    one = np.ones(S)
    key_rows = np.stack([-j2_h / 8, -j2_l / 8, -j2_h / 8, j / 2, j / 2, -one / 2, -one / 2, one])
    return {
        "c_tri": np.triu(np.ones((P, P))).astype(np.float16),
        "c_key_rows": key_rows.astype(np.float16),
        "c_q_mult": q_mult.astype(np.float32),
        "c_k_tab": k_tab.astype(np.float32),
        "c_causal": causal.astype(np.float32),
        "c_ident": np.eye(P, dtype=np.float32),
        "c_iota8": np.tile(np.arange(8, dtype=np.float32), (P, 1)),
    }


class Steps:

    def __init__(self, eng, sem, base=0):
        self.eng, self.sem, self.base, self.k = eng, sem, base, 0

    def done(self, ins):
        ins.then_inc(self.sem, 1)
        self.k += 1

    def wait(self):
        self.eng.wait_ge(self.sem, self.base + self.k)

    def step(self, ins):
        self.done(ins)
        self.wait()


def vector_gate(nc, m):
    return nc.vector.memset(m.gate_v[:, :], 0.0)


def layer_norm_stats(nc, dve, m, n, y, st, mv):
    for c in range(QC):
        last = nc.vector.bn_stats(st[:, c, :], y[:, c, :])
    last.then_inc(m.stats_ready, 1)
    dve.wait_ge(m.stats_ready, n + 1)
    vector_gate(nc, m)
    for c in range(QC):
        last = nc.vector.bn_aggr(mv[:, c, :], st[:, c, :])
    last.then_inc(m.var_ready, 1)


def layer_norm_apply(nc, dve, m, n, y, mv, rstd, out):
    dve.wait_ge(m.rstd_ready, n + 1)
    for c in range(QC):
        last = nc.vector.tensor_scalar(out[:, c, :], y[:, c, :], mv[:, c, 0:1], rstd[:, c:c + 1],
                                       ALU.subtract, ALU.mult)
    return last


def pool_gate(nc, m, rows):
    nc.gpsimd.tensor_tensor(m.gate[rows, 0:1], m.mhalf[rows, 0:1], m.mhalf[rows, 1:2], ALU.add)


def layer_norm_gpsimd(nc, pool, m, n, mv, ve, rstd):
    steps = Steps(pool, m.ln_pool, n)
    pool.wait_ge(m.var_ready, n + 1)
    steps.step(nc.gpsimd.tensor_tensor(ve[:, :], mv[:, :, 1], m.eps[:, :], ALU.add))
    nc.gpsimd.tensor_tensor(rstd[:, :], ve[:, :], m.mhalf[:, :], ALU.pow).then_inc(m.rstd_ready, 1)


def setup_phase(nc, io, m):
    with ExitStack() as ctx:
        sb = lambda name, shape, dt: ctx.enter_context(nc.sbuf_tensor(name, shape, dt))
        sem = lambda name: ctx.enter_context(nc.semaphore(name))
        w_raw = sb("w_raw", [P, 3, H0, HD], F32)
        wo_raw = sb("wo_raw", [P, PAIRS, D], F32)
        posit = sb("posit", [FREQS, H0 * HD], F32)
        qb_rows = sb("qb_rows", [PAIRS, P], F32)
        qb_cols = sb("qb_cols", [P, PAIRS], F32)
        wq_t = sb("wq_t", [P, PAIRS, P], F32)
        pos_t = sb("pos_t", [P, PAIRS, P], F32)
        tab32 = sb("tab32", [P, S], F32)
        mask32 = sb("mask32", [P, P], F32)
        tp = [ctx.enter_context(nc.psum_tensor(f"tp{i}", [P, 512], F32)) for i in range(2)]
        wps = ctx.enter_context(nc.psum_tensor("wps", [P, 2, 512], F32))
        pps = ctx.enter_context(nc.psum_tensor("pps", [P, 512], F32))
        bps = ctx.enter_context(nc.psum_tensor("bps", [P, 512], F32))

        ident_in, w_in, misc_in = sem("ident_in"), sem("w_in"), sem("misc_in")
        xt_mm, xt_hi, xt_lo = sem("xt_mm"), sem("xt_hi"), sem("xt_lo")
        wt_mm, wt_out, g_mm, g_hi, dve_steps = sem("wt_mm"), sem("wt_out"), sem("g_mm"), sem("g_hi"), sem("su_steps")
        act_done, kv_split = sem("act_done"), sem("kv_split")
        block = ctx.enter_context(nc.Block())

        @block.sync
        def _(sp):
            sp.dma_start(m.ident[:, :], io["c_ident"]).then_inc(ident_in, 16)
            for b in range(0, B, 2):
                sp.dma_start(m.x[:, b * QC:(b + 2) * QC, :],
                             io["L0_attn_input"][b:b + 2].rearrange("b (c p) d -> p (b c) d", p=P)).then_inc(m.x_loaded[b // 2], 16)

        @block.scalar
        def _(act):
            act.dma_start(w_raw[:, :, :, :], io["L0_attn_qkv"]).then_inc(w_in, 16)
            act.dma_start(posit[:, :], io["L0_attn_positional"].rearrange("f n h -> f (n h)")).then_inc(misc_in, 16)
            act.dma_start(qb_rows[:, :], io["L0_attn_q_bias"].rearrange("(a n) h -> a (n h)", n=2)).then_inc(misc_in, 16)
            act.dma_start(wo_raw[:, :, :], io["L0_attn_out_kernel"].rearrange("(a p) d -> p a d", p=P)).then_inc(misc_in, 16)
            act.dma_start(tab32[:, :], io["c_k_tab"]).then_inc(misc_in, 16)
            act.dma_start(m.q_mult[:, :, :], io["c_q_mult"]).then_inc(misc_in, 16)
            act.dma_start(mask32[:, :], io["c_causal"]).then_inc(misc_in, 16)
            act.dma_start(m.bo_bc[:, :], io["L0_attn_out_bias"].rearrange("(a d) -> a d", a=1).broadcast_to([P, D])).then_inc(misc_in, 16)
            for b in range(B):
                act.wait_ge(xt_mm, b + 1)
                nc.scalar.activation(m.xt_h[:, b * S:(b + 1) * S], tp[b % 2][:, :], ACT.Copy).then_inc(xt_hi, 1)
            act.wait_ge(wt_mm, 1)
            nc.scalar.activation(wq_t[:, :, :].rearrange("p a b -> p (a b)").rearrange("p (a b) -> p a b", a=2), wps[:, :, :], ACT.Copy).then_inc(act_done, 1)
            act.wait_ge(g_mm, 2)
            nc.scalar.activation(m.w_h[:, :, 64:192], wps[:, :, :].rearrange("p a (b n) -> p (a b) n", n=P),
                                 ACT.Copy).then_inc(g_hi, 1)

        @block.tensor
        def _(pe):
            pe.wait_ge(ident_in, 16)
            for b in range(B):
                pe.wait_ge(m.x_loaded[b // 2], 16)
                if b >= 2:
                    pe.wait_ge(xt_lo, b - 1)
                for c in range(QC):
                    last = nc.tensor.transpose(tp[b % 2][:, c * P:(c + 1) * P], m.x[:, b * QC + c, :], m.ident[:, :])
                last.then_inc(xt_mm, 1)
            pe.wait_ge(w_in, 16)
            for a in range(PAIRS):
                last = nc.tensor.transpose(wps[:, a // 4, (a % 4) * P:(a % 4 + 1) * P],
                                           w_raw[:, 0, 2 * a:2 * a + 2, :].rearrange("p n h -> p (n h)"), m.ident[:, :])
            last.then_inc(wt_mm, 1)
            pe.wait_ge(misc_in, 112)
            for a in range(PAIRS):
                last = nc.tensor.transpose(pps[:, a * FREQS:(a + 1) * FREQS], posit[:, a * P:(a + 1) * P],
                                           m.ident[0:FREQS, 0:FREQS])
            last = nc.tensor.transpose(pps[:, 256:256 + PAIRS], qb_rows[:, :], m.ident[0:PAIRS, 0:PAIRS])
            last.then_inc(wt_mm, 1)
            pe.wait_ge(act_done, 1)
            pe.wait_ge(wt_out, 1)
            for a in range(PAIRS):
                nc.tensor.matmul(bps[0:64, a:a + 1], pos_t[:, a, 64:128], qb_cols[:, a:a + 1], start=True, stop=True)
                last = nc.tensor.matmul(bps[64:128, a:a + 1], pos_t[:, a, 0:64], qb_cols[:, a:a + 1], start=True, stop=True)
            last.then_inc(g_mm, 1)
            for a in range(PAIRS):
                last = nc.tensor.matmul(wps[:, a // 4, (a % 4) * P:(a % 4 + 1) * P], wq_t[:, a, :], pos_t[:, a, :],
                                        start=True, stop=True)
            last.then_inc(g_mm, 1)

        @block.vector
        def _(dve):
            steps = Steps(dve, dve_steps)
            steps.done(nc.vector.memset(pos_t[:, :, :], 0.0))
            steps.done(nc.vector.memset(m.zeros[:, :], 0.0))
            steps.done(nc.vector.memset(m.xt_h[:, NT:NT + S], 0.0))
            steps.done(nc.vector.memset(m.xt_l[:, NT:NT + S], 0.0))
            for b in range(B):
                dve.wait_ge(xt_hi, b + 1)
                nc.vector.tensor_tensor(m.xt_l[:, b * S:(b + 1) * S], tp[b % 2][:, :], m.xt_h[:, b * S:(b + 1) * S],
                                        ALU.subtract).then_inc(xt_lo, 1)
            dve.wait_ge(misc_in, 112)
            dve.wait_ge(wt_mm, 2)
            steps.wait()
            for h in range(2):
                r = slice(64 * h, 64 * h + 64)
                for k in range(2):
                    steps.done(nc.vector.tensor_copy(pos_t[r, :, 64 * h + 32 * k:64 * h + 32 * k + 32],
                                                     pps[r, 0:256].rearrange("p (a f) -> p a f", f=FREQS)))
            nc.vector.tensor_copy(qb_cols[:, :], pps[:, 256:256 + PAIRS]).then_inc(wt_out, 1)
            dve.wait_ge(w_in, 16)
            parts = [(0, 64, w_raw[:, 0, 0::2, :]), (192, 256, w_raw[:, 0, 1::2, :])]
            for lo, hi, src in parts:
                steps.done(nc.vector.tensor_copy(m.w_h[:, :, lo:hi], src))
            steps.wait()
            for lo, hi, src in parts:
                steps.done(nc.vector.tensor_tensor(m.w_l[:, :, lo:hi], src, m.w_h[:, :, lo:hi], ALU.subtract))
            steps.done(nc.vector.tensor_copy(m.wo_h[:, :, :], wo_raw[:, :, :]))
            for h in range(2):
                steps.done(nc.vector.tensor_copy(m.k_h[h][:, :], tab32[:, :]))
            steps.done(nc.vector.tensor_copy(m.causal[:, :], mask32[:, :]))
            steps.done(nc.vector.tensor_copy(m.ident_bf[:, :], m.ident[:, :]))
            steps.wait()
            nc.vector.tensor_tensor(m.wo_l[:, :, :], wo_raw[:, :, :], m.wo_h[:, :, :], ALU.subtract)
            for h in range(2):
                nc.vector.tensor_tensor(m.k_l[h][:, :], tab32[:, :], m.k_h[h][:, :], ALU.subtract)
            dve.wait_ge(g_mm, 1)
            dve.wait_ge(wt_out, 1)
            inv = 1.0 / W_SCALE
            nc.vector.tensor_scalar(m.q_bias[0:64, 0, :], qb_cols[0:64, :], inv, None, ALU.mult)
            nc.vector.tensor_scalar(m.q_bias[64:128, 0, :], bps[64:128, 0:PAIRS], inv, None, ALU.mult)
            nc.vector.tensor_scalar(m.q_bias[0:64, 1, :], bps[0:64, 0:PAIRS], inv, None, ALU.mult)
            nc.vector.tensor_scalar(m.q_bias[64:128, 1, :], qb_cols[64:128, :], inv, None, ALU.mult)
            dve.wait_ge(g_hi, 1)
            nc.vector.tensor_tensor(m.w_l[:, :, 64:192], wps[:, :, :].rearrange("p a (b n) -> p (a b) n", n=P),
                                    m.w_h[:, :, 64:192], ALU.subtract)

        @block.gpsimd
        def _(pool):
            nc.gpsimd.memset(m.mhalf[:, :], -0.5)
            nc.gpsimd.memset(m.eps[:, :], LN_EPS)
            nc.gpsimd.memset(m.b2_blocks[:, :], 0.0)
            pool.wait_ge(w_in, 16)
            kv = [(m.w_h[:, :, lo:lo + P], m.w_l[:, :, lo:lo + P], w_raw[:, k, :, :].rearrange("p (a n) h -> p a (n h)", n=2))
                  for k, lo in ((1, 256), (2, 384))]
            for hi, lo, src in kv:
                nc.gpsimd.affine_select(out=hi, in_=src, compare_op=ALU.is_ge, fill=0.0, base=0,
                                        pattern=[[0, PAIRS], [1, P]], channel_multiplier=0).then_inc(kv_split, 1)
            pool.wait_ge(kv_split, 2)
            for hi, lo, src in kv:
                nc.gpsimd.tensor_tensor(lo, src, hi, ALU.subtract)


def rel_attention_phase(nc, io, m):
    with ExitStack() as ctx:
        sb = lambda name, shape, dt: ctx.enter_context(nc.sbuf_tensor(name, shape, dt))
        sem = lambda name: ctx.enter_context(nc.semaphore(name))
        ps = lambda name: ctx.enter_context(nc.psum_tensor(name, [P, 512], F32))
        q32 = [sb(f"q32_{h}", [P, S], F32) for h in range(2)]
        q_h = [sb(f"q_h{h}", [P, S], F16) for h in range(2)]
        q_l = [sb(f"q_l{h}", [P, S], F16) for h in range(2)]
        k32 = sb("k32", [P, S], F32)
        v_h = sb("v_h", [P, QC, P], F16)
        v_l = sb("v_l", [P, QC, P], F16)
        PW = P * QC * (QC + 1) // 2
        prob = [sb(f"prob{h}", [P, PW], F32) for h in range(2)]
        pt_h = [sb(f"pt_h{h}", [P, PW], F16) for h in range(2)]
        pt_l = [sb(f"pt_l{h}", [P, PW], F16) for h in range(2)]
        o_h = sb("o_h", [P, S], F16)
        o_l = sb("o_l", [P, S], F16)
        nmax = [sb(f"nmax{h}", [P, QC], F32) for h in range(2)]
        sums = [sb(f"sums{h}", [P, QC], F32) for h in range(2)]
        rsum = [sb(f"rsum{h}", [P, QC], F32) for h in range(2)]
        y = sb("ln_y", [P, QC, D], F32)
        st = sb("ln_st", [P, QC, 6], F32)
        mv = sb("ln_mv", [P, QC, 2], F32)
        ve = sb("ln_ve", [P, QC], F32)
        rstd = sb("ln_rstd", [P, QC], F32)
        score_ps = [ps(f"score_ps{u}") for u in range(3)]
        pt_ps = [ps(f"pt_ps{u}") for u in range(2)]
        proj_ps, pv_ps, out_ps = ps("proj_ps"), ps("pv_ps"), ps("out_ps")

        pair = lambda name: [sem(f"{name}{h}") for h in range(2)]
        count = lambda n, u: 3 * n + u + 1
        q_mm, q_out, q_split = pair("q_mm"), pair("q_out"), pair("q_split")
        k_mm, k_out, k_split = sem("k_mm"), sem("k_out"), pair("k_split")
        v_mm, v_hi, v_lo = sem("v_mm"), sem("v_hi"), sem("v_lo")
        s_mm, max_done, exp_done = pair("s_mm"), pair("max_done"), pair("exp_done")
        p_ready = pair("p_ready")
        t_mm, pt_hi, pt_lo = pair("t_mm"), pair("pt_hi"), pair("pt_lo")
        pv_mm, o_hi, o_lo, out_mm, y_done = sem("pv_mm"), sem("o_hi"), sem("o_lo"), sem("out_mm"), sem("y_done")
        dve_steps, pool_steps = sem("ra_dve"), sem("ra_pool")
        ln_dve, bias_in, r_ready = sem("ra_lnd"), sem("bias_in"), sem("r_ready")

        UNIT_CHUNKS = [[(3, 0)], [(2, 0), (0, 384)], [(1, 0)]]
        P_OFF = [P * c * (c + 1) // 2 for c in range(QC)]
        T_UNITS = [[(0, 0)], [(1, 0), (3, 384)], [(2, 0)]]
        T_OFF, T_WIDTH = [0, 512, 1024], [512, 512, 256]
        J_OFF = {0: 0, 1: 512, 3: 896, 2: 1024}

        CLOSE = "close"

        def schedule(eng, first_front, body, close, last):
            first_front()
            body(0, 0, 0, False, False, None)
            body(1, 0, 1, False, True, None)
            with eng.Fori(2, PAIRS - 1) as p:
                body(p, 0, p, False, True, p - 2)
            body(PAIRS - 1, 0, PAIRS - 1, True, True, PAIRS - 3)
            with eng.Fori(1, B) as b:
                body(PAIRS * b, b, 0, False, True, PAIRS - 2)
                body(PAIRS * b + 1, b, 1, False, True, CLOSE)
                with eng.Fori(2, PAIRS - 1) as p:
                    body(PAIRS * b + p, b, p, False, True, p - 2)
                body(PAIRS * b + PAIRS - 1, b, PAIRS - 1, True, True, PAIRS - 3)
            last()

        block = ctx.enter_context(nc.Block())

        @block.sync
        def _(sp):
            load = lambda dst, src: sp.dma_start(dst, src).then_inc(m.f0_loaded, 16)
            load(m.w1_raw[:, :, :], io["L0_ffn_W1"].rearrange("e d f -> d e f"))
            load(m.w2_raw[:, :, :, :], io["L0_ffn_W2"].rearrange("e (c p) d -> p e c d", p=P))
            load(m.wg_raw[:, :], io["L0_ffn_Wg"])
            load(m.bg_bc[:, :], io["L0_ffn_bg"].rearrange("(a e) -> a e", a=1).broadcast_to([P, E0]))
            load(m.b1_rows[:, :], io["L0_ffn_b1"].rearrange("e (c p) -> (e c) p", p=P))
            for c in range(QC):
                load(m.b2_blocks[c * E0:(c + 1) * E0, c * D:(c + 1) * D], io["L0_ffn_b2"])
            load(m.iota8[:, :], io["c_iota8"])
            loads = 0

            def load(dst, src, scattered=False):
                nonlocal loads
                sp.dma_start(dst, src, allow_slow_non_contiguous=scattered).then_inc(m.a_loaded, 16)
                loads += 16

            for k, name in ((0, "wq"), (1, "wk"), (2, "wv"), (4, "wo")):
                load(m.a_w[:, k, :], io[f"L1_attn_{name}"])
            for dst, name in ((m.a_w[:, 3, :], "wfq"), (m.a_wfg[:, :], "wfg")):
                for g in range(4):
                    load(dst[32 * g:32 * g + 32, :], io[f"L1_attn_{name}"].rearrange("(g h d) n -> g d h n", h=4, d=D1)[g])
            for k, name in enumerate(("bq", "bk")):
                for g in range(4):
                    load(m.a_cols[32 * g:32 * g + 32, k:k + 1],
                         io[f"L1_attn_{name}"].rearrange("(g h d a) -> g d h a", h=4, d=D1, a=1)[g], scattered=True)
            for k, name in enumerate(("bfq", "bfg")):
                load(m.a_cols[:, 2 + k:3 + k], io[f"L1_attn_{name}"].rearrange("(p a) -> p a", a=1))
            for k, name in enumerate(("up", "uz")):
                load(m.a_cols[:, 4 + k:5 + k], io[f"L1_attn_{name}"].rearrange("h a d -> (h d) a"))
            for dst, name in ((m.a_bv, "bv"), (m.a_bo, "bo")):
                load(dst[:, :], io[f"L1_attn_{name}"].rearrange("(a d) -> a d", a=1).broadcast_to([P, D]))
            sp.wait_ge(m.f0_loaded, m.F0_LOADS)
            sp.wait_ge(m.a_loaded, loads)
            m.A_LOADS = loads

        @block.tensor
        def _(pe):
            def project_q(h, mth, bx, pw):
                w_hi, w_lo = (t[:, pw, 128 * h:128 * h + 128] if isinstance(pw, int)
                              else m_flat(t)[:, ds(pw * 512 + 128 * h, 128)] for t in (m.w_h, m.w_l))
                x_hi, x_lo = (t[:, ds(bx * S, S)] for t in (m.xt_h, m.xt_l))
                nc.tensor.matmul(proj_ps[:, :], w_hi, x_hi, start=True, stop=False)
                nc.tensor.matmul(proj_ps[:, :], w_lo, x_hi, start=False, stop=False)
                nc.tensor.matmul(proj_ps[:, :], w_hi, x_lo, start=False, stop=True).then_inc(q_mm[h], 1)

            def project_k(bx, pw):
                w_hi, w_lo = (m_flat(t)[:, ds(pw * 512 + 256, 128)] for t in (m.w_h, m.w_l))
                x_hi, x_lo = (t[:, ds(bx * S, S)] for t in (m.xt_h, m.xt_l))
                nc.tensor.matmul(proj_ps[:, :], w_hi, x_hi, start=True, stop=False)
                nc.tensor.matmul(proj_ps[:, :], w_lo, x_hi, start=False, stop=False)
                nc.tensor.matmul(proj_ps[:, :], w_hi, x_lo, start=False, stop=True).then_inc(k_mm, 1)

            def project_v(bx, pw):
                w_hi, w_lo = (m_flat(t)[:, ds(pw * 512 + 384, 128)] for t in (m.w_h, m.w_l))
                for c in range(QC):
                    x_hi, x_lo = (t[:, ds(bx * S + c * P, P)] for t in (m.xt_h, m.xt_l))
                    o = proj_ps[:, c * P:(c + 1) * P]
                    nc.tensor.matmul(o, x_hi, w_hi, start=True, stop=False)
                    nc.tensor.matmul(o, x_hi, w_lo, start=False, stop=False)
                    mm = nc.tensor.matmul(o, x_lo, w_hi, start=False, stop=True)
                mm.then_inc(v_mm, 1)

            def scores(h, n):
                pe.wait_ge(q_split[h], n + 1)
                pe.wait_ge(k_split[h], n + 1)
                for u in range(3):
                    if h == 1 or not (isinstance(n, int) and n == 0):
                        pe.wait_ge(exp_done[1 - h], count(n + h - 1, u))
                    for c, col in UNIT_CHUNKS[u]:
                        w = P * (c + 1)
                        o, qs = score_ps[u][:, col:col + w], slice(c * P, (c + 1) * P)
                        nc.tensor.matmul(o, q_h[h][:, qs], m.k_h[h][:, 0:w], start=True, stop=False)
                        nc.tensor.matmul(o, q_h[h][:, qs], m.k_l[h][:, 0:w], start=False, stop=False)
                        nc.tensor.matmul(o, q_l[h][:, qs], m.k_h[h][:, 0:w], start=False, stop=False)
                        mm = nc.tensor.matmul(o[:, w - P:w], m.ident_bf[:, :], m.causal[:, :], start=False, stop=True)
                    mm.then_inc(s_mm[h], 1)

            def transposes(h, n, u_list):
                for u in u_list:
                    if u == 0:
                        pe.wait_ge(p_ready[h], n + 1)
                    at = 3 * h + u
                    ph, pu = divmod(at - 2 if at >= 2 else at + 4, 3)
                    if at >= 2 or not (isinstance(n, int) and n == 0):
                        pe.wait_ge(pt_lo[ph], count(n if at >= 2 else n - 1, pu))
                    for j, col in T_UNITS[u]:
                        for c in range(j, QC):
                            mm = nc.tensor.transpose(pt_ps[at % 2][:, col + (c - j) * P:col + (c - j + 1) * P],
                                                     prob[h][:, P_OFF[c] + j * P:P_OFF[c] + (j + 1) * P], m.ident[:, :])
                    mm.then_inc(t_mm[h], 1)

            def weighted_values(n):
                for h in range(2):
                    pe.wait_ge(pt_lo[h], count(n, 2))
                pe.wait_ge(v_lo, n + 1)
                pe.wait_ge(o_lo, n)
                for j in range(QC):
                    for term in range(3):
                        pt, v = [(pt_h, v_h), (pt_h, v_l), (pt_l, v_h)][term]
                        for h in range(2):
                            mm = nc.tensor.matmul(pv_ps[64 * h:64 * h + 64, j * P:S], v[:, j, 64 * h:64 * h + 64],
                                                  pt[h][:, J_OFF[j]:J_OFF[j] + S - j * P],
                                                  start=(j == 0 and term == 0), stop=(j == QC - 1 and term == 2))
                mm.then_inc(pv_mm, 1)

            def open_output(b):
                pe.wait_ge(y_done, b)
                nc.tensor.matmul(out_ps[:, :], m.zeros[:, 0:P], m.zeros[:, :], start=True, stop=False, skip_group_check=True)

            def project_out(n, pw, end):
                pe.wait_ge(o_lo, n + 1)
                w_hi, w_lo = (m_flat(t)[:, ds(pw * P, P)] for t in (m.wo_h, m.wo_l))
                for c in range(QC):
                    cs = slice(c * P, (c + 1) * P)
                    for k, (a, w) in enumerate([(o_h, w_hi), (o_h, w_lo), (o_l, w_hi)]):
                        mm = nc.tensor.matmul(out_ps[:, cs], a[:, cs], w, start=False,
                                              stop=(end and c == QC - 1 and k == 2), skip_group_check=True)
                mm.then_inc(out_mm, 1)

            def first_front():
                project_k(0, 0)
                pe.wait_ge(k_out, 1)
                project_q(0, 0, 0, 0)
                pe.wait_ge(q_out[0], 1)
                project_q(1, 0, 0, 0)
                open_output(0)

            def body(n, b, p, wrap, lag, out):
                bx, pw = (b + 1, 0) if wrap else (b, p + 1)
                scores(0, n)
                pe.wait_ge(*((q_out[1], 1) if isinstance(n, int) and n == 0 else (v_lo, n)))
                project_k(bx, pw)
                if out is not None:
                    project_out(n - 2, PAIRS - 1 if out is CLOSE else out, out is CLOSE)
                if lag:
                    transposes(1, n - 1, [0, 1])
                pe.wait_ge(k_out, n + 2)
                project_q(0, n + 1, bx, pw)
                if lag:
                    transposes(1, n - 1, [2])
                pe.wait_ge(q_out[0], n + 2)
                project_q(1, n + 1, bx, pw)
                if lag:
                    weighted_values(n - 1)
                scores(1, n)
                transposes(0, n, [0, 1])
                pe.wait_ge(q_out[1], n + 2)
                project_v(b, p)
                transposes(0, n, [2])
                if out is CLOSE:
                    open_output(b)

            def last():
                n = B * PAIRS - 1
                transposes(1, n, [0, 1, 2])
                weighted_values(n)
                project_out(n - 1, PAIRS - 2, False)
                project_out(n, PAIRS - 1, True)

            schedule(pe, first_front, body, None, last)

        @block.scalar
        def _(act):
            def exps(h, n, u_list):
                for u in u_list:
                    act.wait_ge(max_done[h], count(n, u))
                    if u == 0:
                        act.wait_ge(t_mm[h], 3 * n)
                    for c, col in UNIT_CHUNKS[u]:
                        w = P * (c + 1)
                        ins = nc.scalar.activation(prob[h][:, P_OFF[c]:P_OFF[c] + w], score_ps[u][:, col:col + w], ACT.Exp,
                                                   bias=nmax[h][:, c:c + 1], accum_out=sums[h][:, c:c + 1])
                    ins.then_inc(exp_done[h], 1)

            def pt_high(h, n, u_list):
                for u in u_list:
                    act.wait_ge(t_mm[h], count(n, u))
                    if u == 0:
                        act.wait_ge(pv_mm, n)
                    w = T_WIDTH[u]
                    nc.scalar.activation(pt_h[h][:, T_OFF[u]:T_OFF[u] + w], pt_ps[(3 * h + u) % 2][:, 0:w],
                                         ACT.Copy).then_inc(pt_hi[h], 1)

            def normalise(n):
                act.wait_ge(r_ready, n + 1)
                for c in range(QC):
                    pr = prob[0][:, P_OFF[c]:P_OFF[c] + P * (c + 1)]
                    ins = nc.scalar.activation(pr, pr, ACT.Copy, scale=rsum[0][:, c:c + 1])
                ins.then_inc(p_ready[0], 1)

            def o_high(n):
                act.wait_ge(pv_mm, n + 1)
                if not (isinstance(n, int) and n < 1):
                    act.wait_ge(out_mm, n)
                nc.scalar.activation(o_h[:, :], pv_ps[:, :], ACT.Copy).then_inc(o_hi, 1)

            def v_high(n):
                act.wait_ge(v_mm, n + 1)
                act.wait_ge(pv_mm, n)
                nc.scalar.activation(v_h[:, :, :].rearrange("p c n -> p (c n)"), proj_ps[:, :], ACT.Copy,
                                     scale=W_SCALE).then_inc(v_hi, 1)

            def k_copy(n):
                act.wait_ge(k_mm, n + 1)
                act.wait_ge(k_split[1], n)
                nc.scalar.activation(k32[:, :], proj_ps[:, :], ACT.Copy, scale=W_SCALE * QK_SCALE).then_inc(k_out, 1)

            def body(n, b, p, wrap, lag, out):
                k_copy(n + 1)
                if lag:
                    pt_high(1, n - 1, [0])
                exps(0, n, [0])
                if lag:
                    pt_high(1, n - 1, [1, 2])
                exps(0, n, [1, 2])
                normalise(n)
                if lag:
                    o_high(n - 1)
                exps(1, n, [0])
                pt_high(0, n, [0])
                exps(1, n, [1])
                pt_high(0, n, [1])
                v_high(n)
                exps(1, n, [2])
                pt_high(0, n, [2])

            def last():
                n = B * PAIRS - 1
                pt_high(1, n, [0, 1, 2])
                o_high(n)

            nc.scalar.preload_act_table(ACT.Exp)
            schedule(act, lambda: k_copy(0), body, None, last)

        @block.vector
        def _(dve):
            def maxima(h, n):
                for u in range(3):
                    dve.wait_ge(s_mm[h], count(n, u))
                    for c, col in UNIT_CHUNKS[u]:
                        ins = nc.vector.tensor_reduce(nmax[h][:, c:c + 1], score_ps[u][:, col:col + P * (c + 1)],
                                                      AX.X, ALU.max, negate=True)
                    ins.then_inc(max_done[h], 1)

            def reciprocals(h, n):
                dve.wait_ge(exp_done[h], count(n, 2))
                nc.vector.reciprocal(rsum[h][:, :], sums[h][:, :]).then_inc(dve_steps, 1)
                dve.wait_ge(dve_steps, 2 * n + h + 1)

            def scaled_reciprocals(n):
                reciprocals(0, n)
                nc.vector.tensor_scalar(rsum[0][:, :], rsum[0][:, :], P_SCALE, None, ALU.mult).then_inc(r_ready, 1)

            def normalise(n):
                h = 1
                reciprocals(h, n)
                for c in range(QC):
                    pr = prob[h][:, P_OFF[c]:P_OFF[c] + P * (c + 1)]
                    ins = nc.vector.tensor_scalar(pr, pr, rsum[h][:, c:c + 1], P_SCALE, ALU.mult, ALU.mult)
                ins.then_inc(p_ready[h], 1)

            def pt_low(h, n, u_list):
                for u in u_list:
                    dve.wait_ge(pt_hi[h], count(n, u))
                    w = T_WIDTH[u]
                    nc.vector.tensor_tensor(pt_l[h][:, T_OFF[u]:T_OFF[u] + w], pt_ps[(3 * h + u) % 2][:, 0:w],
                                            pt_h[h][:, T_OFF[u]:T_OFF[u] + w], ALU.subtract).then_inc(pt_lo[h], 1)

            def q_evac(h, n, pw):
                dve.wait_ge(q_mm[h], n + 1)
                dve.wait_ge(q_split[h], n)
                nc.vector.scalar_tensor_tensor(q32[h][:, :], proj_ps[:, :], m_flat(m.q_bias)[:, ds(PAIRS * h + pw, 1)],
                                               m.q_mult[:, h, :], ALU.add, ALU.mult).then_inc(q_out[h], 1)

            def o_low(n):
                dve.wait_ge(o_hi, n + 1)
                nc.vector.tensor_tensor(o_l[:, :], pv_ps[:, :], o_h[:, :], ALU.subtract).then_inc(o_lo, 1)

            def v_low(n):
                dve.wait_ge(v_hi, n + 1)
                nc.vector.scalar_tensor_tensor(v_l[:, :, :].rearrange("p c n -> p (c n)"), proj_ps[:, :], W_SCALE,
                                               v_h[:, :, :].rearrange("p c n -> p (c n)"), ALU.mult, ALU.subtract).then_inc(v_lo, 1)

            def add_bias(b):
                xb = m_flat(m.x)[:, ds(b * S, S)].rearrange("p (c d) -> p c d", d=D)
                nc.vector.tensor_tensor(xb, xb, m.bo_bc[:, :].unsqueeze(1).to_broadcast([P, QC, D]), ALU.add).then_inc(bias_in, 1)

            def batch_sum(b):
                dve.wait_ge(out_mm, PAIRS * (b + 1))
                dve.wait_ge(bias_in, b + 1)
                nc.vector.scalar_tensor_tensor(y[:, :, :].rearrange("p c d -> p (c d)"), out_ps[:, :], O_SCALE / P_SCALE,
                                               m_flat(m.x)[:, ds(b * S, S)], ALU.mult, ALU.add).then_inc(y_done, 1)

            def batch_stats(b):
                dve.wait_ge(y_done, b + 1)
                layer_norm_stats(nc, dve, m, b, y, st, mv)

            def batch_norm(b):
                layer_norm_apply(nc, dve, m, b, y, mv, rstd,
                                 m_flat(m.x)[:, ds(b * S, S)].rearrange("p (c d) -> p c d", d=D)).then_inc(ln_dve, 1)

            def body(n, b, p, wrap, lag, out):
                maxima(0, n)
                if lag:
                    pt_low(1, n - 1, [0])
                q_evac(0, n + 1, 0 if wrap else p + 1)
                if lag:
                    pt_low(1, n - 1, [1, 2])
                behind = wrap and not (isinstance(b, int) and b == 0)
                if behind:
                    batch_stats(b - 1)
                scaled_reciprocals(n)
                if out is CLOSE:
                    dve.wait_ge(ln_dve, b)
                    batch_sum(b - 1)
                q_evac(1, n + 1, 0 if wrap else p + 1)
                maxima(1, n)
                pt_low(0, n, [0])
                if lag:
                    o_low(n - 1)
                pt_low(0, n, [1])
                v_low(n)
                pt_low(0, n, [2])
                normalise(n)
                if wrap:
                    add_bias(b)
                if behind:
                    batch_norm(b - 1)

            def first_front():
                vector_gate(nc, m).then_inc(ln_dve, 1)
                q_evac(0, 0, 0)
                q_evac(1, 0, 0)

            def last():
                n = B * PAIRS - 1
                pt_low(1, n, [0, 1, 2])
                o_low(n)
                batch_sum(B - 1)
                batch_stats(B - 1)
                batch_norm(B - 1)

            schedule(dve, first_front, body, None, last)

        @block.gpsimd
        def _(pool):
            def split(rows, src, hi, lo, chain_n):
                pool_gate(nc, m, rows)
                nc.gpsimd.affine_select(out=hi, in_=src, compare_op=ALU.is_ge, fill=0.0, base=0,
                                        pattern=[[1, S]], channel_multiplier=0).then_inc(pool_steps, 1)
                pool.wait_ge(pool_steps, chain_n)
                return nc.gpsimd.tensor_tensor(lo, src, hi, ALU.subtract)

            def split_q(h, n):
                pool.wait_ge(q_out[h], n + 1)
                pool.wait_ge(s_mm[h], 3 * n)
                pool.wait_ge(k_split[h], n + 1)
                split(slice(0, P), q32[h][:, :], q_h[h][:, :], q_l[h][:, :], 4 * n + 2 + 2 * h).then_inc(q_split[h], 1)

            def split_k(h, n):
                if h == 0:
                    pool.wait_ge(k_out, n + 1)
                pool.wait_ge(s_mm[h], 3 * n)
                pool.wait_ge(q_split[1 - h], n + h)
                r = slice(64 * h, 64 * h + 64)
                split(r, k32[r, :], m.k_h[h][r, :], m.k_l[h][r, :], 4 * n + 1 + 2 * h).then_inc(k_split[h], 1)

            def front(n):
                for h in range(2):
                    split_k(h, n)
                    split_q(h, n)

            def body(n, b, p, wrap, lag, out):
                front(n + 1)
                if wrap and not (isinstance(b, int) and b == 0):
                    layer_norm_gpsimd(nc, pool, m, b - 1, mv, ve, rstd)

            def last():
                layer_norm_gpsimd(nc, pool, m, B - 1, mv, ve, rstd)

            schedule(pool, lambda: front(0), body, None, last)


def moe_top2_phase(nc, io, m):
    with ExitStack() as ctx:
        sb = lambda name, shape, dt: ctx.enter_context(nc.sbuf_tensor(name, shape, dt))
        sem = lambda name: ctx.enter_context(nc.semaphore(name))
        FC = F0 // P
        w1_h, w1_l = (sb(n, [P, E0 * F0], F16) for n in ("w1_h", "w1_l"))
        w2_h, w2_l = (sb(n, [P, E0 * FC * D], F16) for n in ("w2_h", "w2_l"))
        wg_h, wg_l = (sb(n, [P, E0], F16) for n in ("wg_h", "wg_l"))
        b1_cols = sb("b1_cols", [P, E0 * FC], F32)
        logit = sb("logit", [P, NCH, E0], F32)
        lmax = sb("lmax", [P, NCH], F32)
        held, left = (sb(n, [P, NCH, E0], F32) for n in ("held", "left"))
        best, second, share = (sb(n, [P, NCH], F32) for n in ("best", "second", "share"))
        pick = [sb(f"pick{k}", [P, NCH, E0], F32) for k in range(2)]
        comb = sb("comb", [P, NCH, E0], F32)
        comb_t_h, comb_t_l = (sb(n, [QC * E0, B * P], F16) for n in ("comb_t_h", "comb_t_l"))
        b2_h, b2_l = (sb(n, [QC * E0, QC * D], F16) for n in ("b2_h", "b2_l"))
        hid32 = [[sb(f"hid32_{k}{c}", [P, S], F32) for c in range(FC)] for k in range(2)]
        hid_h = [[sb(f"hid_h{k}{c}", [P, S], F16) for c in range(FC)] for k in range(2)]
        hid_l = [[sb(f"hid_l{k}{c}", [P, S], F16) for c in range(FC)] for k in range(2)]
        st = sb("f_st", [P, QC, 6], F32)
        mv = sb("f_mv", [P, QC, 2], F32)
        ve = sb("f_ve", [P, QC], F32)
        rstd = sb("f_rstd", [P, QC], F32)
        banks = [ctx.enter_context(nc.psum_tensor(f"fps{i}", [P, 512], F32)) for i in range(8)]
        hid_ps, y_ps, xt_ps = banks[0:4], banks[4:6], banks[6:8]
        tok_ps = [b[:, :] for b in (xt_ps[0], xt_ps[1], hid_ps[2], hid_ps[3])]

        xt_mm, xt_hi, xt_lo, lg_mm = sem("f_xt_mm"), sem("f_xt_hi"), sem("f_xt_lo"), sem("f_lg_mm")
        wg_split, b1_out = sem("f_wg_split"), sem("f_b1_out")
        w_split, b1_mm, shifted, exps_done = sem("f_w_split"), sem("f_b1_mm"), sem("f_shifted"), sem("f_exps")
        dsteps, comb_done, ct_mm, ct_out, b2_mm, b2_out = (sem(n) for n in ("f_steps", "f_comb", "f_ct_mm", "f_ct_out", "f_b2_mm", "f_b2_out"))
        ct_lo = sem("f_ct_lo")
        h_mm, h_relu, h_hi, h_lo = ([sem(f"f_{n}{c}") for c in range(FC)] for n in ("h_mm", "h_relu", "h_hi", "h_lo"))
        y_out = [sem(f"f_y_out{k}") for k in range(2)]
        y_mm, aw_split = sem("f_y_mm"), sem("f_aw_split")

        def schedule(eng, unit, stats, norm):
            def tile(t, behind):
                unit(E0 * t, E0 // 2 * t, 0, t, 1, t, 0)
                if behind:
                    stats(t - 1)
                unit(E0 * t + 1, E0 // 2 * t, 1, t, 2, t, 1)
                if behind:
                    norm(t - 1)
                with eng.Fori(1, E0 // 2 - 1) as i:
                    for k in range(2):
                        unit(E0 * t + 2 * i + k, E0 // 2 * t + i, k, t, 2 * i + k + 1, t, 2 * i + k)
                half = E0 // 2 * t + E0 // 2 - 1
                unit(E0 * t + E0 - 2, half, 0, t, E0 - 1, t, E0 - 2)
                unit(E0 * t + E0 - 1, half, 1, t + 1, 0, t, E0 - 1)

            tile(0, False)
            with eng.Fori(1, B) as t:
                tile(t, True)
            stats(B - 1)
            norm(B - 1)

        block = ctx.enter_context(nc.Block())

        def router(pe, t):
            pe.wait_ge(xt_lo, t + 1)
            for c in range(QC):
                ch = t * QC + c
                o = y_ps[0][:, ch * E0:(ch + 1) * E0]
                xs = slice(ch * P, (ch + 1) * P)
                nc.tensor.matmul(o, m.xt_h[:, xs], wg_h[:, :], start=True, stop=False)
                nc.tensor.matmul(o, m.xt_h[:, xs], wg_l[:, :], start=False, stop=False)
                last = nc.tensor.matmul(o, m.xt_l[:, xs], wg_h[:, :], start=False, stop=True)
            last.then_inc(lg_mm, 1)

        @block.tensor
        def _(pe):
            for t in range(B):
                if t >= 4:
                    pe.wait_ge(xt_lo, t - 3)
                for c in range(QC):
                    last = nc.tensor.transpose(tok_ps[t % 4][:, c * P:(c + 1) * P], m.x[:, t * QC + c, :], m.ident[:, :])
                last.then_inc(xt_mm, 1)
                if t == 0:
                    pe.wait_ge(m.f0_loaded, m.F0_LOADS)
                    nc.tensor.transpose(hid_ps[0][:, 0:E0 * FC], m.b1_rows[:, :], m.ident[0:E0 * FC, 0:E0 * FC]).then_inc(b1_mm, 1)
                    pe.wait_ge(wg_split, 2)
                if t >= 2:
                    router(pe, t - 2)
            router(pe, B - 2)
            router(pe, B - 1)

            def biases():
                pe.wait_ge(comb_done, 1)
                for t in range(B):
                    last = nc.tensor.transpose(xt_ps[t // 4][0:QC * E0, (t % 4) * P:(t % 4 + 1) * P],
                                               comb[:, t * QC:(t + 1) * QC, :].rearrange("p c e -> p (c e)"), m.ident[:, :])
                    if t % 4 == 3:
                        last.then_inc(ct_mm, 1)
                pe.wait_ge(wg_split, 4)
                for t in range(B):
                    pe.wait_ge(ct_lo, t // 4 + 1)
                    if t >= 2:
                        pe.wait_ge(b2_out, t - 1)
                    ts, o = slice(t * P, (t + 1) * P), y_ps[t % 2][:, :]
                    nc.tensor.matmul(o, comb_t_h[:, ts], b2_h[:, :], start=True, stop=False)
                    nc.tensor.matmul(o, comb_t_h[:, ts], b2_l[:, :], start=False, stop=False)
                    nc.tensor.matmul(o, comb_t_l[:, ts], b2_h[:, :], start=False, stop=True).then_inc(b2_mm, 1)

            def hidden(n, k, t, e):
                for c in range(FC):
                    w_hi, w_lo = (w[:, ds(e * F0 + c * P, P)] for w in (w1_h, w1_l))
                    x_hi, x_lo = (x[:, ds(t * S, S)] for x in (m.xt_h, m.xt_l))
                    o = hid_ps[2 * k + c][:, :]
                    nc.tensor.matmul(o, w_hi, x_hi, start=True, stop=False)
                    nc.tensor.matmul(o, w_lo, x_hi, start=False, stop=False)
                    nc.tensor.matmul(o, w_hi, x_lo, start=False, stop=True).then_inc(h_mm[c], 1)

            def unit(n, half, k, tn, en, t, e):
                hidden(n + 1, 1 - k, tn, en)
                for c in range(FC):
                    pe.wait_ge(h_lo[c], n + 1)
                pe.wait_ge(y_out[k], half + 1)
                for c in range(QC):
                    cs = slice(c * P, (c + 1) * P)
                    for f in range(FC):
                        w_hi, w_lo = (w[:, ds((e * FC + f) * D, D)] for w in (w2_h, w2_l))
                        for j, (a, w) in enumerate([(hid_h, w_hi), (hid_h, w_lo), (hid_l, w_hi)]):
                            mm = nc.tensor.matmul(y_ps[k][:, cs], a[k][f][:, cs], w, start=(f == 0 and j == 0),
                                                  stop=(f == FC - 1 and j == 2))
                mm.then_inc(y_mm, 1)

            pe.wait_ge(w_split, 4)
            pe.wait_ge(b1_out, 1)
            hidden(0, 0, 0, 0)
            biases()
            schedule(pe, unit, lambda t: None, lambda t: None)

        @block.scalar
        def _(act):
            nc.scalar.preload_act_table(ACT.Exp)
            for t in range(B):
                act.wait_ge(xt_mm, t + 1)
                nc.scalar.activation(m.xt_h[:, t * S:(t + 1) * S], tok_ps[t % 4], ACT.Copy).then_inc(xt_hi, 1)
                if t == 0:
                    act.wait_ge(b1_mm, 1)
                    nc.scalar.activation(b1_cols[:, :], hid_ps[0][:, 0:E0 * FC], ACT.Copy).then_inc(b1_out, 1)
            act.wait_ge(shifted, 1)
            nc.scalar.activation(logit[:, :, :], logit[:, :, :], ACT.Exp).then_inc(exps_done, 1)

            def relu(n, k, e):
                for c in range(FC):
                    act.wait_ge(h_mm[c], n + 1)
                    nc.scalar.activation(hid32[k][c][:, :], hid_ps[2 * k + c][:, :], ACT.Relu,
                                         bias=b1_cols[:, ds(e * FC + c, 1)]).then_inc(h_relu[c], 1)

            act.wait_ge(b1_out, 1)
            relu(0, 0, 0)
            for k in range(2):
                act.wait_ge(ct_mm, k + 1)
                nc.scalar.activation(comb_t_h[:, k * S:(k + 1) * S], xt_ps[k][0:QC * E0, :], ACT.Copy).then_inc(ct_out, 1)
            schedule(act, lambda n, half, k, tn, en, t, e: relu(n + 1, 1 - k, en), lambda t: None, lambda t: None)

        @block.vector
        def _(dve):
            steps = Steps(dve, dsteps)
            dve.wait_ge(m.f0_loaded, m.F0_LOADS)
            nc.vector.tensor_copy(wg_h[:, :], m.wg_raw[:, :]).then_inc(wg_split, 1)
            dve.wait_ge(wg_split, 1)
            nc.vector.tensor_tensor(wg_l[:, :], m.wg_raw[:, :], wg_h[:, :], ALU.subtract).then_inc(wg_split, 1)
            nc.vector.tensor_copy(b2_h[:, :], m.b2_blocks[:, :]).then_inc(wg_split, 1)
            dve.wait_ge(wg_split, 3)
            nc.vector.tensor_tensor(b2_l[:, :], m.b2_blocks[:, :], b2_h[:, :], ALU.subtract).then_inc(wg_split, 1)
            for t in range(B):
                dve.wait_ge(xt_hi, t + 1)
                nc.vector.tensor_tensor(m.xt_l[:, t * S:(t + 1) * S], tok_ps[t % 4], m.xt_h[:, t * S:(t + 1) * S],
                                        ALU.subtract).then_inc(xt_lo, 1)
            dve.wait_ge(lg_mm, B)
            lg_ps = y_ps[0][:, 0:NCH * E0].rearrange("p (c e) -> p c e", e=E0)
            steps.step(nc.vector.tensor_tensor(logit[:, :, :], lg_ps, m.bg_bc[:, :].unsqueeze(1).to_broadcast([P, NCH, E0]), ALU.add))
            steps.step(nc.vector.tensor_reduce(lmax[:, :], logit[:, :, :], AX.X, ALU.max))
            nc.vector.tensor_tensor(logit[:, :, :], logit[:, :, :], lmax[:, :].unsqueeze(2).to_broadcast([P, NCH, E0]),
                                    ALU.subtract).then_inc(shifted, 1)
            dve.wait_ge(exps_done, 1)
            wide = lambda a: a[:, :].unsqueeze(2).to_broadcast([P, NCH, E0])
            iota = m.iota8[:, :].unsqueeze(1).to_broadcast([P, NCH, E0])
            full = lambda a: a[:, :, :]
            steps.step(nc.vector.tensor_scalar(full(held), full(logit), 1.0, -float(E0), ALU.is_ge, ALU.mult))
            steps.step(nc.vector.tensor_tensor(full(held), full(held), iota, ALU.add))
            steps.step(nc.vector.tensor_reduce(best[:, :], full(held), AX.X, ALU.min))
            steps.step(nc.vector.tensor_tensor(full(pick[0]), full(held), wide(best), ALU.is_equal))
            steps.step(nc.vector.scalar_tensor_tensor(full(left), full(pick[0]), -2.0, full(logit), ALU.mult, ALU.add))
            steps.step(nc.vector.tensor_reduce(second[:, :], full(left), AX.X, ALU.max))
            steps.done(nc.vector.tensor_scalar(share[:, :], second[:, :], 1.0, None, ALU.add))
            steps.step(nc.vector.tensor_tensor(full(held), full(left), wide(second), ALU.is_ge))
            steps.done(nc.vector.reciprocal(share[:, :], share[:, :]))
            steps.step(nc.vector.scalar_tensor_tensor(full(held), full(held), -float(E0), iota, ALU.mult, ALU.add))
            steps.step(nc.vector.tensor_reduce(best[:, :], full(held), AX.X, ALU.min))
            steps.step(nc.vector.tensor_tensor(full(pick[1]), full(held), wide(best), ALU.is_equal))
            steps.step(nc.vector.tensor_tensor(full(pick[1]), full(pick[1]), wide(second), ALU.mult))
            steps.step(nc.vector.tensor_tensor(full(comb), full(pick[0]), full(pick[1]), ALU.add))
            nc.vector.tensor_tensor(full(comb), full(comb), wide(share), ALU.mult).then_inc(comb_done, 1)
            for k in range(2):
                ks = slice(k * S, (k + 1) * S)
                dve.wait_ge(ct_out, k + 1)
                nc.vector.tensor_tensor(comb_t_l[:, ks], xt_ps[k][0:QC * E0, :], comb_t_h[:, ks], ALU.subtract).then_inc(ct_lo, 1)
            for t in range(B):
                dve.wait_ge(b2_mm, t + 1)
                xs = m.x[:, t * QC:(t + 1) * QC, :].rearrange("p c d -> p (c d)")
                nc.vector.tensor_tensor(xs, y_ps[t % 2][:, :], xs, ALU.add).then_inc(b2_out, 1)

            def high(n, k):
                for c in range(FC):
                    dve.wait_ge(h_relu[c], n + 1)
                    nc.vector.tensor_copy(hid_h[k][c][:, :], hid32[k][c][:, :]).then_inc(h_hi[c], 1)
                dve.wait_ge(h_hi[0], n + 1)
                nc.vector.tensor_tensor(hid_l[k][0][:, :], hid32[k][0][:, :], hid_h[k][0][:, :], ALU.subtract).then_inc(h_lo[0], 1)

            def unit(n, half, k, tn, en, t, e):
                high(n + 1, 1 - k)
                dve.wait_ge(y_mm, n + 1)
                for c in range(QC):
                    xc = m_flat(m.x)[:, ds(t * S + c * D, D)]
                    ins = nc.vector.scalar_tensor_tensor(xc, y_ps[k][:, c * D:(c + 1) * D],
                                                         m_flat(comb)[:, ds(t * (QC * E0) + c * E0 + e, 1)], xc, ALU.mult, ALU.add)
                ins.then_inc(y_out[k], 1)

            def stats(t):
                dve.wait_ge(y_out[1], E0 // 2 * (t + 1) + 1)
                vector_gate(nc, m)
                layer_norm_stats(nc, dve, m, B + t, tokens(t), st, mv)

            def norm(t):
                layer_norm_apply(nc, dve, m, B + t, tokens(t), mv, rstd, tokens(t))

            tokens = lambda t: m_flat(m.x)[:, ds(t * S, S)].rearrange("p (c d) -> p c d", d=D)
            nc.vector.memset(m.gate_v[:, :], 0.0).then_inc(y_out[0], 1)
            nc.vector.memset(m.gate_v2[:, :], 0.0).then_inc(y_out[1], 1)
            high(0, 0)
            schedule(dve, unit, stats, norm)

        @block.gpsimd
        def _(pool):
            def low(n, k):
                pool.wait_ge(h_hi[1], n + 1)
                nc.gpsimd.tensor_tensor(hid_l[k][1][:, :], hid32[k][1][:, :], hid_h[k][1][:, :], ALU.subtract).then_inc(h_lo[1], 1)

            pool.wait_ge(m.f0_loaded, m.F0_LOADS)
            for hi, raw in ((w1_h, m.w1_raw), (w2_h, m.w2_raw)):
                flat = m_flat(raw)
                nc.gpsimd.affine_select(out=hi[:, :], in_=flat, compare_op=ALU.is_ge, fill=0.0, base=0,
                                        pattern=[[1, flat.shape[-1]]], channel_multiplier=0).then_inc(w_split, 1)
            pool.wait_ge(w_split, 2)
            for lo, hi, raw in ((w1_l, w1_h, m.w1_raw), (w2_l, w2_h, m.w2_raw)):
                nc.gpsimd.tensor_tensor(lo[:, :], m_flat(raw), hi[:, :], ALU.subtract).then_inc(w_split, 1)
            pool.wait_ge(m.a_loaded, m.A_LOADS)
            matrices = []
            for k in range(5):
                raw, hi, lo = (t[:, k, :] for t in (m.a_w, m.a_w_h, m.a_w_l))
                if k < 2:
                    raw = raw.rearrange("p (g h d) -> p g d h", g=4, h=4)
                    hi, lo = (t.rearrange("p (g d h) -> p g d h", g=4, h=4) for t in (hi, lo))
                matrices.append((raw, hi, lo))
            for raw, hi, lo in matrices:
                nc.gpsimd.tensor_copy(hi, raw).then_inc(aw_split, 1)
            pool.wait_ge(aw_split, 5)
            for raw, hi, lo in matrices:
                nc.gpsimd.tensor_tensor(lo, raw, hi, ALU.subtract)
            low(0, 0)
            schedule(pool, lambda n, half, k, tn, en, t, e: low(n + 1, 1 - k),
                     lambda t: layer_norm_gpsimd(nc, pool, m, B + t, mv, ve, rstd), lambda t: None)


def gauss_attention_phase(nc, io, m):
    with ExitStack() as ctx:
        sb = lambda name, shape, dt: ctx.enter_context(nc.sbuf_tensor(name, shape, dt))
        sem = lambda name: ctx.enter_context(nc.semaphore(name))
        G = 4
        SC = 64.0
        K_SCALE = SC * D1 ** -0.5
        w_h, w_l = m.a_w_h, m.a_w_l
        upz = sb("a_upz", [P, 2 * H1], F32)
        head_mask = sb("a_head_mask", [P, H1], F32)
        bk_s = sb("a_bk_s", [P, 1], F32)
        bf = sb("a_bf", [P, 1], F32)
        gbias = sb("a_gbias", [P, 1], F32)
        qsum = sb("a_qsum", [P, 1], F32)
        ident16 = sb("a_ident16", [P, P], F16)
        xs = sb("a_xs", [P, QC, D], F32)
        xt_h, xt_l = (sb(n, [P, S], F16) for n in ("a_xt_h", "a_xt_l"))
        q32, k32, c32, v32 = (sb(n, [P, S], F32) for n in ("a_q32", "a_k32", "a_c32", "a_v32"))
        q_h, q_l, k_h, k_l, coef_t = (sb(n, [P, S], F16) for n in ("a_q_h", "a_q_l", "a_k_h", "a_k_l", "a_coef_t"))
        epz = sb("a_epz", [P, QC, 2 * H1], F32)
        cent = sb("a_cent", [P, QC, H1], F32)
        ca, cb, cc = (sb(n, [P, QC, H1], F32) for n in ("a_ca", "a_cb", "a_cc"))
        coef = sb("a_coef", [P, QC, G, 8, G], F16)
        qop = sb("a_qop", [P, G, S], F16)
        kop = sb("a_kop", [P, G, G, S], F16)
        vaug = sb("a_vaug", [P, QC, H1, 32], F32)
        nm = [sb(f"a_nm{k}", [P, QC, G], F16) for k in range(2)]
        nm_t = [sb(f"a_nm_t{k}", [G, S], F16) for k in range(2)]
        pt = [[sb(f"a_pt{k}{r}", [P, 2, S], F32) for r in range(2)] for k in range(2)]
        pvs = sb("a_pvs", [P, S], F32)
        rsum = sb("a_rsum", [P, QC, G], F32)
        ctxt = sb("a_ctx", [P, QC, P], F32)
        ct_h, ct_l = (sb(n, [P, S], F16) for n in ("a_ct_h", "a_ct_l"))
        xres = sb("a_xres", [P, QC, D], F32)
        y = sb("a_y", [P, QC, D], F32)
        st = sb("a_st", [P, QC, 6], F32)
        mv = sb("a_mv", [P, QC, 2], F32)
        ve = sb("a_ve", [P, QC], F32)
        rstd = sb("a_rstd", [P, QC], F32)
        s_ps = [ctx.enter_context(nc.psum_tensor(f"a_s{k}", [P, S], F32)) for k in range(2)]
        st_ps = [ctx.enter_context(nc.psum_tensor(f"a_st{r}", [P, 2, S], F32)) for r in range(2)]
        pv_ps = ctx.enter_context(nc.psum_tensor("a_pv", [P, S], F32))
        misc = ctx.enter_context(nc.psum_tensor("a_misc", [P, S], F32))
        misc16 = misc[:, :].bitcast(F16)

        names = lambda *a: [sem("a_" + n) for n in a]
        setup_done, kzero, kconst, vset = names("setup_done", "kzero", "kconst", "vset")
        misc_mm, misc_out = names("misc_mm", "misc_out")
        xs_in, xt_hi, ct_hi, q_split, k_split, pool_steps = names("xs_in", "xt_hi", "ct_hi", "q_split", "k_split", "pool_steps")
        cf_steps, coef_done, vaug_done, pvs_done, ctx_steps, xres_done = names(
            "cf_steps", "coef_done", "vaug_done", "pvs_done", "ctx_steps", "xres_done")
        ln_dve, pv_mm, parts_out, cent_done, cf_pool = names("ln_dve", "pv_mm", "parts_out", "cent_done", "cf_pool")
        s_mm, max_done, st_mm, exp_done = ([sem(f"a_{n}{k}") for k in range(2)] for n in ("s_mm", "max_done", "st_mm", "exp_done"))
        op_in = [sem(f"a_op_in{g}") for g in range(G)]
        nm_in = [sem(f"a_nm_in{g}") for g in range(G)]
        OP_LOADS = (1 + G) * 16
        PARTS = 7 * 16
        q_dram = nc.dram_tensor("q_parts", (4, 32, G, S), F16).ap()
        k_dram = nc.dram_tensor("k_parts", (3, 32, G, S), F16).ap()

        PREP = ["XT", "Q", "K", "GB", "F", "PZ", "CF", "V"]
        MIDDLE = {4: "nm0", 8: "nm1", 9: "CT", 10: "OUT", 12: "nm2"}
        END = {0: "ctx1", 1: "XT", 2: "Q", 4: "ctx2", 5: "K", 6: "GB", 7: "F", 8: "ctx3", 9: "PZ", 11: "CF", 12: "ctx0",
               13: "V", 15: "nm3"}
        SLOTS = 4 * G
        BEHIND = ["ctx1", "ctx2", "ctx3", "CT", "OUT"]
        PARTS_OF = {"first": ("ahead", "own"), "middle": ("ahead", "own", "behind"), "last": ("own", "behind"), "tail": ("behind",)}

        def part_of(name):
            return "ahead" if name in PREP else "behind" if name in BEHIND else "own"

        def uses(kind):
            order = [t[at] for at in range(SLOTS) for t in (MIDDLE, END) if at in t]
            return [u for u in order if part_of(u) in PARTS_OF[kind]]

        def use(kind, b, name):
            if kind == "prep0":
                return PREP.index(name)
            base = len(PREP)
            if kind != "first":
                base = base + len(uses("first")) + len(uses("middle")) * ((b if kind == "middle" else B - 1) - 1)
            if kind == "tail":
                base = base + len(uses("last"))
            return base + uses(kind).index(name)

        def schedule(eng, do):
            def step(name, *args):
                if name in do:
                    do[name](*args)

            def shared_use(name, kind, b):
                part = part_of(name)
                if part in PARTS_OF[kind]:
                    batch = {"ahead": b + 1, "own": b, "behind": b - 1}[part]
                    if name[-1] in "0123":
                        step(name[:-1], kind, b, batch, int(name[-1]))
                    else:
                        step(name, kind, b, batch)

            def batch(kind, b):
                behind, own = kind != "first", kind != "tail"
                for at in range(SLOTS if own else 12):
                    g, s = divmod(at, G)
                    step("slot", kind, b, at)
                    head = (b, g, s) if own else None
                    unit = ((b, (at - 6) // G, (at - 6) % G, kind == "first" and at == 6) if at >= 6 and own
                            else (b - 1, (at + 10) // G, (at + 10) % G, False) if at < 6 and behind else None)
                    for half, table in ((0, MIDDLE), (1, END)):
                        step("scores", half, head, unit)
                        if half and kind == "tail" and at == 6:
                            step("value", b - 1, G - 1, QC - 1)
                        if half and s == 2 and (at < 8 and behind or at >= 8 and own):
                            step("group_end", *((b - 1, g + 2) if at < 8 else (b, g - 2)))
                        if at in table:
                            shared_use(table[at], kind, b)
                    if at == 11 and behind:
                        step("norm", b - 1)

            step("setup")
            for name in PREP:
                step(name, "prep0", 0, 0)
            step("prepared")
            batch("first", 0)
            with eng.Fori(1, B - 1) as b:
                batch("middle", b)
            batch("last", B - 1)
            batch("tail", B)

        block = ctx.enter_context(nc.Block())

        @block.sync
        def _(sp):
            def setup():
                for dst, src in ((m.e_w1[:, :, :], io["L1_ffn_w1"].rearrange("e d f -> d e f")),
                                 (m.e_w2[:, :, :, :], io["L1_ffn_w2"].rearrange("e (c p) d -> p e c d", p=P)),
                                 (m.e_wg[:, :], io["L1_ffn_gate_w"])):
                    sp.dma_start(dst, src).then_inc(m.e_loaded, 16)
                sp.wait_ge(kzero, 1)
                for hh in range(G):
                    sp.dma_start(kop[96 + hh:P:G, hh, :, :],
                                 io["c_key_rows"].unsqueeze(1).to_broadcast([8, G, S])).then_inc(kconst, 16)
                sp.wait_ge(kconst, 16 * G)

            def spread(nb):
                sp.wait_ge(k_split, nb + 1)
                for g in range(G):
                    sp.wait_ge(op_in[g], OP_LOADS * nb)
                for n, src in ((0, q_h), (1, q_h), (2, q_l)):
                    sp.dma_start(q_dram[n].rearrange("r g n -> g r n"), src[:, :]).then_inc(parts_out, 16)
                for n, src in ((0, k_h), (1, k_l), (2, k_h)):
                    sp.dma_start(k_dram[n].rearrange("r g n -> g r n"), src[:, :]).then_inc(parts_out, 16)

            def spread_coef(kind, b, nb):
                sp.wait_ge(misc_out, use(kind, b, "CF") + 1)
                sp.dma_start(q_dram[3].rearrange("r g n -> g r n"), coef_t[:, :]).then_inc(parts_out, 16)
                sp.wait_ge(parts_out, PARTS * (nb + 1))

            def gather(nb, g):
                if not (isinstance(nb, int) and nb == 0):
                    sp.wait_ge(st_mm[1], 16 * (nb - 1) + 4 * g + 4)
                sp.dma_start(qop[:, g, :], q_dram[:, :, g, :].rearrange("t r n -> (t r) n")).then_inc(op_in[g], 16)
                for hh in range(G):
                    sp.dma_start(kop[hh:96:G, hh, g, :],
                                 k_dram.rearrange("t (d h) g n -> (t d) h g n", h=G)[:, hh, g, :]).then_inc(op_in[g], 16)

            def prepared():
                spread(0)
                spread_coef("prep0", 0, 0)
                for g in range(G):
                    gather(0, g)

            def slot(kind, b, at):
                if kind in ("middle", "last") and at in (1, 5):
                    gather(b, 2 + at // 4)
                if kind in ("first", "middle"):
                    if at == 8:
                        spread(b + 1)
                    if at == 13:
                        spread_coef(kind, b, b + 1)
                        gather(b + 1, 0)
                        gather(b + 1, 1)

            def minus_max(kind, b, _, g):
                sp.wait_ge(misc_out, use(kind, b, f"nm{g}") + 1)
                sp.dma_start(qop[P - G:P, g, :], nm_t[g % 2][:, :]).then_inc(nm_in[g], 16)

            schedule(sp, {"setup": setup, "prepared": prepared, "slot": slot, "nm": minus_max})
            for g in range(G):
                sp.wait_ge(nm_in[g], 16 * B)
            sp.wait_ge(m.e_loaded, 48)
            sp.wait_ge(m.e_loaded, 48)

        @block.tensor
        def _(pe):
            def shared(kind, b, name):
                pe.wait_ge(misc_out, use(kind, b, name))

            def tokens_t(kind, b, nb):
                pe.wait_ge(xs_in, nb + 1)
                shared(kind, b, "XT")
                for c in range(QC):
                    mm = nc.tensor.transpose(misc[:, c * P:(c + 1) * P], xs[:, c, :], m.ident[:, :])
                mm.then_inc(misc_mm, 1)

            def features(name, k, xh, xl):
                def run(kind, b, nb):
                    if name == "F":
                        pe.wait_ge(q_split, nb + 1)
                    shared(kind, b, name)
                    nc.tensor.matmul(misc[:, :], w_h[:, k, :], xh[:, :], start=True, stop=False)
                    nc.tensor.matmul(misc[:, :], w_l[:, k, :], xh[:, :], start=False, stop=False)
                    nc.tensor.matmul(misc[:, :], w_h[:, k, :], xl[:, :], start=False, stop=True).then_inc(misc_mm, 1)
                return run

            def rows(name, k, xh, xl):
                def run(kind, b, nb):
                    shared(kind, b, name)
                    for c in range(QC):
                        cs = slice(c * P, (c + 1) * P)
                        nc.tensor.matmul(misc[:, cs], xh[:, cs], w_h[:, k, :], start=True, stop=False)
                        nc.tensor.matmul(misc[:, cs], xh[:, cs], w_l[:, k, :], start=False, stop=False)
                        mm = nc.tensor.matmul(misc[:, cs], xl[:, cs], w_h[:, k, :], start=False, stop=True)
                    mm.then_inc(misc_mm, 1)
                return run

            def gate_bias(kind, b, nb):
                shared(kind, b, "GB")
                nc.tensor.matmul(misc[:, 0:1], m.a_wfg[:, :], qsum[:, :], start=True, stop=True).then_inc(misc_mm, 1)

            def centre_width(kind, b, nb):
                shared(kind, b, "PZ")
                for c in range(QC):
                    mm = nc.tensor.matmul(misc[:, c * 2 * H1:(c + 1) * 2 * H1], c32[:, c * P:(c + 1) * P], upz[:, :],
                                          start=True, stop=True)
                mm.then_inc(misc_mm, 1)

            def coefficients_t(kind, b, nb):
                pe.wait_ge(coef_done, nb + 1)
                shared(kind, b, "CF")
                for c in range(QC):
                    mm = nc.tensor.transpose(misc16[:, c * P:(c + 1) * P],
                                             coef[:, c, :, :, :].rearrange("p g t h -> p (g t h)"), ident16[:, :])
                mm.then_inc(misc_mm, 1)

            def head_scores(b, g, hh, c):
                if hh == 0 and c == 0:
                    pe.wait_ge(op_in[g], OP_LOADS * (b + 1))
                k = c % 2
                pe.wait_ge(max_done[k], 2 * (16 * b + 4 * g + hh) + c // 2)
                nc.tensor.matmul(s_ps[k][:, :], qop[:, g, c * P:(c + 1) * P], kop[:, hh, g, :], start=True,
                                 stop=True).then_inc(s_mm[k], 1)

            def scores(half, head, unit):
                for c in range(2 * half, 2 * half + 2):
                    if head:
                        head_scores(*head, c)
                    if not unit:
                        continue
                    b, g, kc, first = unit
                    if c == 0 and kc == 0:
                        pe.wait_ge(nm_in[g], 16 * (b + 1))
                    if c % 2 == 0:
                        r = c // 2
                        pe.wait_ge(exp_done[r], 16 * b + 4 * g + kc)
                        for i in range(2):
                            mm = nc.tensor.matmul(st_ps[r][:, i, :], kop[:, 2 * r + i, g, kc * P:(kc + 1) * P], qop[:, g, :],
                                                  start=True, stop=True)
                        mm.then_inc(st_mm[r], 1)
                if unit and half and not first:
                    value(*((b, g, kc - 1) if kc else (b, g - 1, QC - 1) if g else (b - 1, G - 1, QC - 1)))

            def value(b, g, kc):
                for r in range(2):
                    pe.wait_ge(exp_done[r], 16 * b + 4 * g + kc + 1)
                if kc == 0:
                    pe.wait_ge(vaug_done, 4 * b + g + 1)
                    pe.wait_ge(pvs_done, 4 * b + g)
                for hh in range(G):
                    mm = nc.tensor.matmul(pv_ps[32 * hh:32 * hh + 32, :], vaug[:, kc, G * g + hh, :],
                                          pt[kc % 2][hh // 2][:, hh % 2, :], start=(kc == 0), stop=(kc == QC - 1))
                mm.then_inc(pv_mm, 1)

            def context(kind, b, cb, g):
                pe.wait_ge(pvs_done, 4 * cb + g + 1)
                shared(kind, b, f"ctx{g}")
                for c in range(QC):
                    mm = nc.tensor.transpose(misc[:, c * P:(c + 1) * P], pvs[:, c * P:(c + 1) * P], m.ident[:, :])
                mm.then_inc(misc_mm, 1)

            def context_t(kind, b, cb):
                shared(kind, b, "CT")
                for c in range(QC):
                    mm = nc.tensor.transpose(misc[:, c * P:(c + 1) * P], ctxt[:, c, :], m.ident[:, :])
                mm.then_inc(misc_mm, 1)

            def maxima_t(kind, b, _, g):
                for k in range(2):
                    pe.wait_ge(max_done[k], 32 * b + 8 * g + 8)
                shared(kind, b, f"nm{g}")
                for c in range(QC):
                    mm = nc.tensor.transpose(misc16[0:G, c * P:(c + 1) * P], nm[g % 2][:, c, :], ident16[:, :])
                mm.then_inc(misc_mm, 1)

            schedule(pe, {"XT": tokens_t, "Q": features("Q", 0, xt_h, xt_l), "K": features("K", 1, xt_h, xt_l),
                          "V": rows("V", 2, xt_h, xt_l), "GB": gate_bias, "F": features("F", 3, q_h, q_l),
                          "PZ": centre_width, "CF": coefficients_t, "scores": scores, "value": value,
                          "ctx": context, "nm": maxima_t, "CT": context_t, "OUT": rows("OUT", 4, ct_h, ct_l)})

        @block.scalar
        def _(act):
            def setup():
                nc.scalar.preload_act_table(ACT.Exp)
                act.wait_ge(m.a_loaded, m.A_LOADS)
                nc.scalar.activation(bk_s[:, :], m.a_cols[:, 1:2], ACT.Copy, scale=K_SCALE).then_inc(setup_done, 1)
                nc.scalar.activation(xs[:, :, :], m.x[:, 0:QC, :], ACT.Copy).then_inc(xs_in, 1)

            def slot(kind, b, at):
                if at == 0 and kind in ("first", "middle"):
                    nc.scalar.activation(xs[:, :, :].rearrange("p c d -> p (c d)"), m_flat(m.x)[:, ds((b + 1) * S, S)],
                                         ACT.Copy).then_inc(xs_in, 1)

            def used(kind, b, name):
                act.wait_ge(misc_mm, use(kind, b, name) + 1)

            def high(name, dst, signal):
                def run(kind, b, nb):
                    used(kind, b, name)
                    nc.scalar.activation(dst[:, :], misc[:, :], ACT.Copy).then_inc(signal, 1)
                return run

            def queries(kind, b, nb):
                act.wait_ge(q_split, nb)
                used(kind, b, "Q")
                nc.scalar.activation(q32[:, :], misc[:, :], ACT.Identity, bias=m.a_cols[:, 0:1],
                                     accum_out=qsum[:, :]).then_inc(misc_out, 1)

            def keys(kind, b, nb):
                act.wait_ge(k_split, nb)
                act.wait_ge(setup_done, 1)
                used(kind, b, "K")
                nc.scalar.activation(k32[:, :], misc[:, :], ACT.Identity, bias=bk_s[:, :], scale=K_SCALE).then_inc(misc_out, 1)

            def gates(kind, b, nb):
                used(kind, b, "F")
                nc.scalar.activation(c32[:, :], misc[:, :], ACT.Tanh, bias=gbias[:, :]).then_inc(misc_out, 1)

            def sigmoids(kind, b, nb):
                act.wait_ge(coef_done, nb)
                used(kind, b, "PZ")
                nc.scalar.activation(epz[:, :, :].rearrange("p c h -> p (c h)"), misc[:, 0:QC * 2 * H1], ACT.Exp,
                                     scale=-1.0).then_inc(misc_out, 1)

            def coefficients(kind, b, nb):
                act.wait_ge(parts_out, PARTS * nb)
                used(kind, b, "CF")
                nc.scalar.activation(coef_t[:, :], misc16[:, 0:S], ACT.Copy).then_inc(misc_out, 1)

            def exponentials(r, head, unit):
                if not unit:
                    return
                b, g, kc, _ = unit
                n = 16 * b + 4 * g + kc
                act.wait_ge(st_mm[r], n + 1)
                if not isinstance(n, int) or n >= 2:
                    act.wait_ge(pv_mm, n - 1)
                nc.scalar.activation(pt[kc % 2][r][:, :, :], st_ps[r][:, :, :], ACT.Exp, scale=1.0 / SC).then_inc(exp_done[r], 1)

            def group_end(cb, g):
                act.wait_ge(pv_mm, 16 * cb + 4 * g + 4)
                act.wait_ge(ctx_steps, 4 * cb + g)
                nc.scalar.activation(pvs[:, :], pv_ps[:, :], ACT.Copy).then_inc(pvs_done, 1)

            def maxima(kind, b, _, g):
                act.wait_ge(nm_in[(g + 2) % G], 16 * (b + 1) if g >= 2 else 16 * b)
                used(kind, b, f"nm{g}")
                nc.scalar.activation(nm_t[g % 2][:, :], misc16[0:G, 0:S], ACT.Copy).then_inc(misc_out, 1)

            schedule(act, {"setup": setup, "slot": slot, "XT": high("XT", xt_h, xt_hi), "Q": queries, "K": keys, "F": gates,
                           "PZ": sigmoids, "CF": coefficients, "scores": exponentials, "group_end": group_end, "nm": maxima,
                           "CT": high("CT", ct_h, ct_hi)})

        @block.vector
        def _(dve):
            def setup():
                steps = Steps(dve, ln_dve)
                nc.vector.memset(kop[:, :, :, :].rearrange("p a b n -> p (a b n)"), 0.0).then_inc(kzero, 1)
                nc.vector.memset(coef[:, :, :, :, :].rearrange("p c g t h -> p (c g t h)"), 0.0)
                nc.vector.tensor_copy(ident16[:, :], m.ident[:, :])
                dve.wait_ge(m.a_loaded, m.A_LOADS)
                steps.step(nc.vector.tensor_reduce(head_mask[:, :], m.ident[:, :].rearrange("p (h d) -> p h d", d=D1), AX.X, ALU.add))
                for k in range(2):
                    steps.done(nc.vector.tensor_scalar(upz[:, k * H1:(k + 1) * H1], head_mask[:, :], m.a_cols[:, 4 + k:5 + k], None, ALU.mult))
                steps.step(nc.vector.tensor_tensor(bf[:, :], m.a_cols[:, 2:3], m.a_cols[:, 3:4], ALU.add))
                assert steps.k == SETUP_STEPS

            def used(kind, b, name):
                dve.wait_ge(misc_mm, use(kind, b, name) + 1)

            def low(name, hi, lo, signal):
                def run(kind, b, nb):
                    used(kind, b, name)
                    dve.wait_ge(signal, nb + 1)
                    nc.vector.tensor_tensor(lo[:, :], misc[:, :], hi[:, :], ALU.subtract).then_inc(misc_out, 1)
                return run

            def values(kind, b, nb):
                dve.wait_ge(vaug_done, G * nb)
                used(kind, b, "V")
                nc.vector.tensor_copy(v32[:, :], misc[:, :]).then_inc(misc_out, 1)

            def gate_bias(kind, b, nb):
                used(kind, b, "GB")
                nc.vector.scalar_tensor_tensor(gbias[:, :], misc[:, 0:1], 1.0 / S, bf[:, :], ALU.mult, ALU.add).then_inc(misc_out, 1)

            def centres(kind, b, nb):
                steps = Steps(dve, cf_steps, 2 * nb)
                dve.wait_ge(coef_done, nb)
                dve.wait_ge(misc_out, use(kind, b, "PZ") + 1)
                steps.step(nc.vector.tensor_scalar(epz[:, :, :], epz[:, :, :], 1.0, None, ALU.add))
                steps.step(nc.vector.reciprocal(cent[:, :, :], epz[:, :, 0:H1]))
                nc.vector.tensor_scalar(cent[:, :, :], cent[:, :, :], S / 32.0, -(S - 1) / 64, ALU.mult, ALU.add).then_inc(cent_done, 1)

            def maxima(half, head, unit):
                if not head:
                    return
                b, g, hh = head
                n = 16 * b + 4 * g + hh
                if hh == 0 and half == 0:
                    dve.wait_ge(nm_in[(g + 2) % G], 16 * (b + 1) if g >= 2 else 16 * b)
                for c in range(2 * half, 2 * half + 2):
                    dve.wait_ge(s_mm[c % 2], 2 * n + c // 2 + 1)
                    nc.vector.tensor_reduce(nm[g % 2][:, c, hh:hh + 1], s_ps[c % 2][:, :], AX.X, ALU.max,
                                            negate=True).then_inc(max_done[c % 2], 1)

            def context(kind, b, cb, g):
                used(kind, b, f"ctx{g}")
                heads = misc[:, :].rearrange("p (c h e) -> p c h e", c=QC, e=32)
                nc.vector.reciprocal(rsum[:, :, :], heads[:, :, :, D1]).then_inc(ctx_steps, 1)
                dve.wait_ge(ctx_steps, 4 * cb + g + 1)
                nc.vector.tensor_tensor(ctxt[:, :, g * 32:g * 32 + 32].rearrange("p c (h d) -> p c h d", d=D1), heads[:, :, :, 0:D1],
                                        rsum[:, :, :].unsqueeze(3).to_broadcast([P, QC, G, D1]), ALU.mult).then_inc(misc_out, 1)

            def output(kind, b, cb):
                dve.wait_ge(xres_done, cb + 1)
                used(kind, b, "OUT")
                nc.vector.tensor_tensor(y[:, :, :].rearrange("p c d -> p (c d)"), misc[:, :],
                                        xres[:, :, :].rearrange("p c d -> p (c d)"), ALU.add).then_inc(misc_out, 1)
                dve.wait_ge(misc_out, use(kind, b, "OUT") + 1)
                layer_norm_stats(nc, dve, m, 2 * B + cb, y, st, mv)

            def norm(cb):
                layer_norm_apply(nc, dve, m, 2 * B + cb, y, mv, rstd,
                                 m_flat(m.x)[:, ds(cb * S, S)].rearrange("p (c d) -> p c d", d=D)).then_inc(ln_dve, 1)

            SETUP_STEPS = 4
            schedule(dve, {"setup": setup, "XT": low("XT", xt_h, xt_l, xt_hi), "V": values, "GB": gate_bias, "PZ": centres,
                           "scores": maxima, "ctx": context, "CT": low("CT", ct_h, ct_l, ct_hi), "OUT": output, "norm": norm})

        @block.gpsimd
        def _(pool):
            def setup():
                steps = Steps(pool, vset)
                steps.step(nc.gpsimd.memset(vaug[:, :, :, :].rearrange("p c h e -> p (c h e)"), 0.0))
                steps.step(nc.gpsimd.memset(vaug[:, :, :, D1:D1 + 1].rearrange("p c h e -> p (c h) e"), 1.0))

            def split(name, src, hi, lo, done, at):
                def run(kind, b, nb):
                    pool.wait_ge(misc_out, use(kind, b, name) + 1)
                    pool.wait_ge(parts_out, PARTS * nb)
                    pool_gate(nc, m, slice(0, P))
                    nc.gpsimd.affine_select(out=hi[:, :], in_=src[:, :], compare_op=ALU.is_ge, fill=0.0, base=0,
                                            pattern=[[1, S]], channel_multiplier=0).then_inc(pool_steps, 1)
                    pool.wait_ge(pool_steps, 2 * nb + at)
                    nc.gpsimd.tensor_tensor(lo[:, :], src[:, :], hi[:, :], ALU.subtract).then_inc(done, 1)
                return run

            def values(nb, g):
                if not (isinstance(nb, int) and nb == 0):
                    pool.wait_ge(pv_mm, 16 * (nb - 1) + 4 * g + 4)
                by_head = lambda a: a.rearrange("p c (g h d) -> p c g h d", g=G, h=G)[:, :, g, :, :]
                bias = m.a_bv[:, :].unsqueeze(1).to_broadcast([P, QC, D])
                nc.gpsimd.tensor_tensor(vaug[:, :, G * g:G * g + G, 0:D1], by_head(v32[:, :].rearrange("p (c d) -> p c d", d=D)),
                                        by_head(bias), ALU.add).then_inc(vaug_done, 1)

            def first_values():
                pool.wait_ge(misc_out, use("prep0", 0, "V") + 1)
                for g in range(G):
                    values(0, g)

            def slot(kind, b, at):
                if kind in ("middle", "last") and at in (2, 6):
                    values(b, 2 + at // 4)
                if kind in ("first", "middle") and at == 15:
                    pool.wait_ge(misc_out, use(kind, b, "V") + 1)
                    values(b + 1, 0)
                    values(b + 1, 1)
                if kind != "first" and at == 4:
                    xb = m_flat(m.x)[:, ds((b - 1) * S, S)].rearrange("p (c d) -> p c d", d=D)
                    nc.gpsimd.tensor_tensor(xres[:, :, :], xb, m.a_bo[:, :].unsqueeze(1).to_broadcast([P, QC, D]),
                                            ALU.add).then_inc(xres_done, 1)

            def polynomial(kind, b, nb):
                steps = Steps(pool, cf_pool, 3 * nb)
                by_group = lambda t: t.rearrange("p c (g h) -> p c g h", g=G)
                z, c = epz[:, :, H1:], cent[:, :, :]
                pool.wait_ge(cent_done, nb + 1)
                for (x, y_, total, slots) in ((z, z, ca, (0, 1)), (ca[:, :, :], c, cb, (3,)), (cb[:, :, :], c, cc, (5,))):
                    for n in slots:
                        nc.gpsimd.tensor_tensor(coef[:, :, :, n, :], by_group(x), by_group(y_), ALU.mult)
                    steps.step(nc.gpsimd.tensor_tensor(total[:, :, :], x, y_, ALU.mult))
                for hi, lo, t in ((0, 2, ca), (3, 4, cb), (5, 6, cc)):
                    last = nc.gpsimd.tensor_tensor(coef[:, :, :, lo, :], by_group(t[:, :, :]), coef[:, :, :, hi, :], ALU.subtract)
                last.then_inc(coef_done, 1)

            def output(kind, b, cb):
                layer_norm_gpsimd(nc, pool, m, 2 * B + cb, mv, ve, rstd)

            schedule(pool, {"setup": setup, "prepared": first_values, "slot": slot, "Q": split("Q", q32, q_h, q_l, q_split, 1),
                            "K": split("K", k32, k_h, k_l, k_split, 2), "PZ": polynomial, "OUT": output})


def moe_capacity_phase(nc, io, out, m):
    with ExitStack() as ctx:
        sb = lambda name, shape, dt: ctx.enter_context(nc.sbuf_tensor(name, shape, dt))
        sem = lambda name: ctx.enter_context(nc.semaphore("c_" + name))
        FC = F1 // P
        HALF = CAP // 2
        SLOTS = E1 * CAP
        OUT_OF_RANGE = float(1 << 20)
        TILES = [3 * B // 8, B]
        first, count = [0, TILES[0] * QC], [TILES[0] * QC, (B - TILES[0]) * QC]
        chunks = lambda h: slice(first[h], first[h] + count[h])
        wg_h, wg_l = (sb(n, [P, E1], F16) for n in ("cwg_h", "cwg_l"))
        logit, expo, held, onehot, onehot_pos = (sb(n, [P, NCH, E1], F32) for n in ("c_logit", "c_expo", "c_held", "c_onehot", "c_onehot_pos"))
        prefix = [sb(f"c_prefix{k}", [P, NCH, E1], F32) for k in range(2)]
        onehot16 = sb("c_onehot16", [P, NCH, E1], F16)
        lmax, esum, best, pos, over, away, slot = (sb(n, [P, NCH], F32) for n in ("c_lmax", "c_esum", "c_best", "c_pos", "c_over", "c_away", "c_slot"))
        to_slot, from_slot = (sb(n, [P, NCH], U32) for n in ("c_to_slot", "c_from_slot"))
        tri, ones = (sb(n, [P, P], F16) for n in ("tri_ones", "all_ones"))
        zeros = sb("c_zeros", [P, SLOTS], F32)
        xe = sb("c_xe", [HALF, 2 * E1, D], F32)
        xe_t = [sb(f"c_xe_t{k}", [P, CAP], F32) for k in range(2)]
        hid = [sb(f"c_hid{k}", [P, FC, CAP], F32) for k in range(2)]
        ye = sb("c_ye", [HALF, 2 * E1, D], F32)
        yg = sb("c_yg", [P, NCH, D], F32)
        y = [sb(f"c_y{k}", [P, QC, D], F32) for k in range(2)]
        res = [sb(f"c_res{k}", [P, QC, D], F32) for k in range(2)]
        st = sb("c_st", [P, QC, 6], F32)
        mv = [sb(f"c_mv{k}", [P, QC, 2], F32) for k in range(2)]
        ve = [sb(f"c_ve{k}", [P, QC], F32) for k in range(2)]
        rstd = [sb(f"c_rstd{k}", [P, QC], F32) for k in range(2)]
        bank = lambda name: ctx.enter_context(nc.psum_tensor(name, [P, 512], F32))
        xt_ps = [bank(f"c_xt_ps{k}") for k in range(2)]
        y_ps = [bank(f"c_y_ps{k}") for k in range(2)]
        hid_ps = [ctx.enter_context(nc.psum_tensor(f"c_hid_ps{k}", [P, 2, 512], F32)) for k in range(2)]
        tok_ps = [xt_ps[0][:, :], xt_ps[1][:, :], hid_ps[0][:, 1, :], hid_ps[1][:, 1, :]]
        logit_ps = [y_ps[0][:, 0:count[0] * E1], hid_ps[0][:, 0, 0:count[1] * E1]]
        count_ps = [y_ps[1][:, 0:2 * count[0] * E1], hid_ps[1][:, 0, 0:2 * count[1] * E1]]
        slot_rows = nc.dram_tensor("slot_rows", (SLOTS, D), F32).ap()
        expert_rows = nc.dram_tensor("expert_rows", (SLOTS + 1, D), F32).ap()

        xt_mm, xt_hi, xt_lo, lg_mm, steps_done, shifted, exps_done, onehot_done, count_mm = (sem(n) for n in (
            "xt_mm", "xt_hi", "xt_lo", "lg_mm", "steps", "shifted", "exps", "onehot_done", "count_mm"))
        slots_done, tri_in, zeros_set, zeroed, scattered, xe_in, h_mm, relu_done, y_mm, y_out, stored = (sem(n) for n in (
            "slots_done", "tri_in", "zeros_set", "zeroed", "scattered", "xe_in", "h_mm", "relu_done", "y_mm", "y_out", "stored"))
        out_ready = sem("out_ready")
        gathered = [sem(f"gathered{k}") for k in range(3)]
        out_stored = [sem(f"out_stored{k}") for k in range(2)]
        block = ctx.enter_context(nc.Block())
        E_LOADS = 16

        @block.sync
        def _(sp):
            sp.dma_start(tri[:, :], io["c_tri"]).then_inc(tri_in, 16)
            sp.wait_ge(zeros_set, 1)
            sp.dma_start(slot_rows.rearrange("(p r) d -> p (r d)", p=P), zeros[:, :]).then_inc(zeroed, 16)
            sp.dma_start(expert_rows[SLOTS:SLOTS + 1, :], zeros[0:1, 0:D]).then_inc(zeroed, 16)
            sp.wait_ge(scattered, 16 * NCH)
            sp.dma_start(xe[:, :, :], slot_rows.rearrange("(t p) d -> p t d", p=HALF)).then_inc(xe_in, E_LOADS)
            for e in range(E1):
                sp.wait_ge(y_out, e + 1)
                sp.dma_start(expert_rows[e * CAP:(e + 1) * CAP, :].rearrange("(t p) d -> p t d", p=HALF),
                             ye[:, 2 * e:2 * e + 2, :]).then_inc(stored, 16)
            for t in range(B):
                sp.wait_ge(out_ready, t + 1)
                sp.dma_start(out[t].rearrange("(c p) d -> p c d", p=P), res[t % 2][:, :, :]).then_inc(out_stored[t % 2], 16)
            for k in range(2):
                sp.wait_ge(out_stored[k], 16 * (B // 2))
            sp.wait_ge(tri_in, 16)

        def router(pe, t):
            pe.wait_ge(xt_lo, t + 1)
            for c in range(QC):
                ch = t * QC + c
                h = 0 if t < TILES[0] else 1
                o = logit_ps[h][:, (ch - first[h]) * E1:(ch - first[h] + 1) * E1]
                xs = slice(ch * P, (ch + 1) * P)
                nc.tensor.matmul(o, m.xt_h[:, xs], wg_h[:, :], start=True, stop=False)
                nc.tensor.matmul(o, m.xt_h[:, xs], wg_l[:, :], start=False, stop=False)
                last = nc.tensor.matmul(o, m.xt_l[:, xs], wg_h[:, :], start=False, stop=True)
            last.then_inc(lg_mm, 1)

        def counts(pe, h):
            if h == 0:
                pe.wait_ge(tri_in, 16)
            pe.wait_ge(onehot_done, h + 1)
            o16 = onehot16[:, chunks(h), :].rearrange("p c e -> p (c e)")
            nc.tensor.matmul(count_ps[h][:, 0:count[h] * E1], tri[:, :], o16, start=True, stop=True)
            nc.tensor.matmul(count_ps[h][:, count[h] * E1:], ones[:, :], o16, start=True, stop=True).then_inc(count_mm, 1)

        @block.tensor
        def _(pe):
            for t in range(B):
                if t >= 4:
                    pe.wait_ge(xt_lo, t - 3)
                for c in range(QC):
                    last = nc.tensor.transpose(tok_ps[t % 4][:, c * P:(c + 1) * P], m.x[:, t * QC + c, :], m.ident[:, :])
                last.then_inc(xt_mm, 1)
                if t >= 2:
                    router(pe, t - 2)
                if t == TILES[0] + 3:
                    counts(pe, 0)
            router(pe, B - 2)
            router(pe, B - 1)
            counts(pe, 1)
            pe.wait_ge(xe_in, E_LOADS)
            pe.wait_ge(m.e_loaded, 48)

            def rows_t(e):
                if e >= 2:
                    pe.wait_ge(xt_hi, B + e - 1)
                for j in range(2):
                    mm = nc.tensor.transpose(xt_ps[e % 2][:, j * HALF:(j + 1) * HALF], xe[:, 2 * e + j, :],
                                             m.ident[0:HALF, 0:HALF])
                mm.then_inc(xt_mm, 1)

            def hidden(e):
                pe.wait_ge(xt_hi, B + e + 1)
                if e >= 2:
                    pe.wait_ge(relu_done, e - 1)
                for f in range(FC):
                    mm = nc.tensor.matmul(hid_ps[e % 2][:, f // 2, (f % 2) * CAP:(f % 2 + 1) * CAP],
                                          m.e_w1[:, e, f * P:(f + 1) * P], xe_t[e % 2][:, :], start=True, stop=True)
                mm.then_inc(h_mm, 1)

            def output(e):
                pe.wait_ge(relu_done, e + 1)
                if e >= 2:
                    pe.wait_ge(y_out, e - 1)
                for j in range(2):
                    for f in range(FC):
                        mm = nc.tensor.matmul(y_ps[e % 2][0:HALF, j * D:(j + 1) * D],
                                              hid[e % 2][:, f, j * HALF:(j + 1) * HALF], m.e_w2[:, e, f, :],
                                              start=(f == 0), stop=(f == FC - 1))
                mm.then_inc(y_mm, 1)

            rows_t(0)
            rows_t(1)
            hidden(0)
            for e in range(E1):
                if e + 2 < E1:
                    rows_t(e + 2)
                if e + 1 < E1:
                    hidden(e + 1)
                output(e)

        @block.scalar
        def _(act):
            nc.scalar.preload_act_table(ACT.Exp)
            for t in range(B):
                act.wait_ge(xt_mm, t + 1)
                nc.scalar.activation(m.xt_h[:, t * S:(t + 1) * S], tok_ps[t % 4], ACT.Copy).then_inc(xt_hi, 1)
                if t == TILES[0] + 1 or t == B - 1:
                    h = t // (B - 1)
                    act.wait_ge(shifted, h + 1)
                    nc.scalar.activation(expo[:, chunks(h), :], logit[:, chunks(h), :], ACT.Exp).then_inc(exps_done, 1)

            def rows_t(e):
                act.wait_ge(xt_mm, B + e + 1)
                if e >= 2:
                    act.wait_ge(h_mm, e - 1)
                nc.scalar.activation(xe_t[e % 2][:, :], xt_ps[e % 2][:, 0:CAP], ACT.Copy).then_inc(xt_hi, 1)

            rows_t(0)
            rows_t(1)
            for e in range(E1):
                act.wait_ge(h_mm, e + 1)
                if e >= 2:
                    act.wait_ge(y_mm, e - 1)
                nc.scalar.activation(hid[e % 2][:, :, :].rearrange("p (b f) n -> p b (f n)", b=2), hid_ps[e % 2][:, :, 0:2 * CAP],
                                     ACT.Relu).then_inc(relu_done, 1)
                if e + 2 < E1:
                    rows_t(e + 2)

        @block.vector
        def _(dve):
            steps = Steps(dve, steps_done)
            wide = lambda a, n: a.unsqueeze(2).to_broadcast([P, n, E1])
            iota = lambda n: m.iota8[:, :].unsqueeze(1).to_broadcast([P, n, E1])
            dve.wait_ge(m.e_loaded, 48)
            steps.done(nc.vector.memset(ones[:, :], 1.0))
            steps.step(nc.vector.tensor_copy(wg_h[:, :], m.e_wg[:, :]))
            steps.step(nc.vector.tensor_tensor(wg_l[:, :], m.e_wg[:, :], wg_h[:, :], ALU.subtract))

            def low_parts(t):
                dve.wait_ge(xt_hi, t + 1)
                nc.vector.tensor_tensor(m.xt_l[:, t * S:(t + 1) * S], tok_ps[t % 4], m.xt_h[:, t * S:(t + 1) * S],
                                        ALU.subtract).then_inc(xt_lo, 1)

            def shift(h):
                dve.wait_ge(lg_mm, TILES[h])
                lg = logit_ps[h].rearrange("p (c e) -> p c e", e=E1)
                steps.step(nc.vector.tensor_reduce(lmax[:, chunks(h)], lg, AX.X, ALU.max))
                nc.vector.tensor_tensor(logit[:, chunks(h), :], lg, wide(lmax[:, chunks(h)], count[h]), ALU.subtract).then_inc(shifted, 1)

            def choose(h):
                hs = chunks(h)
                dve.wait_ge(exps_done, h + 1)
                steps.done(nc.vector.tensor_reduce(esum[:, hs], expo[:, hs, :], AX.X, ALU.add))
                steps.step(nc.vector.tensor_scalar(held[:, hs, :], expo[:, hs, :], 1.0, -float(E1), ALU.is_ge, ALU.mult))
                steps.step(nc.vector.tensor_tensor(held[:, hs, :], held[:, hs, :], iota(count[h]), ALU.add))
                steps.step(nc.vector.tensor_reduce(best[:, hs], held[:, hs, :], AX.X, ALU.min))
                steps.step(nc.vector.tensor_tensor(onehot[:, hs, :], held[:, hs, :], wide(best[:, hs], count[h]), ALU.is_equal))
                nc.vector.tensor_copy(onehot16[:, hs, :], onehot[:, hs, :]).then_inc(onehot_done, 1)
                steps.done(nc.vector.reciprocal(esum[:, hs], esum[:, hs]))
                steps.done(nc.vector.tensor_scalar(best[:, hs], best[:, hs], float(E1), None, ALU.add))

            def place(h, k, before):
                hs, c0, c1, n = chunks(h), first[h], first[h] + count[h], count[h]
                dve.wait_ge(count_mm, h + 1)
                totals = count_ps[h][:, n * E1:].rearrange("p (c e) -> p c e", e=E1)
                if h == 0:
                    steps.done(nc.vector.memset(prefix[k][:, 0:1, :], 0.0))
                else:
                    steps.done(nc.vector.tensor_tensor(prefix[k][:, c0:c0 + 1, :], prefix[k][:, c0 - 1:c0, :], before, ALU.add))
                steps.step(nc.vector.tensor_copy(prefix[k][:, c0 + 1:c1, :], totals[:, 0:n - 1, :]))
                d = 1
                while d < n:
                    a, b = prefix[k], prefix[1 - k]
                    steps.done(nc.vector.tensor_copy(b[:, c0:c0 + d, :], a[:, c0:c0 + d, :]))
                    steps.step(nc.vector.tensor_tensor(b[:, c0 + d:c1, :], a[:, c0 + d:c1, :], a[:, c0:c1 - d, :], ALU.add))
                    k, d = 1 - k, 2 * d
                running = count_ps[h][:, 0:n * E1].rearrange("p (c e) -> p c e", e=E1)
                steps.step(nc.vector.tensor_tensor(held[:, hs, :], running, prefix[k][:, hs, :], ALU.add))
                steps.step(nc.vector.tensor_tensor(onehot_pos[:, hs, :], held[:, hs, :], onehot[:, hs, :], ALU.mult))
                steps.step(nc.vector.tensor_reduce(pos[:, hs], onehot_pos[:, hs, :], AX.X, ALU.add))
                steps.done(nc.vector.scalar_tensor_tensor(slot[:, hs], best[:, hs], float(CAP), pos[:, hs], ALU.mult, ALU.add))
                steps.done(nc.vector.tensor_scalar(over[:, hs], pos[:, hs], float(CAP), None, ALU.is_gt))
                steps.step(nc.vector.tensor_scalar(away[:, hs], best[:, hs], float(NT), OUT_OF_RANGE, ALU.mult, ALU.add))
                steps.step(nc.vector.tensor_tensor(over[:, hs], over[:, hs], away[:, hs], ALU.mult))
                steps.step(nc.vector.scalar_tensor_tensor(slot[:, hs], slot[:, hs], -1.0, over[:, hs], ALU.add, ALU.add))
                nc.vector.tensor_copy(to_slot[:, hs], slot[:, hs]).then_inc(slots_done, 1)
                nc.vector.tensor_scalar(from_slot[:, hs], slot[:, hs], float(SLOTS), None, ALU.min).then_inc(slots_done, 1)
                return k, totals[:, n - 1:n, :]

            for t in range(TILES[0] + 1):
                low_parts(t)
            shift(0)
            low_parts(TILES[0] + 1)
            choose(0)
            low_parts(TILES[0] + 2)
            low_parts(TILES[0] + 3)
            k, before = place(0, 0, None)
            for t in range(TILES[0] + 4, B):
                low_parts(t)
            shift(1)
            choose(1)
            place(1, k, before)
            for e in range(E1):
                dve.wait_ge(y_mm, e + 1)
                nc.vector.tensor_copy(ye[:, 2 * e:2 * e + 2, :], y_ps[e % 2][0:HALF, 0:2 * D].rearrange("p (j d) -> p j d", d=D)).then_inc(y_out, 1)
            def sums(t):
                dve.wait_ge(gathered[t % 3], 16 * QC * (t // 3 + 1))
                if t >= 2:
                    dve.wait_ge(out_ready, t - 1)
                for c in range(QC):
                    ch = t * QC + c
                    last = nc.vector.scalar_tensor_tensor(y[t % 2][:, c, :], yg[:, ch, :], esum[:, ch:ch + 1], m.x[:, ch, :],
                                                          ALU.mult, ALU.add)
                steps.step(last)
                layer_norm_stats(nc, dve, m, 3 * B + t, y[t % 2], st, mv[t % 2])
                dve.wait_ge(m.var_ready, 3 * B + t + 1)
                nc.vector.tensor_tensor(ve[t % 2][:, :], mv[t % 2][:, :, 1], m.eps[:, :], ALU.add).then_inc(m.ln_pool, 1)

            def norm(t):
                if t >= 2:
                    dve.wait_ge(out_stored[t % 2], 16 * (t // 2))
                layer_norm_apply(nc, dve, m, 3 * B + t, y[t % 2], mv[t % 2], rstd[t % 2], res[t % 2]).then_inc(out_ready, 1)

            sums(0)
            for t in range(1, B):
                sums(t)
                norm(t - 1)
            norm(B - 1)

        @block.gpsimd
        def _(pool):
            nc.gpsimd.memset(zeros[:, :], 0.0).then_inc(zeros_set, 1)
            pool.wait_ge(zeroed, 32)
            for ch in range(NCH):
                if ch in first:
                    pool.wait_ge(slots_done, 2 * (first.index(ch) + 1))
                nc.gpsimd.indirect_dma_start(out=slot_rows[:, :], out_offset=bass.IndirectOffsetOnAxis(ap=to_slot[:, ch:ch + 1], axis=0),
                                             in_=m.x[:, ch, :], in_offset=None, bounds_check=SLOTS - 1,
                                             oob_is_err=False).then_inc(scattered, 16)
            pool.wait_ge(stored, 16 * E1)

            def gather(t):
                for ch in range(t * QC, (t + 1) * QC):
                    nc.gpsimd.indirect_dma_start(out=yg[:, ch, :], out_offset=None, in_=expert_rows[:, :],
                                                 in_offset=bass.IndirectOffsetOnAxis(ap=from_slot[:, ch:ch + 1], axis=0),
                                                 bounds_check=SLOTS, oob_is_err=False).then_inc(gathered[t % 3], 16)

            for t in range(3):
                gather(t)
            for t in range(B):
                pool.wait_ge(m.ln_pool, 3 * B + t + 1)
                nc.gpsimd.tensor_tensor(rstd[t % 2][:, :], ve[t % 2][:, :], m.mhalf[:, :], ALU.pow).then_inc(m.rstd_ready, 1)
                if t + 3 < B:
                    gather(t + 3)


def m_flat(t):
    a = t[tuple(slice(None) for _ in t.shape)]
    names = "abcd"[:len(t.shape) - 1]
    return a if len(names) == 1 else a.rearrange(f"p {' '.join(names)} -> p ({' '.join(names)})")


class Memory:
    pass


def build(nc, io, out):
    ctx = ExitStack()
    with ctx:
        sb = lambda name, shape, dt: ctx.enter_context(nc.sbuf_tensor(name, shape, dt))
        m = Memory()
        m.x = sb("x_tok", [P, NCH, D], F32)
        m.ident = sb("ident", [P, P], F32)
        m.mhalf = sb("mhalf", [P, QC], F32)
        m.eps = sb("ln_eps", [P, QC], F32)
        m.gate_v = sb("gate_v", [P, 1], F32)
        m.gate_v2 = sb("gate_v2", [P, 1], F32)
        m.gate = sb("gate", [P, QC], F32)
        m.x_loaded = [ctx.enter_context(nc.semaphore(f"x_loaded{b}")) for b in range(B // 2)]
        m.var_ready, m.rstd_ready, m.ln_pool = (ctx.enter_context(nc.semaphore(n)) for n in ("var_ready", "rstd_ready", "ln_pool"))
        m.stats_ready = ctx.enter_context(nc.semaphore("stats_ready"))
        m.xt_h = sb("xt_h", [P, NT + S], F16)
        m.xt_l = sb("xt_l", [P, NT + S], F16)
        m.w1_raw = sb("w1_raw", [P, E0, F0], F32)
        m.w2_raw = sb("w2_raw", [P, E0, F0 // P, D], F32)
        m.wg_raw = sb("wg_raw", [P, E0], F32)
        m.bg_bc = sb("bg_bc", [P, E0], F32)
        m.b1_rows = sb("b1_rows", [E0 * F0 // P, P], F32)
        m.b2_blocks = sb("b2_blocks", [QC * E0, QC * D], F32)
        m.iota8 = sb("iota8", [P, E0], F32)
        m.f0_loaded = ctx.enter_context(nc.semaphore("f0_loaded"))
        m.F0_LOADS = 10 * 16
        m.a_w = sb("a_w_raw", [P, 5, D], F32)
        m.a_w_h, m.a_w_l = (sb(n, [P, 5, P], F16) for n in ("a_w_h", "a_w_l"))
        m.a_wfg = sb("a_wfg", [P, D], F32)
        m.a_cols = sb("a_cols", [P, 6], F32)
        m.a_bv = sb("a_bv", [P, D], F32)
        m.a_bo = sb("a_bo", [P, D], F32)
        m.e_w1 = sb("e_w1", [P, E1, F1], F32)
        m.e_w2 = sb("e_w2", [P, E1, F1 // P, D], F32)
        m.e_wg = sb("e_wg", [P, E1], F32)
        m.e_loaded = ctx.enter_context(nc.semaphore("e_loaded"))
        m.a_loaded = ctx.enter_context(nc.semaphore("a_loaded"))
        with ExitStack() as c0:
            sb0 = lambda name, shape, dt: c0.enter_context(nc.sbuf_tensor(name, shape, dt))
            m.w_h = sb0("w_h", [P, PAIRS, 512], F16)
            m.w_l = sb0("w_l", [P, PAIRS, 512], F16)
            m.wo_h = sb0("wo_h", [P, PAIRS, D], F16)
            m.wo_l = sb0("wo_l", [P, PAIRS, D], F16)
            m.k_h = [sb0(f"k_h{h}", [P, S], F16) for h in range(2)]
            m.k_l = [sb0(f"k_l{h}", [P, S], F16) for h in range(2)]
            m.q_mult = sb0("q_mult", [P, 2, S], F32)
            m.q_bias = sb0("q_bias", [P, 2, PAIRS], F32)
            m.bo_bc = sb0("bo_bc", [P, D], F32)
            m.causal = sb0("causal", [P, P], BF16)
            m.ident_bf = sb0("ident_bf", [P, P], BF16)
            m.zeros = sb0("zeros", [P, S], F16)
            setup_phase(nc, io, m)
            rel_attention_phase(nc, io, m)
        moe_top2_phase(nc, io, m)
        gauss_attention_phase(nc, io, m)
        moe_capacity_phase(nc, io, out, m)


_INPUTS = [
    "L0_attn_input", "L0_attn_qkv", "L0_attn_q_bias", "L0_attn_positional", "L0_attn_out_kernel", "L0_attn_out_bias",
    "L0_ffn_Wg", "L0_ffn_bg", "L0_ffn_W1", "L0_ffn_b1", "L0_ffn_W2", "L0_ffn_b2",
    "L1_attn_wq", "L1_attn_bq", "L1_attn_wk", "L1_attn_bk", "L1_attn_wv", "L1_attn_bv", "L1_attn_wo", "L1_attn_bo",
    "L1_attn_wfq", "L1_attn_bfq", "L1_attn_wfg", "L1_attn_bfg", "L1_attn_up", "L1_attn_uz",
    "L1_ffn_gate_w", "L1_ffn_w1", "L1_ffn_w2",
]


def kernel(**inputs):
    import concourse.bacc as bacc
    from concourse.bass_utils import run_bass_kernel_spmd

    nc = bacc.Bacc("TRN2", target_bir_lowering=False, num_devices=1)
    arrays, io = {}, {}
    for name in _INPUTS:
        arrays[f"in_{name}_dram"] = np.ascontiguousarray(inputs[name])
    for name, table in shape_constants().items():
        arrays[f"in_{name}_dram"] = table
    for dram, a in arrays.items():
        io[dram[3:-5]] = nc.dram_tensor(dram, a.shape, mybir.dt.from_np(a.dtype), kind="ExternalInput").ap()
    out = nc.dram_tensor("out_0_dram", (B, S, D), F32, kind="ExternalOutput").ap()
    build(nc, io, out)
    r = run_bass_kernel_spmd(nc, [arrays], core_ids=[0])
    return r.results[0]["out_0_dram"]
```
